# Optimizing a Trainium2 kernel written in Bass

```python
import numpy as np
import jax
import jax.numpy as jnp

def _softmax(x, axis=-1):
    return jax.nn.softmax(x, axis=axis)

def _gelu(x):
    return jax.nn.gelu(x, approximate=True)

def _silu(x):
    return jax.nn.silu(x)

def _sigmoid(x):
    return jax.nn.sigmoid(x)

def _layernorm(x, axis=-1, eps=1e-05):
    m = jnp.mean(x, axis=axis, keepdims=True)
    v = jnp.var(x, axis=axis, keepdims=True)
    return (x - m) / jnp.sqrt(v + eps)

def _scatter_add(tgt, idx, src, axis=0):
    return tgt.at[idx].add(src)

def _segment_sum(src, seg, n):
    return jax.ops.segment_sum(src, seg, n)
kernel_name = 'mk_decoder_preln_d1_seqx_r4_cb5361'

def setup_inputs(seed: int=0):
    np.random.seed(seed)
    _w = jnp.asarray

    def _rec_inputs():
        import jax
        import jax.numpy as jnp
        _rk = jax.random.key(seed)
        x = 7.22e-05 + 1 * jax.random.normal(jax.random.fold_in(_rk, 1), (8, 512, 256), jnp.float32)
        _lenS = 512 - jax.random.randint(jax.random.fold_in(_rk, 7), (8,), 0, max(1, 512 // 4) + 1, jnp.int32)
        _lenS2 = 512 - jax.random.randint(jax.random.fold_in(_rk, 8), (8,), 0, max(1, 512 // 4) + 1, jnp.int32)
        _ctx_1024P = jax.random.normal(jax.random.fold_in(_rk, 11), (8, 16, 256), jnp.float32)
        _ctx_1024c = jax.random.dirichlet(jax.random.fold_in(_rk, 511), 0.3 * jnp.ones((16,), jnp.float32), (8, 512))
        _ctx_1024t = jnp.einsum('bsk,bkd->bsd', _ctx_1024c, _ctx_1024P)
        _ctx_1024t = _ctx_1024t * jax.lax.rsqrt(jnp.mean(jnp.square(_ctx_1024t)) + 1e-12) * 0.953939
        ctx_1024 = 4.13588e-05 + 0.999923 * (_ctx_1024t + 0.3 * jax.random.normal(jax.random.fold_in(_rk, 611), (8, 512, 256), jnp.float32))
        _validS = jnp.arange(512)[None, :] < _lenS[:, None]
        _validS2 = jnp.arange(512)[None, :] < _lenS2[:, None]
        _causal = jnp.tril(jnp.ones((512, 512), dtype=bool))
        mask_1x1xSxS2_ik0 = jnp.where(jnp.broadcast_to(_validS2[0:1, None, None, :], (1, 1, 512, 512)), 0, 1).astype(jnp.int32)
        return (x, ctx_1024, mask_1x1xSxS2_ik0)
    x, ctx_1024, mask_1x1xSxS2_ik0 = _rec_inputs()

    def _L0_attn_setup():
        import jax, jax.numpy as jnp
        import numpy as np
        B, L, D_MODEL = (2, 256, 256)
        D_STATE, D_CONV, EXPAND = (16, 4, 2)
        D_INNER = EXPAND * D_MODEL
        DT_RANK = (D_MODEL + 15) // 16

        def _silu(x):
            return x * jax.nn.sigmoid(x)

        def _layernorm(x, g, b, eps=1e-05):
            m = x.mean(-1, keepdims=True)
            v = ((x - m) ** 2).mean(-1, keepdims=True)
            return (x - m) / jnp.sqrt(v + eps) * g + b

        def _selective_scan(u, delta, A, Bm, Cm):

            def step(h, inp):
                u_t, d_t, B_t, C_t = inp
                dA = jnp.exp(d_t[:, :, None] * A[None])
                h = dA * h + (d_t * u_t)[:, :, None] * B_t[:, None, :]
                y = jnp.einsum('bdn,bn->bd', h, C_t)
                return (h, y)
            h0 = jnp.zeros((u.shape[0], A.shape[0], A.shape[1]), u.dtype)
            xs = (u.swapaxes(0, 1), delta.swapaxes(0, 1), Bm.swapaxes(0, 1), Cm.swapaxes(0, 1))
            _, ys = jax.lax.scan(step, h0, xs)
            return ys.swapaxes(0, 1)

        def _mamba(x, in_w, conv_w, conv_b, xp_w, dt_w, dt_b, A_log, Dp, out_w):
            xz = jnp.einsum('bld,ed->ble', x, in_w)
            xi, z = jnp.split(xz, 2, axis=-1)
            u = jax.lax.conv_general_dilated(xi.swapaxes(1, 2), conv_w, (1,), [(D_CONV - 1, 0)], dimension_numbers=('NCH', 'OIH', 'NCH'), feature_group_count=D_INNER)
            u = _silu(u.swapaxes(1, 2) + conv_b)
            xdbl = jnp.einsum('bld,ed->ble', u, xp_w)
            dt = jax.nn.softplus(jnp.einsum('blr,dr->bld', xdbl[..., :DT_RANK], dt_w) + dt_b)
            Bm = xdbl[..., DT_RANK:DT_RANK + D_STATE]
            Cm = xdbl[..., DT_RANK + D_STATE:]
            A = -jnp.exp(A_log)
            y = _selective_scan(u, dt, A, Bm, Cm) + u * Dp
            y = y * _silu(z)
            return jnp.einsum('bld,ed->ble', y, out_w)

        def _forward(x, norm_g, norm_b, f_in_proj_w, f_conv_w, f_conv_b, f_x_proj_w, f_dt_proj_w, f_dt_proj_b, f_A_log, f_D, f_out_proj_w, b_in_proj_w, b_conv_w, b_conv_b, b_x_proj_w, b_dt_proj_w, b_dt_proj_b, b_A_log, b_D, b_out_proj_w, ffn_g, ffn_b, w1, b1, w2, b2):
            x_norm = _layernorm(x, norm_g, norm_b)
            y_fwd = _mamba(x_norm, f_in_proj_w, f_conv_w, f_conv_b, f_x_proj_w, f_dt_proj_w, f_dt_proj_b, f_A_log, f_D, f_out_proj_w)
            x_rev = jnp.flip(x_norm, axis=1)
            y_bwd = _mamba(x_rev, b_in_proj_w, b_conv_w, b_conv_b, b_x_proj_w, b_dt_proj_w, b_dt_proj_b, b_A_log, b_D, b_out_proj_w)
            y = (y_fwd + jnp.flip(y_bwd, axis=1)) / 2.0
            x = x + y
            h = _layernorm(x, ffn_g, ffn_b)
            h = jax.nn.gelu(jnp.einsum('bld,ed->ble', h, w1) + b1, approximate=False)
            x = x + (jnp.einsum('bld,ed->ble', h, w2) + b2)
            return x
        key = jax.random.key(seed)
        ks = iter(jax.random.split(key, 40))

        def rn(shape, s=0.02):
            return jax.random.normal(next(ks), shape, jnp.float32) * s
        inp = {'x': jax.random.normal(next(ks), (B, L, D_MODEL), jnp.float32)}
        inp['norm_g'] = jnp.ones((D_MODEL,), jnp.float32)
        inp['norm_b'] = jnp.zeros((D_MODEL,), jnp.float32)
        A_log = jnp.log(jnp.tile(jnp.arange(1, D_STATE + 1, dtype=jnp.float32), (D_INNER, 1)))
        for p in ('f_', 'b_'):
            inp[p + 'in_proj_w'] = rn((2 * D_INNER, D_MODEL))
            inp[p + 'conv_w'] = rn((D_INNER, 1, D_CONV), 0.1)
            inp[p + 'conv_b'] = jnp.zeros((D_INNER,), jnp.float32)
            inp[p + 'x_proj_w'] = rn((DT_RANK + 2 * D_STATE, D_INNER))
            inp[p + 'dt_proj_w'] = rn((D_INNER, DT_RANK), 0.1)
            dt = jax.random.uniform(next(ks), (D_INNER,), jnp.float32, 0.001, 0.1)
            inp[p + 'dt_proj_b'] = jnp.log(jnp.expm1(dt))
            inp[p + 'A_log'] = A_log
            inp[p + 'D'] = jnp.ones((D_INNER,), jnp.float32)
            inp[p + 'out_proj_w'] = rn((D_MODEL, D_INNER))
        inp['ffn_g'] = jnp.ones((D_MODEL,), jnp.float32)
        inp['ffn_b'] = jnp.zeros((D_MODEL,), jnp.float32)
        inp['w1'] = rn((4 * D_MODEL, D_MODEL))
        inp['b1'] = jnp.zeros((4 * D_MODEL,), jnp.float32)
        inp['w2'] = rn((D_MODEL, 4 * D_MODEL))
        inp['b2'] = jnp.zeros((D_MODEL,), jnp.float32)
        return inp
    _L0_attn_all = _L0_attn_setup()
    _L0_attn_in = {k: v for k, v in _L0_attn_all.items() if k in ('norm_g', 'norm_b', 'f_in_proj_w', 'f_conv_w', 'f_conv_b', 'f_x_proj_w', 'f_dt_proj_w', 'f_dt_proj_b', 'f_A_log', 'f_D', 'f_out_proj_w', 'b_in_proj_w', 'b_conv_w', 'b_conv_b', 'b_x_proj_w', 'b_dt_proj_w', 'b_dt_proj_b', 'b_A_log', 'b_D', 'b_out_proj_w', 'ffn_g', 'ffn_b', 'w1', 'b1', 'w2', 'b2')}
    del _L0_attn_all

    def _L0_xattn_setup():
        import jax, jax.numpy as jnp
        import numpy as np
        import math
        D_MODEL = 256
        N_HEADS = 16
        D_HEAD = D_MODEL // N_HEADS
        B, S = (4, 512)
        key = jax.random.key(seed)
        ks = jax.random.split(key, 11)
        sc = 1.0 / math.sqrt(D_MODEL)
        inp = {'query': jax.random.normal(ks[0], (B, S, D_MODEL), jnp.float32), 'key': jax.random.normal(ks[1], (B, S, D_MODEL), jnp.float32), 'value': jax.random.normal(ks[2], (B, S, D_MODEL), jnp.float32), 'mask': jnp.tril(jnp.ones((S, S), jnp.int32))[None, None, :, :], 'wq': jax.random.normal(ks[3], (D_MODEL, D_MODEL), jnp.float32) * sc, 'bq': jax.random.normal(ks[4], (D_MODEL,), jnp.float32) * sc, 'wk': jax.random.normal(ks[5], (D_MODEL, D_MODEL), jnp.float32) * sc, 'bk': jax.random.normal(ks[6], (D_MODEL,), jnp.float32) * sc, 'wv': jax.random.normal(ks[7], (D_MODEL, D_MODEL), jnp.float32) * sc, 'bv': jax.random.normal(ks[8], (D_MODEL,), jnp.float32) * sc, 'wo': jax.random.normal(ks[9], (D_MODEL, D_MODEL), jnp.float32) * sc, 'bo': jax.random.normal(ks[10], (D_MODEL,), jnp.float32) * sc}
        return inp
    _L0_xattn_all = _L0_xattn_setup()
    _L0_xattn_in = {k: v for k, v in _L0_xattn_all.items() if k in ('wq', 'bq', 'wk', 'bk', 'wv', 'bv', 'wo', 'bo')}
    del _L0_xattn_all

    def _L0_ffn_setup():
        import jax, jax.numpy as jnp
        import numpy as np
        import math
        BETA = 0.9
        THRESHOLD = 1.0
        NUM_STEPS = 5
        ALPHA = 2.0

        @jax.custom_vjp
        def spike_fn(u):
            return (u > 0).astype(u.dtype)

        def _spike_fwd(u):
            return (spike_fn(u), u)

        def _spike_bwd(u, g):
            s = jnp.pi / 2.0 * ALPHA * u
            return (g * (ALPHA / 2.0) / (1.0 + s * s),)
        spike_fn.defvjp(_spike_fwd, _spike_bwd)
        key = jax.random.key(seed)
        k1, k2, k3 = jax.random.split(key, 3)
        n_embd = 256
        x = jax.random.normal(k1, (4, 512, n_embd), dtype=jnp.float32)
        W_fc = jax.random.normal(k2, (4 * n_embd, n_embd), dtype=jnp.float32) / math.sqrt(n_embd)
        W_proj = jax.random.normal(k3, (n_embd, 4 * n_embd), dtype=jnp.float32) / math.sqrt(4 * n_embd)
        return {'x': x, 'W_fc': W_fc, 'W_proj': W_proj}
    _L0_ffn_all = _L0_ffn_setup()
    _L0_ffn_in = {k: v for k, v in _L0_ffn_all.items() if k in ('W_fc', 'W_proj')}
    del _L0_ffn_all
    return {'x': x, 'ctx_1024': ctx_1024, 'mask_1x1xSxS2_ik0': mask_1x1xSxS2_ik0, 'L0_attn_norm_g': _L0_attn_in['norm_g'], 'L0_attn_norm_b': _L0_attn_in['norm_b'], 'L0_attn_f_in_proj_w': _L0_attn_in['f_in_proj_w'], 'L0_attn_f_conv_w': _L0_attn_in['f_conv_w'], 'L0_attn_f_conv_b': _L0_attn_in['f_conv_b'], 'L0_attn_f_x_proj_w': _L0_attn_in['f_x_proj_w'], 'L0_attn_f_dt_proj_w': _L0_attn_in['f_dt_proj_w'], 'L0_attn_f_dt_proj_b': _L0_attn_in['f_dt_proj_b'], 'L0_attn_f_A_log': _L0_attn_in['f_A_log'], 'L0_attn_f_D': _L0_attn_in['f_D'], 'L0_attn_f_out_proj_w': _L0_attn_in['f_out_proj_w'], 'L0_attn_b_in_proj_w': _L0_attn_in['b_in_proj_w'], 'L0_attn_b_conv_w': _L0_attn_in['b_conv_w'], 'L0_attn_b_conv_b': _L0_attn_in['b_conv_b'], 'L0_attn_b_x_proj_w': _L0_attn_in['b_x_proj_w'], 'L0_attn_b_dt_proj_w': _L0_attn_in['b_dt_proj_w'], 'L0_attn_b_dt_proj_b': _L0_attn_in['b_dt_proj_b'], 'L0_attn_b_A_log': _L0_attn_in['b_A_log'], 'L0_attn_b_D': _L0_attn_in['b_D'], 'L0_attn_b_out_proj_w': _L0_attn_in['b_out_proj_w'], 'L0_attn_ffn_g': _L0_attn_in['ffn_g'], 'L0_attn_ffn_b': _L0_attn_in['ffn_b'], 'L0_attn_w1': _L0_attn_in['w1'], 'L0_attn_b1': _L0_attn_in['b1'], 'L0_attn_w2': _L0_attn_in['w2'], 'L0_attn_b2': _L0_attn_in['b2'], 'L0_xattn_wq': _L0_xattn_in['wq'], 'L0_xattn_bq': _L0_xattn_in['bq'], 'L0_xattn_wk': _L0_xattn_in['wk'], 'L0_xattn_bk': _L0_xattn_in['bk'], 'L0_xattn_wv': _L0_xattn_in['wv'], 'L0_xattn_bv': _L0_xattn_in['bv'], 'L0_xattn_wo': _L0_xattn_in['wo'], 'L0_xattn_bo': _L0_xattn_in['bo'], 'L0_ffn_W_fc': _L0_ffn_in['W_fc'], 'L0_ffn_W_proj': _L0_ffn_in['W_proj']}

def reference(x, ctx_1024, mask_1x1xSxS2_ik0, L0_attn_norm_g, L0_attn_norm_b, L0_attn_f_in_proj_w, L0_attn_f_conv_w, L0_attn_f_conv_b, L0_attn_f_x_proj_w, L0_attn_f_dt_proj_w, L0_attn_f_dt_proj_b, L0_attn_f_A_log, L0_attn_f_D, L0_attn_f_out_proj_w, L0_attn_b_in_proj_w, L0_attn_b_conv_w, L0_attn_b_conv_b, L0_attn_b_x_proj_w, L0_attn_b_dt_proj_w, L0_attn_b_dt_proj_b, L0_attn_b_A_log, L0_attn_b_D, L0_attn_b_out_proj_w, L0_attn_ffn_g, L0_attn_ffn_b, L0_attn_w1, L0_attn_b1, L0_attn_w2, L0_attn_b2, L0_xattn_wq, L0_xattn_bq, L0_xattn_wk, L0_xattn_bk, L0_xattn_wv, L0_xattn_bv, L0_xattn_wo, L0_xattn_bo, L0_ffn_W_fc, L0_ffn_W_proj):
    import jax
    import jax.numpy as jnp

    def _L0_attn_ref(x, norm_g, norm_b, f_in_proj_w, f_conv_w, f_conv_b, f_x_proj_w, f_dt_proj_w, f_dt_proj_b, f_A_log, f_D, f_out_proj_w, b_in_proj_w, b_conv_w, b_conv_b, b_x_proj_w, b_dt_proj_w, b_dt_proj_b, b_A_log, b_D, b_out_proj_w, ffn_g, ffn_b, w1, b1, w2, b2):
        import jax, jax.numpy as jnp
        import numpy as np
        B, L, D_MODEL = (2, 256, 256)
        D_STATE, D_CONV, EXPAND = (16, 4, 2)
        D_INNER = EXPAND * D_MODEL
        DT_RANK = (D_MODEL + 15) // 16

        def _silu(x):
            return x * jax.nn.sigmoid(x)

        def _layernorm(x, g, b, eps=1e-05):
            m = x.mean(-1, keepdims=True)
            v = ((x - m) ** 2).mean(-1, keepdims=True)
            return (x - m) / jnp.sqrt(v + eps) * g + b

        def _selective_scan(u, delta, A, Bm, Cm):

            def step(h, inp):
                u_t, d_t, B_t, C_t = inp
                dA = jnp.exp(d_t[:, :, None] * A[None])
                h = dA * h + (d_t * u_t)[:, :, None] * B_t[:, None, :]
                y = jnp.einsum('bdn,bn->bd', h, C_t)
                return (h, y)
            h0 = jnp.zeros((u.shape[0], A.shape[0], A.shape[1]), u.dtype)
            xs = (u.swapaxes(0, 1), delta.swapaxes(0, 1), Bm.swapaxes(0, 1), Cm.swapaxes(0, 1))
            _, ys = jax.lax.scan(step, h0, xs)
            return ys.swapaxes(0, 1)

        def _mamba(x, in_w, conv_w, conv_b, xp_w, dt_w, dt_b, A_log, Dp, out_w):
            xz = jnp.einsum('bld,ed->ble', x, in_w)
            xi, z = jnp.split(xz, 2, axis=-1)
            u = jax.lax.conv_general_dilated(xi.swapaxes(1, 2), conv_w, (1,), [(D_CONV - 1, 0)], dimension_numbers=('NCH', 'OIH', 'NCH'), feature_group_count=D_INNER)
            u = _silu(u.swapaxes(1, 2) + conv_b)
            xdbl = jnp.einsum('bld,ed->ble', u, xp_w)
            dt = jax.nn.softplus(jnp.einsum('blr,dr->bld', xdbl[..., :DT_RANK], dt_w) + dt_b)
            Bm = xdbl[..., DT_RANK:DT_RANK + D_STATE]
            Cm = xdbl[..., DT_RANK + D_STATE:]
            A = -jnp.exp(A_log)
            y = _selective_scan(u, dt, A, Bm, Cm) + u * Dp
            y = y * _silu(z)
            return jnp.einsum('bld,ed->ble', y, out_w)

        def _forward(x, norm_g, norm_b, f_in_proj_w, f_conv_w, f_conv_b, f_x_proj_w, f_dt_proj_w, f_dt_proj_b, f_A_log, f_D, f_out_proj_w, b_in_proj_w, b_conv_w, b_conv_b, b_x_proj_w, b_dt_proj_w, b_dt_proj_b, b_A_log, b_D, b_out_proj_w, ffn_g, ffn_b, w1, b1, w2, b2):
            x_norm = _layernorm(x, norm_g, norm_b)
            y_fwd = _mamba(x_norm, f_in_proj_w, f_conv_w, f_conv_b, f_x_proj_w, f_dt_proj_w, f_dt_proj_b, f_A_log, f_D, f_out_proj_w)
            x_rev = jnp.flip(x_norm, axis=1)
            y_bwd = _mamba(x_rev, b_in_proj_w, b_conv_w, b_conv_b, b_x_proj_w, b_dt_proj_w, b_dt_proj_b, b_A_log, b_D, b_out_proj_w)
            y = (y_fwd + jnp.flip(y_bwd, axis=1)) / 2.0
            x = x + y
            h = _layernorm(x, ffn_g, ffn_b)
            h = jax.nn.gelu(jnp.einsum('bld,ed->ble', h, w1) + b1, approximate=False)
            x = x + (jnp.einsum('bld,ed->ble', h, w2) + b2)
            return x
        return _forward(x, norm_g, norm_b, f_in_proj_w, f_conv_w, f_conv_b, f_x_proj_w, f_dt_proj_w, f_dt_proj_b, f_A_log, f_D, f_out_proj_w, b_in_proj_w, b_conv_w, b_conv_b, b_x_proj_w, b_dt_proj_w, b_dt_proj_b, b_A_log, b_D, b_out_proj_w, ffn_g, ffn_b, w1, b1, w2, b2)

    def _L0_xattn_ref(query, key, value, mask, wq, bq, wk, bk, wv, bv, wo, bo):
        import jax, jax.numpy as jnp
        import numpy as np
        import math
        D_MODEL = 256
        N_HEADS = 16
        D_HEAD = D_MODEL // N_HEADS
        B, S = (4, 512)
        b, s, _ = query.shape
        q = query @ wq.T + bq
        k = key @ wk.T + bk
        v = value @ wv.T + bv
        q = q.reshape(b, s, N_HEADS, D_HEAD).transpose(0, 2, 1, 3)
        k = k.reshape(b, s, N_HEADS, D_HEAD).transpose(0, 2, 1, 3)
        v = v.reshape(b, s, N_HEADS, D_HEAD).transpose(0, 2, 1, 3)
        scores = jnp.einsum('bhqd,bhkd->bhqk', q, k) / math.sqrt(D_HEAD)
        scores = jnp.where(mask == 0, jnp.float32(-1000000000.0), scores)
        attn = jax.nn.softmax(scores, axis=-1)
        out = jnp.einsum('bhqk,bhkd->bhqd', attn, v)
        out = out.transpose(0, 2, 1, 3).reshape(b, s, D_MODEL)
        return out @ wo.T + bo

    def _L0_ffn_ref(x, W_fc, W_proj):
        import jax, jax.numpy as jnp
        import numpy as np
        import math
        BETA = 0.9
        THRESHOLD = 1.0
        NUM_STEPS = 5
        ALPHA = 2.0

        @jax.custom_vjp
        def spike_fn(u):
            return (u > 0).astype(u.dtype)

        def _spike_fwd(u):
            return (spike_fn(u), u)

        def _spike_bwd(u, g):
            s = jnp.pi / 2.0 * ALPHA * u
            return (g * (ALPHA / 2.0) / (1.0 + s * s),)
        spike_fn.defvjp(_spike_fwd, _spike_bwd)
        h = jnp.square(jax.nn.relu(jnp.einsum('bsd,fd->bsf', x, W_fc)))
        y = jnp.einsum('bsf,df->bsd', h, W_proj)

        def step(mem, _):
            reset = jax.lax.stop_gradient(spike_fn(mem - THRESHOLD))
            mem_new = BETA * mem + y - reset * THRESHOLD
            spk = spike_fn(mem_new - THRESHOLD)
            return (mem_new, spk)
        mem0 = jnp.zeros_like(y)
        _, spks = jax.lax.scan(step, mem0, None, length=NUM_STEPS)
        return jnp.sum(spks, axis=0) / NUM_STEPS
    x = x + _L0_attn_ref(_layernorm(x, axis=-1), L0_attn_norm_g, L0_attn_norm_b, L0_attn_f_in_proj_w, L0_attn_f_conv_w, L0_attn_f_conv_b, L0_attn_f_x_proj_w, L0_attn_f_dt_proj_w, L0_attn_f_dt_proj_b, L0_attn_f_A_log, L0_attn_f_D, L0_attn_f_out_proj_w, L0_attn_b_in_proj_w, L0_attn_b_conv_w, L0_attn_b_conv_b, L0_attn_b_x_proj_w, L0_attn_b_dt_proj_w, L0_attn_b_dt_proj_b, L0_attn_b_A_log, L0_attn_b_D, L0_attn_b_out_proj_w, L0_attn_ffn_g, L0_attn_ffn_b, L0_attn_w1, L0_attn_b1, L0_attn_w2, L0_attn_b2)
    x = x + _L0_xattn_ref(_layernorm(x, axis=-1), ctx_1024, ctx_1024, mask_1x1xSxS2_ik0, L0_xattn_wq, L0_xattn_bq, L0_xattn_wk, L0_xattn_bk, L0_xattn_wv, L0_xattn_bv, L0_xattn_wo, L0_xattn_bo)
    x = x + _L0_ffn_ref(_layernorm(x, axis=-1), L0_ffn_W_fc, L0_ffn_W_proj)
    return x

_drawn_inputs = setup_inputs


def setup_inputs(seed=0):
    import zlib

    import numpy as np

    out = dict(_drawn_inputs(seed))
    spreads = {'L0_attn_norm_g': (1.0, 0.2),
     'L0_attn_norm_b': (0.0, 0.1),
     'L0_attn_f_conv_b': (0.0, 0.1),
     'L0_attn_f_D': (1.0, 0.2),
     'L0_attn_b_conv_b': (0.0, 0.1),
     'L0_attn_b_D': (1.0, 0.2),
     'L0_attn_ffn_g': (1.0, 0.2),
     'L0_attn_ffn_b': (0.0, 0.1),
     'L0_attn_b1': (0.0, 0.1),
     'L0_attn_b2': (0.0, 0.1)}
    factors = {}
    for name, (base, spread) in spreads.items():
        noise = np.random.default_rng([zlib.crc32(name.encode()), seed]).standard_normal(out[name].shape)
        drawn = base * np.exp(spread * noise) if base else spread * noise
        out[name] = jnp.asarray(drawn.astype(out[name].dtype))
    for name, factor in factors.items():
        out[name] = (out[name] * factor).astype(out[name].dtype)
    return out
```

```python
import concourse.bass as bass
import concourse.mybir as mybir
import numpy as np
from contextlib import ExitStack

B, T, D = 8, 512, 256
DI, NS, RK, CW = 512, 16, 16, 4
FF = 1024
H, DH = 16, 16
P = 128
KD, KI, KF, TT = D // P, DI // P, FF // P, T // P
CC = P // NS
NM = KI
NV = 4
NQ = 4
NG, NC = NM * NV, NM * NV * NQ
QR = 6 * DH + 3
EPS = 1e-5
MASKED = -float(2 ** 32)
STEPS, BETA, THRESHOLD = 5, 0.9, 1.0

COLS = {}
def _cols():
    at = 0
    for name, n in [("norm_g", KD), ("norm_b", KD), ("ffn_g", KD), ("ffn_b", KD), ("b1", KF), ("bq", KD), ("bk", KD)]:
        COLS[name] = at
        at += n
    for d in "fb":
        for name, n in [("conv_w", KI * CW), ("conv_b", KI), ("dt_b", KI), ("D", KI), ("A_log", NC)]:
            COLS[d + name] = at
            at += n
    COLS["end"] = at
_cols()

Q_PART = [0, 0, 1, 0, 2, 1]
K_PART = [0, 1, 0, 2, 0, 1]


class Stage:

    def __init__(self, sem, step=1, ahead=0):
        self.sem, self.step, self.ahead = sem, step, ahead

    def credit(self, eng):
        if self.ahead:
            eng.sem_inc(self.sem, self.ahead)

    def done(self, instruction):
        instruction.then_inc(self.sem, 1)

    def wait(self, eng, index):
        eng.wait_ge(self.sem, (index + 1) * self.step + self.ahead)


class Slots:

    def __init__(self, banks, full, free, keys):
        self.banks, self.full, self.free = banks, full, free
        self.where, self.uses = {}, [0] * len(banks)
        for n, key in enumerate(keys):
            k = n % len(banks)
            self.where[key] = (k, self.uses[k])
            self.uses[k] += 1

    def _at(self, key, b):
        k, n = self.where[key]
        return k, b * self.uses[k] + n

    def bank(self, key):
        return self.banks[self.where[key][0]]

    def claim(self, pe, key, b):
        k, n = self._at(key, b)
        self.free[k].wait(pe, n - 1)
        return self.banks[k]

    def written(self, key, instruction):
        self.full[self.where[key][0]].done(instruction)

    def wait_full(self, eng, key, b):
        k, n = self._at(key, b)
        self.full[k].wait(eng, n)
        return self.banks[k]

    def read(self, key, instruction):
        self.free[self.where[key][0]].done(instruction)

    def wait_read(self, eng, key, b):
        k, n = self._at(key, b)
        self.free[k].wait(eng, n)


def slot_keys():
    keys = [("nf", k) for k in range(KD)] + [("nr", k) for k in range(KD)]
    for d in range(2):
        keys += [("xi", d, m) for m in range(KI)] + [("z", d, m) for m in range(KI)]
        keys += [("xd", d)] + [("dt", d, m) for m in range(KI)] + [("Br", d), ("Cr", d)]
        keys += [("op", d, j) for j in range(TT // 2)]
    keys += [("fl", j) for j in range(TT // 2)]
    keys += [("hT", k) for k in range(KD)] + [("w1", m) for m in range(KF)] + [("w2", j) for j in range(TT // 2)]
    keys += [("k", m) for m in range(KD)] + [("v", j) for j in range(TT // 2)]
    keys += [("qn", k) for k in range(KD)] + [("q", m) for m in range(KD)] + [("mt",)]
    for g in range(H // 4):
        keys += [("av", g), ("ot", g)]
    keys += [("on", k) for k in range(KD)] + [("wo", j) for j in range(TT // 2)]
    keys += [("fn", k) for k in range(KD)] + [("fc", m) for m in range(KF)] + [("pr", j) for j in range(TT // 2)]
    return keys


def build(nc, a, out):
    f32, f32r, bf16, i32 = mybir.dt.float32, mybir.dt.float32r, mybir.dt.bfloat16, mybir.dt.int32
    ALU, ACT, AX = mybir.AluOpType, mybir.ActivationFunctionType, mybir.AxisListType

    at = [-(-nc.sbuf_base // 32) * 32]

    def sb(name, shape, dt=f32, offset=None):
        size = int(np.prod(shape[1:])) * (2 if dt == bf16 else 4)
        size = -(-size // 32) * 32
        if offset is None:
            offset = at[0]
            at[0] += size
        t = nc.alloc_sbuf_tensor_at(name, shape, dt, offset=offset)
        return t

    KB = 1024
    ident = sb("ident", [P, P])
    flip = sb("flip", [P, P])
    ident_bf = sb("ident_bf", [P, P], bf16)
    ones_bf = sb("ones_bf", [P, P], bf16)
    sel_r = sb("sel_r", [P, 2, NV, P], f32r)
    sel_y = sb("sel_y", [P, NV, 32])
    sel_bc = sb("sel_bc", [RK + 2 * NS, 2, P])
    cols = sb("cols", [P, COLS["end"]])
    minus_half = sb("minus_half", [P, TT])
    rows = sb("rows", [P, 3, D])
    w_xp = sb("w_xp", [P, 2, KI, RK + 2 * NS])
    w_dt = sb("w_dt", [RK, 2, DI])
    w_out = sb("w_out", [P, 2, KI, D])
    w_att = sb("w_att", [P, 4, KD, D])
    w_big = sb("w_big", [P, 16 * KB // 4])
    x_in = sb("x_in", [P, TT, D])
    x0 = sb("x0", [P, TT, D])
    x1 = sb("x1", [P, TT, D])
    xn = sb("xn", [P, TT, D])
    xnT = sb("xnT", [P, 2, KD, T])
    ctxT = xnT[:, 1, :, :]
    mask_bias = sb("mask_bias", [P, TT, T], bf16)
    mask_biasT = sb("mask_biasT", [P, TT, T], bf16)
    not_full = sb("not_full", [P, T])
    stats = sb("stats", [P, TT, 6])
    mv = sb("mv", [P, TT, 2])
    rstd = sb("rstd", [P, TT])
    row_keep = sb("row_keep", [P, TT])
    xd_sb = sb("xd_sb", [RK + 2 * NS, T])
    B_rep = sb("B_rep", [P, T])
    C_rep = sb("C_rep", [P, T])
    yt = sb("yt", [P, T])
    f0 = at[0]
    u = sb("u", [P, KI, T])
    zs = sb("zs", [P, KI, T])
    delta = sb("delta", [P, KI, T])
    xi = sb("xi", [P, KI, T + CW - 1])
    arena = at[0]
    parts = sb("parts", [P, NG, T], f32r, arena)
    a2 = arena + 32 * KB
    h = sb("h", [P, 2, NQ, T], f32, a2)
    hC = sb("hC", [P, 2, NQ, T], f32, a2 + 16 * KB)
    dA = sb("dA", [P, NQ, T], f32, a2 + 32 * KB)
    dBu = sb("dBu", [P, NQ, T], f32, a2 + 40 * KB)
    cut = [sb(f"cut{s}", [P, KI, T], f32r, a2 + 8 * KB * s) for s in range(4)]
    th_z = sb("th_z", [P, KI, T], f32, a2 + 32 * KB)
    th_c = sb("th_c", [P, KI, T], f32, a2 + 40 * KB)
    q_st = sb("q_st", [P, H, T], bf16, arena)
    k_st = sb("k_st", [P, H, T], bf16, arena + 16 * KB)
    pr = sb("pr", [P, 4, TT, T], f32, arena + 32 * KB)
    v_sb = sb("v_sb", [P, TT, H, 32], f32, arena + 64 * KB)
    g1 = sb("g1", [P, KF, T], f32, arena + 32 * KB)
    g0 = sb("g0", [P, T], f32, arena + 48 * KB)
    at[0] = arena + 80 * KB
    assert at[0] <= nc.sbuf_usable_end, (at[0], nc.sbuf_usable_end)
    qk = sb("qk", [P, 2, KD, T], f32, f0)
    qk_part = sb("qk_part", [P, 2, 3, KD, T], bf16, f0 + 8 * KB)
    oT = sb("oT", [P, 2, T], f32, f0 + 20 * KB)
    mask_i = sb("mask_i", [P, TT, T], i32, arena)
    maskT_i = sb("maskT_i", [P, TT, T], i32, arena + 8 * KB)
    keep = sb("keep", [P, TT, T], f32, arena + 16 * KB)
    keep_bf = sb("keep_bf", [P, TT, T], bf16, arena + 24 * KB)
    sel_raw = sb("sel_raw", [P, 2, NV, P], f32, arena + 32 * KB)
    m_col = sb("m_col", [P, TT, H], f32, f0 + 24 * KB)
    m_part = sb("m_part", [H, 3, T], bf16, f0 + 24 * KB + 256)
    m_rest = sb("m_rest", [H, T], f32, f0 + 24 * KB + 256 + 3 * KB)
    rsum = sb("rsum", [P, TT, 4], f32, f0 + 24 * KB + 256 + 5 * KB)
    mem = sb("mem", [P, TT, D], f32, f0)
    spk = sb("spk", [P, TT, D], f32, f0 + 4 * KB)
    cnt = sb("cnt", [P, TT, D], f32, f0 + 8 * KB)
    y_sb = sb("y_sb", [P, TT, D], f32, f0 + 12 * KB)
    tmp = sb("tmp", [P, TT, D], f32, f0 + 16 * KB)
    o_sb = xn

    w_in = w_big[:, :].rearrange("p (d k e) -> p d k e", d=2, k=KD)
    half = KD * FF
    w_up = w_big[:, 0:half].rearrange("p (k e) -> p k e", k=KD)
    w_down = w_big[:, half:].rearrange("p (k e) -> p k e", k=KF)

    qk_dram = nc.dram_tensor("qk_parts", (2, 3, D, T), bf16).ap()
    m_dram = nc.dram_tensor("max_parts", (3, H, T), bf16).ap()

    ctx = ExitStack()
    with ctx:
        pair = [ctx.enter_context(nc.psum_tensor(f"pair{i}", [P, 2, T], f32)) for i in range(2)]
        bank = [pair[i // 2][:, i % 2, :] for i in range(4)]
        y_bank = ctx.enter_context(nc.psum_tensor("y_bank", [P, T], f32))
        general = [ctx.enter_context(nc.psum_tensor(f"general{i}", [P, T], f32)) for i in range(3)]

        def stage(name, step=1, ahead=0):
            return Stage(ctx.enter_context(nc.semaphore(name)), step, ahead)

        G = Slots(general, [stage(f"full{i}") for i in range(3)], [stage(f"free{i}", ahead=1) for i in range(3)],
                  slot_keys())
        s_const = stage("const_dma", 16 * 13)
        s_mask = stage("mask_dma", 32)
        s_wbig = stage("w_big_dma", 32)
        s_x = stage("x_dma", 16)
        s_ctx = stage("ctx_dma", 16)
        s_parts = stage("parts_dma", 16 * 16)
        s_qkw = stage("qk_write_dma", 48)
        s_qkr = stage("qk_read_dma", 16 * 12)
        s_mw = stage("max_write_dma", 16)
        s_mr = stage("max_read_dma", 16)
        s_out = stage("out_dma", 16, ahead=16)
        setup_dve = stage("setup_dve")
        setup_pe = stage("setup_pe")
        setup_act = stage("setup_act")
        ln_stats = stage("ln_stats")
        ln_rstd = stage("ln_rstd")
        ln_out = stage("ln_out")
        conv = stage("conv")
        th_conv = stage("th_conv")
        th_gate = stage("th_gate")
        u_ready = stage("u_ready")
        soft = stage("soft")
        d_ready = stage("d_ready")
        hi_ready = stage("hi_ready")
        lo_ready = stage("lo_ready")
        s_rd = stage("spread_delta")
        s_ru = stage("spread_du")
        s_dA = stage("dA", ahead=2)
        s_dBu = stage("dBu", ahead=2)
        s_scan = stage("scan", ahead=4)
        s_hC = stage("hC", ahead=2)
        s_y = stage("y_sum", ahead=2)
        s_yread = stage("y_read", ahead=1)
        s_yT = stage("yT")
        x_free = stage("x_free", ahead=1)
        s_v = stage("v_const")
        s_part = stage("qk_cut")
        qk_hi = stage("qk_hi")
        qk_lo = stage("qk_lo")
        s_pre = stage("prescore")
        s_max = stage("maximum", ahead=4)
        m_cut = stage("m_cut")
        s_sc = stage("score")
        s_exp = stage("exp", ahead=2)
        o_ready = stage("o_ready")
        g_out = stage("g_out")
        out_ready = stage("out_ready")
        carrier = stage("carrier")
        block = ctx.enter_context(nc.Block())

        def col(name, k=0, n=1):
            return cols[:, COLS[name] + k:COLS[name] + k + n]

        def settle(eng):
            eng.sem_inc(carrier.sem, 1)

        @block.sync
        def _(sp):
            s_out.credit(sp)

            def dma(st, o, i):
                sp.dma_start(o, i).then_inc(st.sem, 16)

            def load_x(b):
                dma(s_x, x_in[:, :, :], a["x"][bass.ds(b * TT, TT)].rearrange("j p f -> p j f"))

            def load_in_proj():
                for d in range(2):
                    dma(s_wbig, w_in[:, d], a["w_in"][d].rearrange("(k p) e -> p k e", p=P))

            load_x(0)
            dma(s_const, ident[:, :], a["ident"])
            dma(s_const, flip[:, :], a["flip"])
            dma(s_const, cols[:, :], a["cols"])
            load_in_proj()
            dma(s_mask, mask_i[:, :, :], a["mask"].rearrange("(j p) t -> p j t", p=P))
            dma(s_mask, maskT_i[:, :, :], a["maskT"].rearrange("(j p) t -> p j t", p=P))
            dma(s_const, sel_raw[:, :, :, :], a["sel_r"])
            dma(s_const, sel_y[:, :, :], a["sel_y"])
            dma(s_const, sel_bc[:, :, :], a["sel_bc"])
            dma(s_const, rows[:, :, :], a["rows"].unsqueeze(0).broadcast_to((P, 3, D)))
            for d in range(2):
                dma(s_const, w_xp[:, d], a["w_xp"][d].rearrange("(k p) e -> p k e", p=P))
                dma(s_const, w_out[:, d], a["w_out"][d].rearrange("(k p) e -> p k e", p=P))
            dma(s_const, w_dt[:, :, :], a["w_dt"].rearrange("d r e -> r d e"))
            dma(s_const, w_att[:, :, :, :].rearrange("p w k e -> p (w k) e"),
                a["w_att"].rearrange("w (k p) e -> p (w k) e", p=P))

            with sp.Fori(0, B) as b:
                for d in range(2):
                    for s in range(4):
                        (lo_ready if s % 2 else hi_ready).wait(sp, 4 * b + 2 * d + s // 2)
                        for q in range(NQ):
                            dma(s_parts, parts[32 * s:32 * s + 32, q:NG:NQ, :].bitcast(f32),
                                cut[s][32 * q:32 * q + 32, :, :].bitcast(f32))
                G.wait_full(sp, ("z", 1, KI - 1), b)
                dma(s_ctx, ctxT, a["ctxT"][:, bass.ds(b * T, T)].rearrange("(k p) t -> p k t", p=P))
                dma(s_wbig, w_up, a["w1"].rearrange("(k p) e -> p k e", p=P))
                dma(s_wbig, w_down, a["w2"].rearrange("(k p) e -> p k e", p=P))
                x_free.wait(sp, b)
                settle(sp)
                load_x((b + 1) % B)
                G.wait_full(sp, ("w2", TT // 2 - 1), b)
                dma(s_wbig, w_up, a["w_fc"].rearrange("(k p) e -> p k e", p=P))
                dma(s_wbig, w_down, a["w_proj"].rearrange("(k p) e -> p k e", p=P))
                for n, (dst, which) in enumerate([(k_st, K_PART), (q_st, Q_PART)]):
                    s_part.wait(sp, 2 * b + n)
                    for part in range(3):
                        dma(s_qkw, qk_dram[n, part].rearrange("(k p) t -> p k t", p=P), qk_part[:, n, part])
                    s_qkw.wait(sp, 2 * b + n)
                    for band, part in enumerate(which):
                        dma(s_qkr, dst[DH * band:DH * band + DH, :, :],
                            qk_dram[n, part].rearrange("(h e) t -> e h t", e=DH))
                m_cut.wait(sp, b)
                dma(s_mw, m_dram.rearrange("s h t -> h s t"), m_part[:, :, :])
                s_mw.wait(sp, b)
                dma(s_mr, q_st[6 * DH:QR, :, :], m_dram)
                G.wait_full(sp, ("pr", TT // 2 - 1), b)
                load_in_proj()
                out_ready.wait(sp, b)
                dma(s_out, out[bass.ds(b * TT, TT)].rearrange("j p f -> p j f"), tmp[:, :, :])
                s_out.wait(sp, b)
                settle(sp)
            s_x.wait(sp, B)
            s_wbig.wait(sp, 3 * B)

        @block.tensor
        def _(pe):
            s_y.credit(pe)

            def mm(o, lhsT, rhs, start=True, stop=True):
                return pe.matmul(o, lhsT, rhs, start=start, stop=stop)

            def to_features(keys, src, b):
                for k in range(KD):
                    bk = G.claim(pe, (keys, k), b)
                    for j in range(TT):
                        last = pe.transpose(bk[:, j * P:(j + 1) * P], src[:, j, k * P:(k + 1) * P], ident[:, :])
                    G.written((keys, k), last)

            def project(key, w, rhs, kn, b, rows_out=P):
                bk = G.claim(pe, key, b)
                for k in range(kn):
                    last = mm(bk[0:rows_out, :], w(k), rhs(k), k == 0, k == kn - 1)
                G.written(key, last)

            def project_tokens(key, lhsT, w, kn, jj, b):
                bk = G.claim(pe, key, b)
                for half_ in range(2):
                    for k in range(kn):
                        last = mm(bk[:, half_ * D:(half_ + 1) * D], lhsT(k, 2 * jj + half_), w(k), k == 0, k == kn - 1)
                G.written(key, last)

            def tok(src):
                return lambda k, j: src[:, k, j * P:(j + 1) * P]

            setup_dve.wait(pe, 0)
            for k in range(TT):
                last = mm(y_bank[:, :], ones_bf[:, :], keep_bf[:, k, :], k == 0, k == TT - 1)
            setup_pe.done(last)
            s_const.wait(pe, 0)
            setup_dve.wait(pe, 1)

            def spread(U, m, v):
                for q in range(NQ):
                    c = U * NC + m * NV * NQ + v * NQ + q
                    s_dA.wait(pe, c - 2)
                    s_rd.done(mm(bank[q % 2], sel_r[:, 0, v, :], parts[:, bass.ds(m * NQ + q, 1), :].squeeze(1)))
                    s_dBu.wait(pe, c - 2)
                    s_ru.done(mm(bank[2 + q % 2], sel_r[:, 1, v, :], parts[:, bass.ds(m * NQ + q, 1), :].squeeze(1)))

            def sum_states(U, m, v):
                s_hC.wait(pe, U * NG + m * NV + v)
                if v == 0:
                    s_yread.wait(pe, U * NM + m - 1)
                for q in range(NQ):
                    last = mm(y_bank[32 * q:32 * q + 32, :], sel_y[:, v, :], hC[:, v % 2, q, :], v == 0, v == NV - 1)
                s_y.done(last)

            with pe.Fori(0, B) as b:
                ln_out.wait(pe, 5 * b + 1)
                to_features("nf", xn, b)
                for k in range(KD):
                    bk = G.claim(pe, ("nr", k), b)
                    for j in range(TT):
                        r = TT - 1 - j
                        last = mm(bk[:, r * P:(r + 1) * P], xn[:, j, k * P:(k + 1) * P], flip[:, :])
                    G.written(("nr", k), last)
                s_wbig.wait(pe, 3 * b)
                for d in range(2):
                    U = 2 * b + d
                    for k in range(KD):
                        G.wait_read(pe, ("nr" if d else "nf", k), b)
                    for key, first in (("xi", 0), ("z", DI)):
                        for m in range(KI):
                            e = first + m * P
                            project((key, d, m), lambda k: w_in[:, d, k, e:e + P], lambda k: xnT[:, d, k, :], KD, b)
                    u_ready.wait(pe, U)
                    project(("xd", d), lambda k: w_xp[:, d, k, :], lambda k: u[:, k, :], KI, b, RK + 2 * NS)
                    G.wait_read(pe, ("xd", d), b)
                    for m in range(KI):
                        project(("dt", d, m), lambda k: w_dt[:, d, m * P:(m + 1) * P], lambda k: xd_sb[0:RK, :], 1, b)
                    for n, key in enumerate(("Br", "Cr")):
                        project((key, d), lambda k: sel_bc[:, n, :], lambda k: xd_sb[:, :], 1, b)
                    s_parts.wait(pe, U)
                    for v in range(NV):
                        spread(U, 0, v)
                        if v >= 2:
                            sum_states(U, 0, v - 2)
                    with pe.Fori(1, NM) as m:
                        for v in range(NV):
                            spread(U, m, v)
                            sum_states(U, m if v >= 2 else m - 1, (v + 2) % NV)
                    for v in (2, 3):
                        sum_states(U, NM - 1, v)
                    s_yT.wait(pe, U * NM + NM - 1)
                    for jj in range(TT // 2):
                        project_tokens(("op", d, jj), tok(delta), lambda k: w_out[:, d, k, :], KI, jj, b)
                for jj in range(TT // 2):
                    G.wait_read(pe, ("op", 1, jj), b)
                for jj in range(TT // 2):
                    bk = G.claim(pe, ("fl", jj), b)
                    for half_ in range(2):
                        j = 2 * jj + half_
                        last = mm(bk[:, half_ * D:(half_ + 1) * D], flip[:, :], xn[:, TT - 1 - j, :])
                    G.written(("fl", jj), last)
                ln_out.wait(pe, 5 * b + 2)
                to_features("hT", xn, b)
                s_wbig.wait(pe, 3 * b + 1)
                for k in range(KD):
                    G.wait_read(pe, ("hT", k), b)
                for m in range(KF):
                    project(("w1", m), lambda k: w_up[:, k, m * P:(m + 1) * P], lambda k: xnT[:, 0, k, :], KD, b)
                for m in range(KF):
                    G.wait_read(pe, ("w1", m), b)
                for jj in range(TT // 2):
                    project_tokens(("w2", jj), tok(g1), lambda k: w_down[:, k, :], KF, jj, b)
                s_ctx.wait(pe, b)
                for m in range(KD):
                    project(("k", m), lambda k: w_att[:, 1, k, m * P:(m + 1) * P], lambda k: ctxT[:, k, :], KD, b)
                for jj in range(TT // 2):
                    project_tokens(("v", jj), tok(ctxT), lambda k: w_att[:, 2, k, :], KD, jj, b)
                ln_out.wait(pe, 5 * b + 3)
                to_features("qn", xn, b)
                for k in range(KD):
                    G.wait_read(pe, ("qn", k), b)
                for m in range(KD):
                    project(("q", m), lambda k: w_att[:, 0, k, m * P:(m + 1) * P], lambda k: xnT[:, 0, k, :], KD, b)
                s_qkr.wait(pe, b)
                settle(pe)
                with pe.Fori(0, H) as h_:
                    for j in range(TT):
                        n = (b * H + h_) * TT + j
                        s_max.wait(pe, n - 4)
                        mm(bank[j], q_st[0:6 * DH, bass.ds(h_, 1), j * P:(j + 1) * P].squeeze(1),
                           k_st[0:6 * DH, bass.ds(h_, 1), :].squeeze(1), True, False)
                        s_pre.done(mm(bank[j], ident_bf[:, :], mask_bias[:, j, :], False, True))
                s_max.wait(pe, (b + 1) * H * TT - 1)
                bk = G.claim(pe, ("mt",), b)
                for j in range(TT):
                    last = pe.transpose(bk[0:H, j * P:(j + 1) * P], m_col[:, j, :], ident[:, :])
                G.written(("mt",), last)
                s_mr.wait(pe, b)
                s_v.wait(pe, b)
                for jj in range(TT // 2):
                    G.wait_read(pe, ("v", jj), b)
                for g in range(H // 4):
                    for hh in range(4):
                        hd = 4 * g + hh
                        for s in range(2):
                            n = (b * H + hd) * 2 + s
                            s_exp.wait(pe, n - 2)
                            for t in range(2):
                                kt = 2 * s + t
                                mm(pair[s][:, t, :], k_st[0:QR, hd, kt * P:(kt + 1) * P], q_st[0:QR, hd, :], True, False)
                                last = mm(pair[s][:, t, :], ident_bf[:, :], mask_biasT[:, kt, :], False, True)
                            s_sc.done(last)
                    s_exp.wait(pe, (b * H + 4 * g + 3) * 2 + 1)
                    bk = G.claim(pe, ("av", g), b)
                    for kt in range(TT):
                        for hh in range(4):
                            last = mm(bk[32 * hh:32 * hh + 32, :], v_sb[:, kt, 4 * g + hh, :], pr[:, hh, kt, :],
                                      kt == 0, kt == TT - 1)
                    G.written(("av", g), last)
                    G.wait_read(pe, ("av", g), b)
                    bk = G.claim(pe, ("ot", g), b)
                    for j in range(TT):
                        last = pe.transpose(bk[:, j * P:(j + 1) * P], oT[:, g % 2, j * P:(j + 1) * P], ident[:, :])
                    G.written(("ot", g), last)
                o_ready.wait(pe, (H // 4) * (b + 1) - 1)
                to_features("on", o_sb, b)
                for k in range(KD):
                    G.wait_read(pe, ("on", k), b)
                for jj in range(TT // 2):
                    project_tokens(("wo", jj), tok(xnT[:, 0]), lambda k: w_att[:, 3, k, :], KD, jj, b)
                ln_out.wait(pe, 5 * b + 4)
                to_features("fn", xn, b)
                s_wbig.wait(pe, 3 * b + 2)
                for k in range(KD):
                    G.wait_read(pe, ("fn", k), b)
                for m in range(KF):
                    project(("fc", m), lambda k: w_up[:, k, m * P:(m + 1) * P], lambda k: xnT[:, 0, k, :], KD, b)
                g_out.wait(pe, KF * (b + 1) - 1)
                for jj in range(TT // 2):
                    project_tokens(("pr", jj), tok(g1), lambda k: w_down[:, k, :], KF, jj, b)

        @block.scalar
        def _(act):
            s_dA.credit(act)
            s_exp.credit(act)

            def f(o, i, fn=ACT.Copy, **kw):
                return act.activation(o, i, fn, **kw)

            def evacuate(key, o, b, fn=ACT.Copy, view=None, **kw):
                bk = G.wait_full(act, key, b)
                G.read(key, f(o, bk[:, :] if view is None else view(bk), fn, **kw))

            s_const.wait(act, 0)
            for n, d in enumerate("fb"):
                last = f(col(d + "A_log", 0, NC), col(d + "A_log", 0, NC), ACT.Exp)
            setup_act.done(last)
            setup_dve.wait(act, 1)

            with act.Fori(0, B) as b:
                for n, key in enumerate(("nf", "nr")):
                    for k in range(KD):
                        evacuate((key, k), xnT[:, n, k, :], b, ACT.Identity, scale=col("norm_g", k), bias=col("norm_b", k))
                for d in range(2):
                    U, dn = 2 * b + d, "fb"[d]
                    for m in range(KI):
                        evacuate(("xi", d, m), xi[:, m, CW - 1:], b)
                    for m in range(KI):
                        bk = G.wait_full(act, ("z", d, m), b)
                        th_gate.done(f(th_z[:, m, :], bk[:, :], ACT.Tanh, scale=0.5))
                    conv.wait(act, U)
                    th_conv.done(f(th_c[:, :, :], delta[:, :, :], ACT.Tanh))
                    evacuate(("xd", d), xd_sb[:, :], b, view=lambda bk: bk[0:RK + 2 * NS, :])
                    for m in range(KI):
                        bk = G.wait_full(act, ("dt", d, m), b)
                        f(th_z[:, m, :], bk[:, :], ACT.Abs, bias=col(dn + "dt_b", m))
                        G.read(("dt", d, m), f(delta[:, m, :], bk[:, :], ACT.Relu, bias=col(dn + "dt_b", m)))
                    evacuate(("Br", d), B_rep[:, :], b)
                    evacuate(("Cr", d), C_rep[:, :], b)
                    act.drain()
                    f(th_z[:, :, :], th_z[:, :, :], ACT.Exp, scale=-1.0)
                    act.drain()
                    soft.done(f(th_z[:, :, :], th_z[:, :, :], ACT.Ln, bias=1.0))
                    d_ready.wait(act, 2 * U)
                    hi_ready.done(f(cut[0][:, :, :], delta[:, :, :]))
                    d_ready.wait(act, 2 * U + 1)
                    hi_ready.done(f(cut[2][:, :, :], xi[:, :, CW - 1:]))
                    with act.Fori(0, NM) as m:
                        for v in range(NV):
                            for q in range(NQ):
                                c = U * NC + m * NV * NQ + v * NQ + q
                                s_rd.wait(act, c)
                                s_scan.wait(act, c - 4)
                                at_ = COLS[dn + "A_log"] + v * NQ + q
                                s_dA.done(f(dA[:, q, :], bank[q % 2], ACT.Exp,
                                            scale=cols[:, bass.ds(m * (NV * NQ) + at_, 1)]))
                    if d == 1:
                        for jj in range(TT // 2):
                            evacuate(("op", 1, jj), xn[:, 2 * jj:2 * jj + 2, :], b,
                                     view=lambda bk: bk[:, :].rearrange("p (j f) -> p j f", j=2))
                for k in range(KD):
                    evacuate(("hT", k), xnT[:, 0, k, :], b, ACT.Identity, scale=col("ffn_g", k), bias=col("ffn_b", k))
                for m in range(KF):
                    evacuate(("w1", m), g1[:, m, :], b, ACT.Gelu, bias=col("b1", m))
                for n in range(2):
                    if n == 0:
                        for m in range(KD):
                            evacuate(("k", m), qk[:, 0, m, :], b, ACT.Identity, bias=col("bk", m))
                        act.drain()
                    else:
                        for k in range(KD):
                            evacuate(("qn", k), xnT[:, 0, k, :], b)
                        for m in range(KD):
                            G.wait_read(act, ("q", m), b)
                    qk_hi.done(f(qk_part[:, n, 0], qk[:, n]))
                    qk_lo.wait(act, 2 * b + n)
                    qk_hi.done(f(qk_part[:, n, 1], qk[:, n]))
                for g in range(H // 4):
                    for hh in range(4):
                        for s in range(2):
                            s_sc.wait(act, (b * H + 4 * g + hh) * 2 + s)
                            s_exp.done(f(pr[:, hh, 2 * s:2 * s + 2, :], pair[s][:, :, :], ACT.Exp, scale=0.25))
                    evacuate(("av", g), oT[:, g % 2, :], b)
                for k in range(KD):
                    evacuate(("on", k), xnT[:, 0, k, :], b)
                for k in range(KD):
                    evacuate(("fn", k), xnT[:, 0, k, :], b)
                for m in range(KF):
                    evacuate(("fc", m), g0[:, :], b, ACT.Relu)
                    act.drain()
                    g_out.done(f(g1[:, m, :], g0[:, :], ACT.Square))
                    act.drain()

        @block.vector
        def _(dve):
            for st in (s_dBu, s_scan, s_yread, s_max, x_free):
                st.credit(dve)
            for st in G.free:
                st.credit(dve)

            def norm(n, b, src, dst):
                for j in range(TT):
                    dve.bn_stats(stats[:, j, :], src[:, j, :])
                dve.drain()
                for j in range(TT):
                    last = dve.bn_aggr(mv[:, j, :], stats[:, j, :])
                ln_stats.done(last)
                ln_rstd.wait(dve, 5 * b + n)
                for j in range(TT):
                    last = dve.tensor_scalar(dst[:, j, :], src[:, j, :], mv[:, j, 0:1], rstd[:, j:j + 1],
                                             ALU.subtract, ALU.mult)
                ln_out.done(last)
                dve.drain()

            def two(ap, jj):
                return ap[:, 2 * jj:2 * jj + 2, :]

            def add_bank(key, dst, jj, b):
                bk = G.wait_full(dve, key, b)
                G.read(key, dve.tensor_tensor(two(dst, jj), two(dst, jj), bk[:, :].rearrange("p (j f) -> p j f", j=2), ALU.add))

            s_const.wait(dve, 0)
            s_mask.wait(dve, 0)
            setup_act.wait(dve, 0)
            dve.memset(ones_bf[:, :], 1.0)
            dve.memset(minus_half[:, :], -0.5)
            dve.tensor_copy(ident_bf[:, :], ident[:, :])
            dve.tensor_copy(sel_r[:, :, :, :], sel_raw[:, :, :, :])
            dve.tensor_scalar(keep_bf[:, :, :], maskT_i[:, :, :], 0.0, None, ALU.not_equal)
            for dn in "fb":
                cw = col(dn + "conv_w", 0, KI * CW + KI)
                dve.tensor_scalar(cw, cw, 0.5, None, ALU.mult)
                al = col(dn + "A_log", 0, NC)
                dve.tensor_scalar(al, al, -1.0, None, ALU.mult)
            last = dve.tensor_scalar(w_out[:, :, :, :], w_out[:, :, :, :], 0.25, None, ALU.mult)
            setup_dve.done(last)
            setup_pe.wait(dve, 0)
            dve.tensor_scalar(not_full[:, :], y_bank[:, :], 0.0, None, ALU.is_gt)
            dve.tensor_scalar(keep[:, :, :], maskT_i[:, :, :], 0.0, MASKED, ALU.is_equal, ALU.mult)
            dve.drain()
            dve.tensor_tensor(mask_biasT[:, :, :], keep[:, :, :],
                              not_full[:, :].unsqueeze(1).broadcast_to((P, TT, T)), ALU.mult)
            dve.drain()
            dve.tensor_scalar(keep[:, :, :], mask_i[:, :, :], 0.0, None, ALU.not_equal)
            dve.drain()
            dve.reduce_max(row_keep[:, :], keep[:, :, :], AX.X)
            dve.drain()
            dve.tensor_scalar(keep[:, :, :], mask_i[:, :, :], 0.0, MASKED, ALU.is_equal, ALU.mult)
            dve.drain()
            for j in range(TT):
                last = dve.tensor_scalar(mask_bias[:, j, :], keep[:, j, :], row_keep[:, j:j + 1], None, ALU.mult)
            setup_dve.done(last)
            dve.drain()

            def group(U, m, v):
                for q in range(NQ + 1):
                    if q < NQ:
                        c = U * NC + m * NV * NQ + v * NQ + q
                        s_ru.wait(dve, c)
                        s_scan.wait(dve, c - 4)
                        s_dBu.done(dve.tensor_tensor(dBu[:, q, :], bank[2 + q % 2], B_rep[:, :], ALU.mult))
                    if q == 1:
                        s_hC.wait(dve, U * NG + m * NV + v - 2)
                    if q > 0:
                        c = U * NC + m * NV * NQ + v * NQ + q - 1
                        s_dA.wait(dve, c)
                        s_dBu.wait(dve, c)
                        s_scan.done(dve.tensor_tensor_scan(h[:, v % 2, q - 1, :], dA[:, q - 1, :], dBu[:, q - 1, :],
                                                           0.0, ALU.mult, ALU.add))

            def read_y(U, m, dn):
                s_y.wait(dve, U * NG + m * NV + NV - 1)
                blk = bass.ds(m, 1)
                s_yread.done(dve.scalar_tensor_tensor(yt[:, :], u[:, blk, :].squeeze(1), cols[:, bass.ds(m + COLS[dn + "D"], 1)],
                                                      y_bank[:, :], ALU.mult, ALU.add))
                s_yread.wait(dve, U * NM + m)
                s_yT.done(dve.tensor_tensor(delta[:, blk, :].squeeze(1), yt[:, :], zs[:, blk, :].squeeze(1), ALU.mult))

            with dve.Fori(0, B) as b:
                s_x.wait(dve, b)
                norm(0, b, x_in, x0)
                norm(1, b, x0, xn)
                s_out.wait(dve, b - 1)
                for d in range(2):
                    U, dn = 2 * b + d, "fb"[d]
                    dve.memset(xi[:, :, 0:CW - 1], 0.0)
                    for m in range(KI):
                        G.wait_read(dve, ("xi", d, m), b)
                    settle(dve)
                    dve.drain()
                    for k in range(CW):
                        for m in range(KI):
                            w = col(dn + "conv_w", CW * m + k)
                            if k == 0:
                                last = dve.tensor_scalar(delta[:, m, :], xi[:, m, 0:T], w, col(dn + "conv_b", m),
                                                         ALU.mult, ALU.add)
                            else:
                                last = dve.scalar_tensor_tensor(delta[:, m, :], xi[:, m, k:k + T], w, delta[:, m, :],
                                                                ALU.mult, ALU.add)
                        if k < CW - 1:
                            dve.drain()
                    conv.done(last)
                    for m in range(KI):
                        th_gate.wait(dve, U * KI + m)
                        G.read(("z", d, m), dve.scalar_tensor_tensor(zs[:, m, :], th_z[:, m, :], 1.0, G.bank(("z", d, m))[:, :],
                                                                     ALU.add, ALU.mult))
                    th_conv.wait(dve, U)
                    u_ready.done(dve.scalar_tensor_tensor(u[:, :, :], th_c[:, :, :], 1.0, delta[:, :, :], ALU.add, ALU.mult))
                    soft.wait(dve, U)
                    du = xi[:, :, CW - 1:]
                    d_ready.done(dve.tensor_tensor(delta[:, :, :], delta[:, :, :], th_z[:, :, :], ALU.add))
                    dve.drain()
                    d_ready.done(dve.tensor_tensor(du, delta[:, :, :], u[:, :, :], ALU.mult))
                    dve.drain()
                    for n, src in enumerate((delta[:, :, :], du)):
                        hi_ready.wait(dve, 2 * U + n)
                        lo_ready.done(dve.tensor_tensor(cut[2 * n + 1][:, :, :], src, cut[2 * n][:, :, :].bitcast(f32),
                                                        ALU.subtract))
                    G.wait_read(dve, ("Br", d), b)
                    for v in range(NV):
                        if v == 0:
                            s_parts.wait(dve, U)
                        group(U, 0, v)
                    with dve.Fori(1, NM) as m:
                        for v in range(NV):
                            group(U, m, v)
                            if v == 1:
                                read_y(U, m - 1, dn)
                    read_y(U, NM - 1, dn)
                    if d == 0:
                        for jj in range(TT // 2):
                            add_bank(("op", 0, jj), x0, jj, b)
                for jj in range(TT // 2):
                    add_bank(("fl", jj), x0, jj, b)
                dve.drain()
                x_free.done(dve.tensor_tensor(x1[:, :, :], x_in[:, :, :], x0[:, :, :], ALU.add))
                norm(2, b, x0, xn)
                dve.tensor_tensor(x1[:, :, :], x1[:, :, :], rows[:, 0, :].unsqueeze(1).broadcast_to((P, TT, D)), ALU.add)
                dve.drain()
                for jj in range(TT // 2):
                    add_bank(("w2", jj), x1, jj, b)
                dve.drain()

                def cut_three(n):
                    qk_hi.wait(dve, 4 * b + 2 * n)
                    qk_lo.done(dve.tensor_tensor(qk[:, n], qk[:, n], qk_part[:, n, 0], ALU.subtract))
                    qk_hi.wait(dve, 4 * b + 2 * n + 1)
                    s_part.done(dve.tensor_tensor(qk_part[:, n, 2], qk[:, n], qk_part[:, n, 1], ALU.subtract))

                norm(3, b, x1, xn)
                cut_three(0)
                for jj in range(TT // 2):
                    key = ("v", jj)
                    bk = G.wait_full(dve, key, b)
                    G.read(key, dve.tensor_tensor(
                        v_sb[:, 2 * jj:2 * jj + 2, :, 0:DH], bk[:, :].rearrange("p (j h e) -> p j h e", j=2, h=H),
                        rows[:, 1, :].rearrange("p (h e) -> p h e", h=H).unsqueeze(1).broadcast_to((P, 2, H, DH)), ALU.add))
                for m in range(KD):
                    bk = G.wait_full(dve, ("q", m), b)
                    G.read(("q", m), dve.scalar_tensor_tensor(qk[:, 1, m, :], bk[:, :], col("bq", m), not_full[:, :],
                                                              ALU.add, ALU.mult))
                cut_three(1)
                with dve.Fori(0, H) as h_:
                    for j in range(TT):
                        s_pre.wait(dve, (b * H + h_) * TT + j)
                        s_max.done(dve.reduce_max(m_col[:, j, bass.ds(h_, 1)], bank[j], AX.X))
                bk = G.wait_full(dve, ("mt",), b)
                dve.tensor_scalar(m_part[:, 0, :], bk[0:H, :], -1.0, None, ALU.mult)
                dve.drain()
                G.read(("mt",), dve.scalar_tensor_tensor(m_rest[:, :], bk[0:H, :], -1.0, m_part[:, 0, :], ALU.mult, ALU.subtract))
                dve.drain()
                dve.tensor_copy(m_part[:, 1, :], m_rest[:, :])
                dve.drain()
                m_cut.done(dve.tensor_tensor(m_part[:, 2, :], m_rest[:, :], m_part[:, 1, :], ALU.subtract))
                for g in range(H // 4):
                    bk = G.wait_full(dve, ("ot", g), b)
                    o = bk[:, :].rearrange("p (j h e) -> p j h e", j=TT, h=4)
                    dve.reciprocal(rsum[:, :, :], o[:, :, :, DH:DH + 1].squeeze(3))
                    dve.drain()
                    dst = o_sb[:, :, g * 4 * DH:(g + 1) * 4 * DH].rearrange("p j (h e) -> p j h e", h=4)
                    for j in range(TT):
                        last = dve.tensor_tensor(dst[:, j], o[:, j, :, 0:DH],
                                                 rsum[:, j, :].unsqueeze(2).broadcast_to((P, 4, DH)), ALU.mult)
                        if j == TT - 2:
                            o_last = last
                    G.read(("ot", g), last)
                    dve.drain()
                    o_ready.done(dve.memset(rsum[:, 0, 0:1], 0.0))
                    dve.drain()
                for jj in range(TT // 2):
                    add_bank(("wo", jj), x1, jj, b)
                dve.drain()
                dve.tensor_tensor(x1[:, :, :], x1[:, :, :], rows[:, 2, :].unsqueeze(1).broadcast_to((P, TT, D)), ALU.add)
                dve.drain()
                norm(4, b, x1, xn)
                for jj in range(TT // 2):
                    key = ("pr", jj)
                    bk = G.wait_full(dve, key, b)
                    G.read(key, dve.tensor_copy(two(y_sb, jj), bk[:, :].rearrange("p (j f) -> p j f", j=2)))
                dve.drain()
                A3 = (slice(None),) * 3
                dve.tensor_scalar(spk[A3], y_sb[A3], THRESHOLD, None, ALU.is_gt)
                dve.tensor_scalar(cnt[A3], y_sb[A3], THRESHOLD, None, ALU.is_gt)
                for step in range(1, STEPS):
                    prev = y_sb if step == 1 else mem
                    dve.drain()
                    dve.scalar_tensor_tensor(tmp[A3], prev[A3], BETA, y_sb[A3], ALU.mult, ALU.add)
                    dve.drain()
                    dve.tensor_tensor(mem[A3], tmp[A3], spk[A3], ALU.subtract)
                    dve.drain()
                    dve.scalar_tensor_tensor(cnt[A3], mem[A3], THRESHOLD, cnt[A3], ALU.is_gt, ALU.add)
                    if step < STEPS - 1:
                        dve.tensor_scalar(spk[A3], mem[A3], THRESHOLD, None, ALU.is_gt)
                dve.drain()
                out_ready.done(dve.scalar_tensor_tensor(tmp[A3], cnt[A3], 1.0 / STEPS, x1[A3], ALU.mult, ALU.add))
                dve.drain()

        @block.gpsimd
        def _(pool):
            s_hC.credit(pool)

            def rstd_of(n, b):
                ln_stats.wait(pool, 5 * b + n)
                settle(pool)
                pool.tensor_scalar(rstd[:, :], mv[:, :, 1], EPS, None, ALU.add)
                pool.drain()
                ln_rstd.done(pool.tensor_tensor(rstd[:, :], rstd[:, :], minus_half[:, :], ALU.pow))
                pool.drain()

            setup_dve.wait(pool, 1)
            with pool.Fori(0, B) as b:
                rstd_of(0, b)
                rstd_of(1, b)
                for d in range(2):
                    U = 2 * b + d
                    G.wait_read(pool, ("Cr", d), b)
                    settle(pool)
                    with pool.Fori(0, NM) as m:
                        for v in range(NV):
                            s_scan.wait(pool, U * NC + m * NV * NQ + v * NQ + NQ - 1)
                            s_y.wait(pool, U * NG + m * NV + v - 2)
                            s_hC.done(pool.tensor_tensor(hC[:, v % 2], h[:, v % 2],
                                                         C_rep[:, :].unsqueeze(1).broadcast_to((P, NQ, T)), ALU.mult))
                rstd_of(2, b)
                pool.memset(k_st[6 * DH:QR, :, :], 1.0)
                pool.drain()
                pool.memset(v_sb[:, :, :, DH:32], 0.0)
                pool.drain()
                s_v.done(pool.memset(v_sb[:, :, :, DH:DH + 1], 1.0))
                rstd_of(3, b)
                rstd_of(4, b)


def _selectors():
    i = np.arange(P)
    ident = np.eye(P, dtype=np.float32)
    sel_r = np.zeros((P, 2, NV, P), np.float32)
    sel_y = np.zeros((P, NV, 32), np.float32)
    sel_bc = np.zeros((RK + 2 * NS, 2, P), np.float32)
    for v in range(NV):
        for p in range(P):
            channel = CC * v + p // NS
            for part in range(2):
                sel_r[32 * part + channel, 0, v, p] = 1
                sel_r[64 + 32 * part + channel, 1, v, p] = 1
            sel_y[p, v, channel] = 1
    for n in range(2):
        sel_bc[RK + NS * n + i % NS, n, i] = 1
    return {"ident": ident, "flip": ident[::-1].copy(), "sel_r": sel_r, "sel_y": sel_y, "sel_bc": sel_bc}


def _layout(x):
    def blocks(v):
        return v.reshape(-1, P).T

    cols = np.zeros((P, COLS["end"]), np.float32)

    def put(name, v):
        cols[:, COLS[name]:COLS[name] + v.shape[1]] = v

    m, t = "L0_attn_", "L0_xattn_"
    for name, key in [("norm_g", m + "norm_g"), ("norm_b", m + "norm_b"), ("ffn_g", m + "ffn_g"), ("ffn_b", m + "ffn_b"),
                      ("b1", m + "b1"), ("bq", t + "bq"), ("bk", t + "bk")]:
        put(name, blocks(x[key]))
    for d in "fb":
        p = m + d + "_"
        put(d + "conv_w", x[p + "conv_w"].reshape(KI, P, CW).transpose(1, 0, 2).reshape(P, KI * CW))
        put(d + "conv_b", blocks(x[p + "conv_b"]))
        put(d + "dt_b", blocks(x[p + "dt_proj_b"]))
        put(d + "D", blocks(x[p + "D"]))
        al = x[p + "A_log"].reshape(NM, NQ, NV, CC, NS).transpose(3, 4, 0, 2, 1)
        put(d + "A_log", al.reshape(P, NC))

    def both(key):
        return np.stack([np.ascontiguousarray(x[m + d + "_" + key].T) for d in "fb"])

    arrays = _selectors()
    arrays["x"] = x["x"].reshape(B * TT, P, D)
    arrays["ctxT"] = x["ctx_1024"].reshape(B * T, D).T
    arrays["mask"] = x["mask_1x1xSxS2_ik0"].reshape(T, T)
    arrays["maskT"] = arrays["mask"].T
    arrays["cols"] = cols
    arrays["rows"] = np.stack([x[m + "b2"], x[t + "bv"], x[t + "bo"]])
    arrays["w_in"] = both("in_proj_w")
    arrays["w_xp"] = both("x_proj_w")
    arrays["w_dt"] = both("dt_proj_w")
    arrays["w_out"] = both("out_proj_w")
    arrays["w_att"] = np.stack([x[t + w].T for w in ("wq", "wk", "wv", "wo")])
    arrays["w1"] = x[m + "w1"].T
    arrays["w2"] = x[m + "w2"].T
    arrays["w_fc"] = x["L0_ffn_W_fc"].T
    arrays["w_proj"] = x["L0_ffn_W_proj"].T
    return {k: np.ascontiguousarray(v) for k, v in arrays.items()}


def kernel(**inputs):
    import concourse.bacc as bacc
    from concourse.bass_utils import run_bass_kernel_spmd

    arrays = _layout({k: np.asarray(v) for k, v in inputs.items()})
    nc = bacc.Bacc("TRN2", target_bir_lowering=False, num_devices=1)
    aps = {k: nc.dram_tensor(k, v.shape, mybir.dt.from_np(v.dtype), kind="ExternalInput").ap() for k, v in arrays.items()}
    out = nc.dram_tensor("out", (B * TT, P, D), mybir.dt.float32, kind="ExternalOutput").ap()
    build(nc, aps, out)
    r = run_bass_kernel_spmd(nc, [arrays], core_ids=[0])
    return r.results[0]["out"].reshape(B, T, D)
```

```python
import concourse.bass as bass
import concourse.mybir as mybir
import numpy as np
from contextlib import ExitStack

B, T, D = 8, 512, 256
DI, NS, RK, CW = 512, 16, 16, 4
FF = 1024
H, DH = 16, 16
P = 128
KD, KI, KF, TT = D // P, DI // P, FF // P, T // P
CC = P // NS
NM = KI
NV = 4
NQ = 4
NG, NC = NM * NV, NM * NV * NQ
QR = 6 * DH + 3
EPS = 1e-5
MASKED = -float(2 ** 32)
STEPS, BETA, THRESHOLD = 5, 0.9, 1.0

COLS = {}
def _cols():
    at = 0
    for name, n in [("norm_g", KD), ("norm_b", KD), ("ffn_g", KD), ("ffn_b", KD), ("b1", KF), ("bq", KD), ("bk", KD)]:
        COLS[name] = at
        at += n
    for d in "fb":
        for name, n in [("conv_w", KI * CW), ("conv_b", KI), ("dt_b", KI), ("D", KI), ("A_log", NC)]:
            COLS[d + name] = at
            at += n
    COLS["end"] = at
_cols()

Q_PART = [0, 0, 1, 0, 2, 1]
K_PART = [0, 1, 0, 2, 0, 1]


class Stage:

    def __init__(self, sem, step=1, ahead=0):
        self.sem, self.step, self.ahead = sem, step, ahead

    def credit(self, eng, less=0):
        if self.ahead > less:
            eng.sem_inc(self.sem, self.ahead - less)

    def done(self, instruction):
        instruction.then_inc(self.sem, 1)

    def wait(self, eng, index):
        value = (index + 1) * self.step + self.ahead
        if not isinstance(value, int) or value > 0:
            eng.wait_ge(self.sem, value)


class Slots:

    def __init__(self, banks, full, free, keys):
        self.banks, self.full, self.free = banks, full, free
        self.where, self.uses = {}, [0] * len(banks)
        for n, key in enumerate(keys):
            k = n % len(banks)
            self.where[key] = (k, self.uses[k])
            self.uses[k] += 1

    def _at(self, key, b):
        k, n = self.where[key]
        return k, b * self.uses[k] + n

    def bank(self, key):
        return self.banks[self.where[key][0]]

    def claim(self, pe, key, b):
        k, n = self._at(key, b)
        self.free[k].wait(pe, n - 1)
        return self.banks[k]

    def written(self, key, instruction):
        self.full[self.where[key][0]].done(instruction)

    def wait_full(self, eng, key, b):
        k, n = self._at(key, b)
        self.full[k].wait(eng, n)
        return self.banks[k]

    def read(self, key, instruction):
        self.free[self.where[key][0]].done(instruction)

    def wait_read(self, eng, key, b):
        k, n = self._at(key, b)
        self.free[k].wait(eng, n)

def attention_keys():
    keys = [("hT", k) for k in range(KD)] + [("w1", m) for m in range(KF)] + [("w2", j) for j in range(TT // 2)]
    keys += [("k", m) for m in range(KD)] + [("v", j) for j in range(TT // 2)]
    keys += [("qn", k) for k in range(KD)] + [("q", m) for m in range(KD)] + [("mt",)]
    for g in range(H // 4):
        keys += [("av", g), ("ot", g)]
    keys += [("on", k) for k in range(KD)] + [("wo", j) for j in range(TT // 2)]
    keys += [("fn", k) for k in range(KD)] + [("fc", m) for m in range(KF)] + [("pr", j) for j in range(TT // 2)]
    return keys


IN_AT = [((0, 1), (3, 4)), ((5, 7), (8, 9)), ((23, 24), (25, 27)), ((29, 31), (32, 33))]
XD_AT = (37, 39, 40, 41)
DT_AT = (12, 28, 44, 60)
REP_AT = (45, 47)
OP_AT = [(11, 13, 15, 16), (17, 19, 20, 21)]
FL_AT = (35, 36)
NF_AT = (52, 53)
NR_AT = [(55, 56), (57, 59)]
SUM_AT, READ_AT = 2, 8
LN_AT = ((28, 30, 33, 41), (44, 45, 46, 50))
LN_GROUP = (7, 10)
ACC_AT = 40


def mamba_keys():
    before = [("nf", k) for k in range(KD)] + [("nr", k) for k in range(KD)]
    for k in range(KI):
        before += [("xi", k), ("z", k)]
    before += [("xd", 0), ("dt", 0), ("rep", 0), ("rep", 1), ("dt", 1)]
    loop = []
    for d in range(2):
        at = [(IN_AT[k][n][0], (kind, KI * d + k)) for k in range(KI) for n, kind in enumerate(("xi", "z"))]
        at += [(XD_AT[0], ("xd", d))] + [(p, ("dt", NM * d + i)) for i, p in enumerate(DT_AT)]
        at += [(p, ("rep", 2 * d + i)) for i, p in enumerate(REP_AT)]
        at += [(OP_AT[j][0], (("opb", "opf")[d], j)) for j in range(TT // 2)]
        if d == 0:
            at += [(p, ("fl", j)) for j, p in enumerate(FL_AT)]
            at += [(p, ("nf", k)) for k, p in enumerate(NF_AT)] + [(p[0], ("nr", k)) for k, p in enumerate(NR_AT)]
        loop += [key for _, key in sorted(at)]
    after = [("opb", j) for j in range(TT // 2)] + [("fl", j) for j in range(TT // 2)]
    return before, loop, after


BEFORE, AFTER = "before", "after"


class Ring:

    def __init__(self, banks, kinds, before, loop, after):
        self.banks, self.kinds, self.where = banks, kinds, {}
        users = {}
        for n, key in enumerate(before):
            k = n % len(banks)
            self.where[BEFORE, key] = (k, (BEFORE, users.get(k)))
            users[k] = key
        final = {}
        for n, key in enumerate(loop):
            final[n % len(banks)] = key
        users = {}
        for n, key in enumerate(loop):
            k = n % len(banks)
            self.where["loop", key] = (k, ("this", users[k]) if k in users else ("last", final[k]))
            users[k] = key
        users = {}
        for n, key in enumerate(after):
            k = n % len(banks)
            self.where[AFTER, key] = (k, ("this", users[k]) if k in users else ("last", final[k]))
            users[k] = key

    def index(self, key, b):
        kind, i = key
        full, done, per, first = self.kinds[kind]
        if isinstance(b, str) and b == BEFORE:
            return i
        return per * (B if isinstance(b, str) else b) + first + i

    def _at(self, key, b):
        return self.where[b if isinstance(b, str) else "loop", key]

    def bank(self, key, b):
        return self.banks[self._at(key, b)[0]]

    def claim(self, pe, key, b):
        k, (when, prev) = self._at(key, b)
        if prev is not None:
            per = self.kinds[prev[0]][2]
            self.kinds[prev[0]][1].wait(pe, self.index(prev, b) - (per if when == "last" else 0))
        return self.banks[k]

    def written(self, key, instruction):
        self.kinds[key[0]][0].done(instruction)

    def wait_full(self, eng, key, b):
        self.kinds[key[0]][0].wait(eng, self.index(key, b))
        return self.bank(key, b)

    def read(self, key, instruction):
        self.kinds[key[0]][1].done(instruction)

    def wait_read(self, eng, key, b):
        self.kinds[key[0]][1].wait(eng, self.index(key, b))


def mamba_pass(nc, ctx, a, mid, sb, where, stage, psum, consts, handover):
    f32, f32r = mybir.dt.float32, mybir.dt.float32r
    ALU, ACT = mybir.AluOpType, mybir.ActivationFunctionType
    ident, flip, cols, minus_half, col, settle, s_const = consts
    pair, bank, y_bank, general = psum

    sel_r = sb("sel_r", [P, 2, NV, P], f32r)
    sel_y = sb("sel_y", [P, NV, 32])
    sel_bc = sb("sel_bc", [RK + 2 * NS, 2, P])
    w_xp = sb("w_xp", [P, 2, KI, RK + 2 * NS])
    w_dt = sb("w_dt", [RK, 2, DI])
    w_out = sb("w_out", [P, 2, KI, D])
    w_in = sb("w_in", [P, 2, KD, 2 * DI])
    x_in = sb("x_in", [P, TT, D])
    x0 = sb("x0", [P, TT, D])
    acc = sb("acc", [P, TT, D])
    xn = sb("xn", [P, TT, D])
    r_bwd = sb("r_bwd", [P, TT, D])
    x_out = sb("x_out", [P, TT, D])
    xnT = sb("xnT", [P, 2, KD, T])
    stats = sb("stats", [P, TT, 6])
    mv = sb("mv", [P, TT, 2])
    rstd = sb("rstd", [P, TT])
    u = sb("u", [P, 2, KI, T])
    zs = sb("zs", [P, 2, KI, T])
    B_rep = sb("B_rep", [P, 2, T])
    C_rep = sb("C_rep", [P, 2, T])
    yT = sb("yT", [P, KI, T])
    yt = sb("yt", [P, T])
    xd_sb = sb("xd_sb", [RK + 2 * NS, T])
    xi = sb("xi", [P, T + CW - 1])
    cv = sb("cv", [P, 2, T])
    th_c = sb("th_c", [P, T])
    th_z = sb("th_z", [P, T])
    ab = sb("ab", [P, T])
    delta = sb("delta", [P, T])
    du = sb("du", [P, T])
    cut = [sb(f"cut{s}", [P, T], f32r) for s in range(4)]
    parts = sb("parts", [P, 2, NQ, T], f32r)
    h = sb("h", [P, 2, NQ, T])
    hC = sb("hC", [P, 2, NQ, T])
    dA = sb("dA", [P, NQ, T])
    dBu = sb("dBu", [P, 2, T])
    sel_raw = sb("sel_raw", [P, 2, NV, P], f32, where["h"])

    def kind(name, per, first=0):
        return stage(name + "_full"), stage(name + "_done", ahead=per), per, first

    kinds = {"nf": kind("nf", KD, KD), "nr": kind("nr", KD, KD), "xi": kind("xi", 2 * KI, KI),
             "z": kind("z", 2 * KI, KI), "xd": kind("xd", 2, 1), "dt": kind("dt", 2 * NM, 2),
             "rep": kind("rep", 4, 2), "opf": kind("opf", TT // 2), "opb": kind("opb", TT // 2),
             "fl": kind("fl", TT // 2)}
    readers = {"z": "dve", "opf": "dve", "fl": "dve"}
    G = Ring(general, kinds, *mamba_keys())
    s_w = stage("mamba_weights_dma", 16 * 11)
    s_x = stage("x_dma", 16)
    s_parts = stage("parts_dma", 16 * 16)
    s_mid = stage("mid_dma", 16, ahead=16)
    setup = stage("setup_dve")
    a_log = stage("a_log")
    ln_stats = stage("ln_stats")
    ln_rstd = stage("ln_rstd")
    ln_out = stage("ln_out")
    acc_set = stage("acc_set")
    tap = stage("conv_tap")
    th_conv = stage("th_conv")
    th_gate = stage("th_gate")
    u_done = stage("u_done")
    soft_exp = stage("soft_exp")
    soft = stage("soft")
    d_ready = stage("d_ready")
    hi_ready = stage("hi_ready")
    lo_ready = stage("lo_ready", ahead=2)
    s_rd = stage("spread_delta")
    s_ru = stage("spread_du", ahead=1)
    s_dA = stage("dA", ahead=2)
    s_dBu = stage("dBu", ahead=2)
    s_scan = stage("scan", ahead=4)
    s_hC = stage("hC", ahead=2)
    s_y = stage("y_sum", ahead=4)
    s_yread = stage("y_read", ahead=2 * NM)
    s_yT = stage("yT", ahead=2 * NM)

    def credits(eng, name):
        for k, (_, done, _, _) in kinds.items():
            if readers.get(k, "act") == name:
                done.credit(eng)

    def targets(U, d):
        return [(p, U * NM + 1 + i, (d + (1 + i) // NM) % 2, (1 + i) % NM)
                for i, p in enumerate((DT_AT[-1] - NC,) + DT_AT)]

    class Plan:

        def __init__(self):
            self.steps = {}

        def at(self, p, fn):
            if 0 <= p < NC:
                self.steps.setdefault(p, []).append(fn)

        def run(self, p):
            for fn in self.steps.get(p, []):
                fn()

    with nc.Block() as block:
        @block.sync
        def _(sp):
            s_mid.credit(sp)

            def dma(st, o, i):
                sp.dma_start(o, i).then_inc(st.sem, 16)

            def load_x(b):
                dma(s_x, x_in[:, :, :], a["x"][bass.ds(b * TT, TT)].rearrange("j p f -> p j f"))

            def stack(tb, m):
                if not isinstance(tb, int):
                    s_ru.wait(sp, (tb - 2) * NV * NQ + NV * NQ - 1)
                for s in range(4):
                    (lo_ready if s % 2 else hi_ready).wait(sp, 2 * tb + s // 2)
                    for q in range(NQ):
                        dma(s_parts, parts[32 * s:32 * s + 32, m % 2, q, :].bitcast(f32),
                            cut[s][32 * q:32 * q + 32, :].bitcast(f32))

            def store(b, slot):
                G.wait_read(sp, ("fl", TT // 2 - 1), b)
                dma(s_mid, mid[bass.ds(slot * TT, TT)].rearrange("j p f -> p j f"), x_out[:, :, :])

            load_x(0)
            dma(s_const, ident[:, :], a["ident"])
            dma(s_const, flip[:, :], a["flip"])
            dma(s_const, cols[:, :], a["cols"])
            for d in range(2):
                dma(s_w, w_in[:, d], a["w_in"][d].rearrange("(k p) e -> p k e", p=P))
            dma(s_w, sel_raw[:, :, :, :], a["sel_r"])
            dma(s_w, sel_y[:, :, :], a["sel_y"])
            dma(s_w, sel_bc[:, :, :], a["sel_bc"])
            for d in range(2):
                dma(s_w, w_xp[:, d], a["w_xp"][d].rearrange("(k p) e -> p k e", p=P))
                dma(s_w, w_out[:, d], a["w_out"][d].rearrange("(k p) e -> p k e", p=P))
                dma(s_w, w_dt[:, d], a["w_dt"][d])
            ln_out.wait(sp, 0)
            load_x(1)
            stack(0, 0)
            with sp.Fori(0, B) as b:
                for d in range(2):
                    U = 2 * b + d
                    stack(U * NM + 1, 1)
                    stack(U * NM + 2, 2)
                    if d == 0:
                        store(b, b)
                    stack(U * NM + 3, 3)
                    if d == 0:
                        ln_out.wait(sp, 2 * b + 2)
                        settle(sp)
                        load_x((b + 2) % B)
                    stack(U * NM + 4, 0)
                settle(sp)
            s_mid.wait(sp, B - 1)
            store(AFTER, B)
            s_mid.wait(sp, B)
            s_x.wait(sp, B + 1)
            s_parts.wait(sp, 2 * B * NM)
            sp.sem_inc(handover.sem, 1)

        @block.tensor
        def _(pe):
            s_ru.credit(pe)
            s_y.credit(pe, less=2)

            def mm(o, lhsT, rhs, start=True, stop=True):
                return pe.matmul(o, lhsT, rhs, start=start, stop=stop)

            def step(key, b, n, steps, products):
                bk = G.claim(pe, key, b) if n == 0 else G.bank(key, b)
                last = products(bk)
                if n == steps - 1:
                    G.written(key, last)

            def in_proj(kind, slot, beta, n, k, kk, b):
                if k == 0 and kk == 0 and kind == "xi":
                    kinds["nr" if n else "nf"][1].wait(pe, KD * beta + KD - 1)
                e = (DI if kind == "z" else 0) + k * P
                step((kind, KI * slot + k), b, kk, KD,
                     lambda bk: mm(bk[:, :], w_in[:, n, kk, e:e + P], xnT[:, n, kk, :], kk == 0, kk == KD - 1))

            def x_proj(slot, N, n, kk, b):
                u_done.wait(pe, N * KI + kk)
                step(("xd", slot), b, kk, KI,
                     lambda bk: mm(bk[0:RK + 2 * NS, :], w_xp[:, n, kk, :], u[:, n, kk, :], kk == 0, kk == KI - 1))

            def dt_proj(i, N, n, m, b):
                if m == 0:
                    kinds["xd"][1].wait(pe, N)
                step(("dt", i), b, 0, 1, lambda bk: mm(bk[:, :], w_dt[:, n, m * P:(m + 1) * P], xd_sb[0:RK, :]))

            def rep(slot, n, b):
                step(("rep", 2 * slot + n), b, 0, 1, lambda bk: mm(bk[:, :], sel_bc[:, n, :], xd_sb[:, :]))

            def out_proj(kind, U, d, jj, part, b):
                half, first = part // 2, 2 * (part % 2)
                if jj == 0 and part == 0:
                    s_yT.wait(pe, U * NM + NM - 1)

                def products(bk):
                    j = 2 * jj + half
                    for k in (first, first + 1):
                        last = mm(bk[:, half * D:(half + 1) * D], yT[:, k, j * P:(j + 1) * P], w_out[:, d, k, :],
                                  k == 0, k == KI - 1)
                    return last
                step((kind, jj), b, part, 4, products)

            def flip_back(jj, b):
                G.wait_read(pe, ("opb", TT // 2 - 1), b)

                def products(bk):
                    for half in range(2):
                        j = TT - 1 - (2 * jj + half)
                        last = mm(bk[:, half * D:(half + 1) * D], flip[:, :], r_bwd[:, j, :])
                    return last
                step(("fl", jj), b, 0, 1, products)

            def to_features(k, beta, b):
                ln_out.wait(pe, 2 * beta + 1)

                def products(bk):
                    for j in range(TT):
                        last = pe.transpose(bk[:, j * P:(j + 1) * P], xn[:, j, k * P:(k + 1) * P], ident[:, :])
                    return last
                step(("nf", k), b, 0, 1, products)

            def to_features_reversed(k, part, b):
                def products(bk):
                    for j in (2 * part, 2 * part + 1):
                        r = TT - 1 - j
                        last = mm(bk[:, r * P:(r + 1) * P], xn[:, j, k * P:(k + 1) * P], flip[:, :])
                    return last
                step(("nr", k), b, part, 2, products)

            def spread(c, m, v, q, U):
                if v == 0 and q == 0:
                    s_parts.wait(pe, U * NM + m)
                s_dA.wait(pe, c - 2)
                s_rd.done(mm(bank[q % 2], sel_r[:, 0, v, :], parts[:, m % 2, q, :]))
                s_dBu.wait(pe, c - 2)
                s_ru.done(mm(bank[2 + q % 2], sel_r[:, 1, v, :], parts[:, m % 2, q, :]))

            def sum_states(U, g):
                v = g % NV
                s_hC.wait(pe, U * NG + g)
                if v == 0:
                    s_yread.wait(pe, U * NM + g // NV - 1)
                for q in range(NQ):
                    last = mm(y_bank[32 * q:32 * q + 32, :], sel_y[:, v, :], hC[:, v % 2, q, :], v == 0, v == NV - 1)
                s_y.done(last)

            s_const.wait(pe, 0)
            s_w.wait(pe, 0)
            setup.wait(pe, 0)
            for v in range(2):
                for q in range(NQ):
                    mm(y_bank[32 * q:32 * q + 32, :], sel_y[:, v, :], hC[:, v % 2, q, :], v == 0, False)
            for k in range(KD):
                to_features(k, 0, BEFORE)
            for k in range(KD):
                for part in range(2):
                    to_features_reversed(k, part, BEFORE)
            for k in range(KI):
                for kind in ("xi", "z"):
                    for kk in range(KD):
                        in_proj(kind, 0, 0, 0, k, kk, BEFORE)
            for kk in range(KI):
                x_proj(0, 0, 0, kk, BEFORE)
            dt_proj(0, 0, 0, 0, BEFORE)
            for n in range(2):
                rep(0, n, BEFORE)
            dt_proj(1, 0, 0, 1, BEFORE)
            for key in mamba_keys()[0][-3:]:
                G.wait_read(pe, key, BEFORE)

            with pe.Fori(0, B) as b:
                for d in range(2):
                    U, N, n, beta = 2 * b + d, 2 * b + d + 1, 1 - d, b + d
                    plan = Plan()
                    for k in range(KI):
                        for kind, at in zip(("xi", "z"), IN_AT[k]):
                            for kk in range(KD):
                                plan.at(at[kk], lambda kind=kind, k=k, kk=kk: in_proj(kind, d, beta, n, k, kk, b))
                    for kk, p in enumerate(XD_AT):
                        plan.at(p, lambda kk=kk: x_proj(d, N, n, kk, b))
                    for i, p in enumerate(DT_AT):
                        ahead = (i + 2) // NM
                        plan.at(p, lambda i=i, ahead=ahead: dt_proj(NM * d + i, N, (d + ahead) % 2, (i + 2) % NM, b))
                    for i, p in enumerate(REP_AT):
                        plan.at(p, lambda i=i: rep(d, i, b))
                    for jj in range(TT // 2):
                        for part, p in enumerate(OP_AT[jj]):
                            plan.at(p, lambda jj=jj, part=part: out_proj(("opb", "opf")[d], U - 1, 1 - d, jj, part, b))
                    if d == 0:
                        for jj, p in enumerate(FL_AT):
                            plan.at(p, lambda jj=jj: flip_back(jj, b))
                        for k, p in enumerate(NF_AT):
                            plan.at(p, lambda k=k: to_features(k, b + 1, b))
                        for k in range(KD):
                            for part, p in enumerate(NR_AT[k]):
                                plan.at(p, lambda k=k, part=part: to_features_reversed(k, part, b))
                    for g in range(NC):
                        m, v, q = g // (NV * NQ), g // NQ % NV, g % NQ
                        spread(U * NC + g, m, v, q, U)
                        if q == SUM_AT:
                            sum_states(U, g // NQ - 2)
                        plan.run(g)
            for i in range(2):
                sum_states(2 * B, i - 2)
            for jj in range(TT // 2):
                for part in range(4):
                    out_proj("opb", 2 * B - 1, 1, jj, part, AFTER)
            for jj in range(TT // 2):
                flip_back(jj, AFTER)
            settle(pe)
            pe.sem_inc(handover.sem, 1)

        @block.scalar
        def _(act):
            s_dA.credit(act)
            credits(act, "act")

            def f(o, i, fn=ACT.Copy, **kw):
                return act.activation(o, i, fn, **kw)

            def evacuate(key, o, b, fn=ACT.Copy, view=None, **kw):
                bk = G.wait_full(act, key, b)
                G.read(key, f(o, bk[:, :] if view is None else view(bk), fn, **kw))

            def normed(kind, n, k, b):
                evacuate((kind, k), xnT[:, n, k, :], b, ACT.Identity, scale=col("norm_g", k), bias=col("norm_b", k))

            def conv_in(slot, N, n, k, b):
                tap.wait(act, (CW - 1) * (N * KI + k) - 1)
                u_done.wait(act, N * KI + k - 2)
                key = ("xi", KI * slot + k)
                bk = G.wait_full(act, key, b)
                f(xi[:, CW - 1:], bk[:, :])
                G.read(key, f(cv[:, k % 2, :], bk[:, :], ACT.Identity, scale=col("fb"[n] + "conv_w", CW * k + CW - 1),
                              bias=col("fb"[n] + "conv_b", k)))

            def gate_tanh(slot, N, k, b):
                kinds["z"][1].wait(act, N * KI + k - 1)
                bk = G.wait_full(act, ("z", KI * slot + k), b)
                th_gate.done(f(th_z[:, :], bk[:, :], ACT.Tanh, scale=0.5))

            def conv_tanh(N, k):
                tap.wait(act, (CW - 1) * (N * KI + k) + CW - 2)
                th_conv.done(f(th_c[:, :], cv[:, k % 2, :], ACT.Tanh))

            def soft_in(i, tb, n, m, b):
                lo_ready.wait(act, 2 * tb - 2)
                bk = G.wait_full(act, ("dt", i), b)
                bias = col("fb"[n] + "dt_b", m)
                f(ab[:, :], bk[:, :], ACT.Abs, bias=bias)
                G.read(("dt", i), f(delta[:, :], bk[:, :], ACT.Relu, bias=bias))

            def soft_1(tb):
                kinds["dt"][1].wait(act, tb)
                soft_exp.done(f(ab[:, :], ab[:, :], ACT.Exp, scale=-1.0))

            def soft_2(tb):
                soft_exp.wait(act, tb)
                soft.done(f(ab[:, :], ab[:, :], ACT.Ln, bias=1.0))

            def high(tb, which):
                if which == 0:
                    s_parts.wait(act, tb - 1)
                d_ready.wait(act, 2 * tb + which)
                hi_ready.done(f(cut[2 * which][:, :], (du if which else delta)[:, :]))

            def copy_acc(b):
                G.wait_read(act, ("fl", TT // 2 - 1), b)
                ln_out.wait(act, 2 * b)
                acc_set.done(f(acc[:, :, :], x0[:, :, :]))

            s_const.wait(act, 0)
            for d in "fb":
                last = f(col(d + "A_log", 0, NC), col(d + "A_log", 0, NC), ACT.Exp)
            a_log.done(last)
            setup.wait(act, 0)
            for n, kind in enumerate(("nf", "nr")):
                for k in range(KD):
                    normed(kind, n, k, BEFORE)
            for k in range(KI):
                conv_in(0, 0, 0, k, BEFORE)
                gate_tanh(0, 0, k, BEFORE)
                conv_tanh(0, k)
            evacuate(("xd", 0), xd_sb[:, :], BEFORE, view=lambda bk: bk[0:RK + 2 * NS, :])
            soft_in(0, 0, 0, 0, BEFORE)
            soft_1(0)
            soft_2(0)
            evacuate(("rep", 0), B_rep[:, 0, :], BEFORE)
            evacuate(("rep", 1), C_rep[:, 0, :], BEFORE)
            high(0, 0)
            high(0, 1)
            soft_in(1, 1, 0, 1, BEFORE)
            soft_1(1)
            soft_2(1)

            with act.Fori(0, B) as b:
                for d in range(2):
                    U, N, n = 2 * b + d, 2 * b + d + 1, 1 - d
                    plan = Plan()
                    for k in range(KI):
                        (_, x_end), (_, z_end) = IN_AT[k]
                        plan.at(x_end + 1, lambda k=k: conv_in(d, N, n, k, b))
                        plan.at(z_end + 1, lambda k=k: gate_tanh(d, N, k, b))
                        plan.at(x_end + 6, lambda k=k: conv_tanh(N, k))
                    plan.at(XD_AT[-1] + 1, lambda: evacuate(("xd", d), xd_sb[:, :], b, view=lambda bk: bk[0:RK + 2 * NS, :]))
                    for i, rows in enumerate((B_rep, C_rep)):
                        plan.at(REP_AT[i] + 1, lambda i=i, rows=rows: evacuate(("rep", 2 * d + i), rows[:, n, :], b))
                    for i, (p, tb, nt, m) in enumerate(targets(U, d)):
                        plan.at(p + 1, lambda i=i, tb=tb, nt=nt, m=m: soft_in(NM * d + i - 1, tb, nt, m, b))
                        plan.at(p + 2, lambda tb=tb: soft_1(tb))
                        plan.at(p + 3, lambda tb=tb: soft_2(tb))
                        plan.at(p + 6, lambda tb=tb: high(tb, 0))
                        plan.at(p + 8, lambda tb=tb: high(tb, 1))
                    if d == 0:
                        for jj in range(TT // 2):
                            plan.at(OP_AT[jj][-1] + 1, lambda jj=jj: evacuate(
                                ("opb", jj), r_bwd[:, 2 * jj:2 * jj + 2, :], b,
                                view=lambda bk: bk[:, :].rearrange("p (j f) -> p j f", j=2)))
                        plan.at(ACC_AT, lambda: copy_acc(b))
                        for k, p in enumerate(NF_AT):
                            plan.at(p + 1, lambda k=k: normed("nf", 0, k, b))
                        for k, p in enumerate(NR_AT):
                            plan.at(p[-1] + 1, lambda k=k: normed("nr", 1, k, b))
                    for g in range(NC):
                        m, v, q = g // (NV * NQ), g // NQ % NV, g % NQ
                        c = U * NC + g
                        s_rd.wait(act, c)
                        s_scan.wait(act, c - 4)
                        s_dA.done(f(dA[:, q, :], bank[q % 2], ACT.Exp, scale=col("fb"[d] + "A_log", g)))
                        plan.run(g)
            for jj in range(TT // 2):
                evacuate(("opb", jj), r_bwd[:, 2 * jj:2 * jj + 2, :], AFTER,
                         view=lambda bk: bk[:, :].rearrange("p (j f) -> p j f", j=2))
            act.sem_inc(handover.sem, 1)

        @block.vector
        def _(dve):
            s_dBu.credit(dve)
            s_scan.credit(dve)
            lo_ready.credit(dve)
            s_yread.credit(dve, less=1)
            s_yT.credit(dve, less=1)
            credits(dve, "dve")

            def norm_stats(src, half):
                for j in (2 * half, 2 * half + 1):
                    dve.bn_stats(stats[:, j, :], src[:, j, :])

            def norm_mean():
                dve.drain()
                for j in range(TT):
                    last = dve.bn_aggr(mv[:, j, :], stats[:, j, :])
                ln_stats.done(last)

            def norm_apply(n, beta, src, dst):
                ln_rstd.wait(dve, 2 * beta + n)
                for j in range(TT):
                    last = dve.tensor_scalar(dst[:, j, :], src[:, j, :], mv[:, j, 0:1], rstd[:, j:j + 1],
                                             ALU.subtract, ALU.mult)
                ln_out.done(last)

            def norm_steps(beta, b):
                def load():
                    s_x.wait(dve, beta)
                    norm_stats(x_in, 0)

                def apply_0():
                    if not isinstance(beta, int):
                        acc_set.wait(dve, b)
                    norm_apply(0, beta, x_in, x0)

                def stats_1():
                    ln_out.wait(dve, 2 * beta)
                    norm_stats(x0, 0)

                def apply_1():
                    if not isinstance(beta, int):
                        kinds["nr"][0].wait(dve, KD * beta - 1)
                    norm_apply(1, beta, x0, xn)
                return ((load, lambda: norm_stats(x_in, 1), norm_mean, apply_0),
                        (stats_1, lambda: norm_stats(x0, 1), norm_mean, apply_1))

            def conv_tap(N, n, k, t):
                i = (CW - 1) * (N * KI + k) + t
                if t == 0:
                    kinds["xi"][1].wait(dve, N * KI + k)
                else:
                    tap.wait(dve, i - 1)
                tap.done(dve.scalar_tensor_tensor(cv[:, k % 2, :], xi[:, t:t + T], col("fb"[n] + "conv_w", CW * k + t),
                                                  cv[:, k % 2, :], ALU.mult, ALU.add))

            def gate(slot, N, n, k, b):
                th_gate.wait(dve, N * KI + k)
                s_yT.wait(dve, (N - 2) * NM + k)
                key = ("z", KI * slot + k)
                G.read(key, dve.scalar_tensor_tensor(zs[:, n, k, :], th_z[:, :], 1.0, G.bank(key, b)[:, :], ALU.add, ALU.mult))

            def make_u(N, n, k):
                th_conv.wait(dve, N * KI + k)
                s_yread.wait(dve, (N - 2) * NM + k)
                u_done.done(dve.scalar_tensor_tensor(u[:, n, k, :], th_c[:, :], 1.0, cv[:, k % 2, :], ALU.add, ALU.mult))

            def make_delta(tb):
                soft.wait(dve, tb)
                d_ready.done(dve.tensor_tensor(delta[:, :], delta[:, :], ab[:, :], ALU.add))

            def make_du(tb, n, m):
                hi_ready.wait(dve, 2 * tb - 1)
                d_ready.wait(dve, 2 * tb)
                d_ready.done(dve.tensor_tensor(du[:, :], delta[:, :], u[:, n, m, :], ALU.mult))

            def low(tb, which):
                hi_ready.wait(dve, 2 * tb + which)
                if which:
                    d_ready.wait(dve, 2 * tb + 1)
                lo_ready.done(dve.tensor_tensor(cut[2 * which + 1][:, :], (du if which else delta)[:, :],
                                                cut[2 * which][:, :].bitcast(f32), ALU.subtract))

            def read_y(tb, n, m):
                s_y.wait(dve, NV * tb + NV - 1)
                s_yT.wait(dve, tb - 1)
                s_yread.done(dve.scalar_tensor_tensor(yt[:, :], u[:, n, m, :], col("fb"[n] + "D", m), y_bank[:, :],
                                                      ALU.mult, ALU.add))

            def gate_y(tb, n, m):
                s_yread.wait(dve, tb)
                s_yT.done(dve.tensor_tensor(yT[:, m, :], yt[:, :], zs[:, n, m, :], ALU.mult))

            def tiles(ap, jj):
                return ap[:, 2 * jj:2 * jj + 2, :]

            def add_forward(jj, b):
                acc_set.wait(dve, b)
                bk = G.wait_full(dve, ("opf", jj), b)
                G.read(("opf", jj), dve.tensor_tensor(tiles(acc, jj), tiles(acc, jj),
                                                      bk[:, :].rearrange("p (j f) -> p j f", j=2), ALU.add))

            def add_backward(jj, b):
                bb = B if isinstance(b, str) else b
                s_mid.wait(dve, bb - 1)
                kinds["opf"][1].wait(dve, (TT // 2) * bb - 1)
                bk = G.wait_full(dve, ("fl", jj), b)
                G.read(("fl", jj), dve.tensor_tensor(tiles(x_out, jj), tiles(acc, jj),
                                                     bk[:, :].rearrange("p (j f) -> p j f", j=2), ALU.add))

            dve.memset(hC[:, :, :, :], 0.0)
            dve.memset(u[:, 1], 0.0)
            dve.memset(zs[:, 1], 0.0)
            dve.memset(yT[:, :, :], 0.0)
            dve.memset(acc[:, :, :], 0.0)
            dve.memset(xi[:, 0:CW - 1], 0.0)
            dve.memset(minus_half[:, :], -0.5)
            s_const.wait(dve, 0)
            s_w.wait(dve, 0)
            dve.tensor_copy(sel_r[:, :, :, :], sel_raw[:, :, :, :])
            for dn in "fb":
                cw = col(dn + "conv_w", 0, KI * CW + KI)
                dve.tensor_scalar(cw, cw, 0.5, None, ALU.mult)
            a_log.wait(dve, 0)
            for dn in "fb":
                al = col(dn + "A_log", 0, NC)
                dve.tensor_scalar(al, al, -1.0, None, ALU.mult)
            setup.done(dve.tensor_scalar(w_out[:, :, :, :], w_out[:, :, :, :], 0.25, None, ALU.mult))
            dve.drain()
            for norm in norm_steps(0, BEFORE):
                for fn in norm:
                    fn()
            for k in range(KI):
                for t in range(CW - 1):
                    conv_tap(0, 0, k, t)
                gate(0, 0, 0, k, BEFORE)
                make_u(0, 0, k)
            make_delta(0)
            make_du(0, 0, 0)
            low(0, 0)
            low(0, 1)

            with dve.Fori(0, B) as b:
                for d in range(2):
                    U, N, n = 2 * b + d, 2 * b + d + 1, 1 - d
                    plan = Plan()
                    for k in range(KI):
                        (_, x_end), (_, z_end) = IN_AT[k]
                        for t in range(CW - 1):
                            plan.at(x_end + 2 + t, lambda k=k, t=t: conv_tap(N, n, k, t))
                        plan.at(z_end + 3, lambda k=k: gate(d, N, n, k, b))
                        plan.at(x_end + 8, lambda k=k: make_u(N, n, k))
                    for p, tb, nt, m in targets(U, d):
                        plan.at(p + 5, lambda tb=tb: make_delta(tb))
                        plan.at(p + 6, lambda tb=tb, nt=nt, m=m: make_du(tb, nt, m))
                        plan.at(p + 8, lambda tb=tb: low(tb, 0))
                        plan.at(p + 10, lambda tb=tb: low(tb, 1))
                    for m in range(NM):
                        tb = U * NM + m - 1
                        nm = (1 - d, NM - 1) if m == 0 else (d, m - 1)
                        plan.at(NV * NQ * m + READ_AT, lambda tb=tb, nm=nm: read_y(tb, *nm))
                        plan.at(NV * NQ * m + READ_AT + 1, lambda tb=tb, nm=nm: gate_y(tb, *nm))
                    if d == 0:
                        for jj, p in enumerate(FL_AT):
                            plan.at(p + 2, lambda jj=jj: add_backward(jj, b))
                        for at, norm in zip(LN_AT, norm_steps(b + 1, b)):
                            for p, fn in zip(at, norm):
                                plan.at(p, fn)
                    else:
                        for jj in range(TT // 2):
                            plan.at(OP_AT[jj][-1] + 2, lambda jj=jj: add_forward(jj, b))
                    for g in range(NC + 1):
                        c = U * NC + g
                        if g < NC:
                            if g == 0:
                                kinds["rep"][1].wait(dve, 2 * U + 1)
                            s_ru.wait(dve, c)
                            s_scan.wait(dve, c - 2)
                            s_dBu.done(dve.tensor_tensor(dBu[:, g % 2, :], bank[2 + g % 2], B_rep[:, d, :], ALU.mult))
                        if g > 0:
                            v, q = (g - 1) // NQ % NV, (g - 1) % NQ
                            if q == 0:
                                s_hC.wait(dve, U * NG + (g - 1) // NQ - 2)
                            s_dA.wait(dve, c - 1)
                            s_dBu.wait(dve, c - 1)
                            s_scan.done(dve.tensor_tensor_scan(h[:, v % 2, q, :], dA[:, q, :], dBu[:, (g - 1) % 2, :],
                                                               0.0, ALU.mult, ALU.add))
                        plan.run(g)
            read_y(2 * B * NM - 1, 1, NM - 1)
            gate_y(2 * B * NM - 1, 1, NM - 1)
            for jj in range(TT // 2):
                add_backward(jj, AFTER)
            dve.sem_inc(handover.sem, 1)

        @block.gpsimd
        def _(pool):
            s_hC.credit(pool)

            def rstd_of(n, beta):
                ln_stats.wait(pool, 2 * beta + n)
                settle(pool)
                pool.tensor_scalar(rstd[:, :], mv[:, :, 1], EPS, None, ALU.add)
                pool.drain()
                ln_rstd.done(pool.tensor_tensor(rstd[:, :], rstd[:, :], minus_half[:, :], ALU.pow))
                pool.drain()

            setup.wait(pool, 0)
            rstd_of(0, 0)
            rstd_of(1, 0)
            with pool.Fori(0, B) as b:
                for d in range(2):
                    U = 2 * b + d
                    kinds["rep"][1].wait(pool, 2 * U + 1)
                    for g in range(NG):
                        s_scan.wait(pool, U * NC + g * NQ + NQ - 1)
                        s_y.wait(pool, U * NG + g - 2)
                        s_hC.done(pool.tensor_tensor(hC[:, g % 2], h[:, g % 2],
                                                     C_rep[:, d, :].unsqueeze(1).broadcast_to((P, NQ, T)), ALU.mult))
                        if d == 0 and g in LN_GROUP:
                            rstd_of(LN_GROUP.index(g), b + 1)
            pool.sem_inc(handover.sem, 1)


def attention_pass(nc, ctx, a, mid, out, sb, where, stage, psum, consts, handover):
    f32, bf16, i32 = mybir.dt.float32, mybir.dt.bfloat16, mybir.dt.int32
    ALU, ACT, AX = mybir.AluOpType, mybir.ActivationFunctionType, mybir.AxisListType
    ident, flip, cols, minus_half, col, settle, s_const = consts
    pair, bank, y_bank, general = psum
    KB = 1024

    ident_bf = sb("ident_bf", [P, P], bf16)
    ones_bf = sb("ones_bf", [P, P], bf16)
    rows = sb("rows", [P, 3, D])
    w_att = sb("w_att", [P, 4, KD, D])
    w_up = sb("w_up", [P, 2, KD, FF])
    w_down = sb("w_down", [P, 2, KF, D])
    x_in = sb("x_in2", [P, TT, D])
    x0 = sb("x_mid", [P, TT, D])
    x1 = sb("x1", [P, TT, D])
    xn = sb("xn2", [P, TT, D])
    xT = sb("xT", [P, KD, T])
    ctxT = sb("ctxT", [P, KD, T])
    mask_bias = sb("mask_bias", [P, TT, T], bf16)
    mask_biasT = sb("mask_biasT", [P, TT, T], bf16)
    not_full = sb("not_full", [P, T])
    stats = sb("stats2", [P, TT, 6])
    mv = sb("mv2", [P, TT, 2])
    rstd = sb("rstd2", [P, TT])
    row_keep = sb("row_keep", [P, TT])
    q_st = sb("q_st", [P, H, T], bf16)
    k_st = sb("k_st", [P, H, T], bf16)
    pr = sb("pr", [P, 4, TT, T])
    v_sb = sb("v_sb", [P, TT, H, 32])
    f0 = where["next"]
    qk = sb("qk", [P, 2, KD, T])
    qk_part = sb("qk_part", [P, 2, 3, KD, T], bf16)
    oT = sb("oT", [P, 2, T])
    m_col = sb("m_col", [P, TT, H])
    m_part = sb("m_part", [H, 3, T], bf16)
    m_rest = sb("m_rest", [H, T])
    rsum = sb("rsum", [P, TT, 4])
    g1 = sb("g1", [P, KF, T], f32, where["pr"])
    g0 = sb("g0", [P, T], f32, where["pr"] + 16 * KB)
    mem = sb("mem", [P, TT, D], f32, f0)
    spk = sb("spk", [P, TT, D], f32, f0 + 4 * KB)
    cnt = sb("cnt", [P, TT, D], f32, f0 + 8 * KB)
    y_sb = sb("y_sb", [P, TT, D], f32, f0 + 12 * KB)
    tmp = sb("tmp", [P, TT, D], f32, where["oT"])
    mask_i = sb("mask_i", [P, TT, T], i32, where["pr"])
    maskT_i = sb("maskT_i", [P, TT, T], i32, where["pr"] + 8 * KB)
    keep = sb("keep", [P, TT, T], f32, where["pr"] + 16 * KB)
    keep_bf = sb("keep_bf", [P, TT, T], bf16, where["pr"] + 24 * KB)
    o_sb = xn

    qk_dram = nc.dram_tensor("qk_parts", (2, 3, D, T), bf16).ap()
    m_dram = nc.dram_tensor("max_parts", (3, H, T), bf16).ap()

    G = Slots(general, [stage(f"full{i}") for i in range(3)], [stage(f"free{i}", ahead=1) for i in range(3)],
              attention_keys())
    s_w = stage("weights2_dma", 16 * 6)
    s_mask = stage("mask_dma", 32)
    s_x = stage("x2_dma", 32)
    s_ctx = stage("ctx_dma", 16)
    s_qkw = stage("qk_write_dma", 48)
    s_qkr = stage("qk_read_dma", 16 * 12)
    s_mw = stage("max_write_dma", 16)
    s_mr = stage("max_read_dma", 16)
    s_out = stage("out_dma", 16, ahead=16)
    setup_dve = stage("setup2_dve")
    setup_pe = stage("setup_pe")
    ln_stats = stage("ln_stats2")
    ln_rstd = stage("ln_rstd2")
    ln_out = stage("ln_out2")
    x_free = stage("x_free", ahead=1)
    s_v = stage("v_const")
    s_part = stage("qk_cut")
    qk_hi = stage("qk_hi")
    qk_lo = stage("qk_lo")
    s_pre = stage("prescore")
    s_max = stage("maximum", ahead=4)
    m_cut = stage("m_cut")
    s_sc = stage("score")
    s_exp = stage("exp", ahead=2)
    o_ready = stage("o_ready")
    g_out = stage("g_out")
    out_ready = stage("out_ready")

    with nc.Block() as block:
        @block.sync
        def _(sp):
            s_out.credit(sp)
            handover.wait(sp, 0)

            def dma(st, o, i):
                sp.dma_start(o, i).then_inc(st.sem, 16)

            def load_x(b):
                dma(s_x, x_in[:, :, :], a["x"][bass.ds(b * TT, TT)].rearrange("j p f -> p j f"))
                dma(s_x, x0[:, :, :], mid[bass.ds((b + 1) * TT, TT)].rearrange("j p f -> p j f"))

            def load_ctx(b):
                dma(s_ctx, ctxT[:, :, :], a["ctxT"][:, bass.ds(b * T, T)].rearrange("(k p) t -> p k t", p=P))

            load_x(0)
            dma(s_mask, mask_i[:, :, :], a["mask"].rearrange("(j p) t -> p j t", p=P))
            dma(s_mask, maskT_i[:, :, :], a["maskT"].rearrange("(j p) t -> p j t", p=P))
            dma(s_w, rows[:, :, :], a["rows"].unsqueeze(0).broadcast_to((P, 3, D)))
            for n, key in enumerate(("w1", "w_fc")):
                dma(s_w, w_up[:, n], a[key].rearrange("(k p) e -> p k e", p=P))
            for n, key in enumerate(("w2", "w_proj")):
                dma(s_w, w_down[:, n], a[key].rearrange("(k p) e -> p k e", p=P))
            dma(s_w, w_att[:, :, :, :].rearrange("p w k e -> p (w k) e"),
                a["w_att"].rearrange("w (k p) e -> p (w k) e", p=P))

            load_ctx(0)
            with sp.Fori(0, B) as b:
                x_free.wait(sp, b)
                settle(sp)
                load_x((b + 1) % B)
                G.wait_full(sp, ("v", TT // 2 - 1), b)
                settle(sp)
                load_ctx((b + 1) % B)
                for n, (dst, which) in enumerate([(k_st, K_PART), (q_st, Q_PART)]):
                    s_part.wait(sp, 2 * b + n)
                    for part in range(3):
                        dma(s_qkw, qk_dram[n, part].rearrange("(k p) t -> p k t", p=P), qk_part[:, n, part])
                    s_qkw.wait(sp, 2 * b + n)
                    for band, part in enumerate(which):
                        dma(s_qkr, dst[DH * band:DH * band + DH, :, :],
                            qk_dram[n, part].rearrange("(h e) t -> e h t", e=DH))
                m_cut.wait(sp, b)
                dma(s_mw, m_dram.rearrange("s h t -> h s t"), m_part[:, :, :])
                s_mw.wait(sp, b)
                dma(s_mr, q_st[6 * DH:QR, :, :], m_dram)
                out_ready.wait(sp, b)
                dma(s_out, out[bass.ds(b * TT, TT)].rearrange("j p f -> p j f"), tmp[:, :, :])
                s_out.wait(sp, b)
                settle(sp)
            s_x.wait(sp, B)
            s_ctx.wait(sp, B)

        @block.tensor
        def _(pe):
            handover.wait(pe, 0)

            def mm(o, lhsT, rhs, start=True, stop=True):
                return pe.matmul(o, lhsT, rhs, start=start, stop=stop)

            def to_features(keys, src, b):
                for k in range(KD):
                    bk = G.claim(pe, (keys, k), b)
                    for j in range(TT):
                        last = pe.transpose(bk[:, j * P:(j + 1) * P], src[:, j, k * P:(k + 1) * P], ident[:, :])
                    G.written((keys, k), last)

            def project(key, w, rhs, kn, b, rows_out=P):
                bk = G.claim(pe, key, b)
                for k in range(kn):
                    last = mm(bk[0:rows_out, :], w(k), rhs(k), k == 0, k == kn - 1)
                G.written(key, last)

            def project_tokens(key, lhsT, w, kn, jj, b):
                bk = G.claim(pe, key, b)
                for half_ in range(2):
                    for k in range(kn):
                        last = mm(bk[:, half_ * D:(half_ + 1) * D], lhsT(k, 2 * jj + half_), w(k), k == 0, k == kn - 1)
                G.written(key, last)

            def tok(src):
                return lambda k, j: src[:, k, j * P:(j + 1) * P]

            setup_dve.wait(pe, 0)
            for k in range(TT):
                last = mm(y_bank[:, :], ones_bf[:, :], keep_bf[:, k, :], k == 0, k == TT - 1)
            setup_pe.done(last)
            s_w.wait(pe, 0)
            setup_dve.wait(pe, 1)

            with pe.Fori(0, B) as b:
                ln_out.wait(pe, 3 * b + 0)
                to_features("hT", xn, b)
                for k in range(KD):
                    G.wait_read(pe, ("hT", k), b)
                for m in range(KF):
                    project(("w1", m), lambda k: w_up[:, 0, k, m * P:(m + 1) * P], lambda k: xT[:, k, :], KD, b)
                for m in range(KF - 3, KF):
                    G.wait_read(pe, ("w1", m), b)
                for jj in range(TT // 2):
                    project_tokens(("w2", jj), tok(g1), lambda k: w_down[:, 0, k, :], KF, jj, b)
                s_ctx.wait(pe, b)
                for m in range(KD):
                    project(("k", m), lambda k: w_att[:, 1, k, m * P:(m + 1) * P], lambda k: ctxT[:, k, :], KD, b)
                for jj in range(TT // 2):
                    project_tokens(("v", jj), tok(ctxT), lambda k: w_att[:, 2, k, :], KD, jj, b)
                ln_out.wait(pe, 3 * b + 1)
                to_features("qn", xn, b)
                for k in range(KD):
                    G.wait_read(pe, ("qn", k), b)
                for m in range(KD):
                    project(("q", m), lambda k: w_att[:, 0, k, m * P:(m + 1) * P], lambda k: xT[:, k, :], KD, b)
                s_qkr.wait(pe, b)
                settle(pe)
                with pe.Fori(0, H) as h_:
                    for j in range(TT):
                        n = (b * H + h_) * TT + j
                        s_max.wait(pe, n - 4)
                        mm(bank[j], q_st[0:6 * DH, bass.ds(h_, 1), j * P:(j + 1) * P].squeeze(1),
                           k_st[0:6 * DH, bass.ds(h_, 1), :].squeeze(1), True, False)
                        s_pre.done(mm(bank[j], ident_bf[:, :], mask_bias[:, j, :], False, True))
                s_max.wait(pe, (b + 1) * H * TT - 1)
                bk = G.claim(pe, ("mt",), b)
                for j in range(TT):
                    last = pe.transpose(bk[0:H, j * P:(j + 1) * P], m_col[:, j, :], ident[:, :])
                G.written(("mt",), last)
                s_mr.wait(pe, b)
                s_v.wait(pe, 0)
                for jj in range(TT // 2):
                    G.wait_read(pe, ("v", jj), b)
                for g in range(H // 4):
                    for hh in range(4):
                        hd = 4 * g + hh
                        for s in range(2):
                            n = (b * H + hd) * 2 + s
                            s_exp.wait(pe, n - 2)
                            for t in range(2):
                                kt = 2 * s + t
                                mm(pair[s][:, t, :], k_st[0:QR, hd, kt * P:(kt + 1) * P], q_st[0:QR, hd, :], True, False)
                                last = mm(pair[s][:, t, :], ident_bf[:, :], mask_biasT[:, kt, :], False, True)
                            s_sc.done(last)
                    s_exp.wait(pe, (b * H + 4 * g + 3) * 2 + 1)
                    bk = G.claim(pe, ("av", g), b)
                    for kt in range(TT):
                        for hh in range(4):
                            last = mm(bk[32 * hh:32 * hh + 32, :], v_sb[:, kt, 4 * g + hh, :], pr[:, hh, kt, :],
                                      kt == 0, kt == TT - 1)
                    G.written(("av", g), last)
                    G.wait_read(pe, ("av", g), b)
                    bk = G.claim(pe, ("ot", g), b)
                    for j in range(TT):
                        last = pe.transpose(bk[:, j * P:(j + 1) * P], oT[:, g % 2, j * P:(j + 1) * P], ident[:, :])
                    G.written(("ot", g), last)
                o_ready.wait(pe, (H // 4) * (b + 1) - 1)
                to_features("on", o_sb, b)
                for k in range(KD):
                    G.wait_read(pe, ("on", k), b)
                for jj in range(TT // 2):
                    project_tokens(("wo", jj), tok(xT), lambda k: w_att[:, 3, k, :], KD, jj, b)
                ln_out.wait(pe, 3 * b + 2)
                to_features("fn", xn, b)
                for k in range(KD):
                    G.wait_read(pe, ("fn", k), b)
                for m in range(KF):
                    project(("fc", m), lambda k: w_up[:, 1, k, m * P:(m + 1) * P], lambda k: xT[:, k, :], KD, b)
                g_out.wait(pe, KF * (b + 1) - 1)
                for jj in range(TT // 2):
                    project_tokens(("pr", jj), tok(g1), lambda k: w_down[:, 1, k, :], KF, jj, b)

        @block.scalar
        def _(act):
            s_exp.credit(act)
            handover.wait(act, 0)

            def f(o, i, fn=ACT.Copy, **kw):
                return act.activation(o, i, fn, **kw)

            def evacuate(key, o, b, fn=ACT.Copy, view=None, **kw):
                bk = G.wait_full(act, key, b)
                G.read(key, f(o, bk[:, :] if view is None else view(bk), fn, **kw))

            setup_dve.wait(act, 1)
            with act.Fori(0, B) as b:
                for k in range(KD):
                    evacuate(("hT", k), xT[:, k, :], b, ACT.Identity, scale=col("ffn_g", k), bias=col("ffn_b", k))
                for m in range(KF):
                    evacuate(("w1", m), g1[:, m, :], b, ACT.Gelu, bias=col("b1", m))
                for n in range(2):
                    if n == 0:
                        for m in range(KD):
                            evacuate(("k", m), qk[:, 0, m, :], b, ACT.Identity, bias=col("bk", m))
                        act.drain()
                    else:
                        for k in range(KD):
                            evacuate(("qn", k), xT[:, k, :], b)
                        for m in range(KD):
                            G.wait_read(act, ("q", m), b)
                    qk_hi.done(f(qk_part[:, n, 0], qk[:, n]))
                    qk_lo.wait(act, 2 * b + n)
                    qk_hi.done(f(qk_part[:, n, 1], qk[:, n]))
                for g in range(H // 4):
                    for hh in range(4):
                        for s in range(2):
                            s_sc.wait(act, (b * H + 4 * g + hh) * 2 + s)
                            s_exp.done(f(pr[:, hh, 2 * s:2 * s + 2, :], pair[s][:, :, :], ACT.Exp, scale=0.25))
                    evacuate(("av", g), oT[:, g % 2, :], b)
                for k in range(KD):
                    evacuate(("on", k), xT[:, k, :], b)
                for k in range(KD):
                    evacuate(("fn", k), xT[:, k, :], b)
                for m in range(KF):
                    evacuate(("fc", m), g0[:, :], b, ACT.Relu)
                    act.drain()
                    g_out.done(f(g1[:, m, :], g0[:, :], ACT.Square))
                    act.drain()

        @block.vector
        def _(dve):
            for st in (s_max, x_free):
                st.credit(dve)
            for st in G.free:
                st.credit(dve)

            handover.wait(dve, 0)

            def norm(n, b, src, dst):
                for j in range(TT):
                    dve.bn_stats(stats[:, j, :], src[:, j, :])
                dve.drain()
                for j in range(TT):
                    last = dve.bn_aggr(mv[:, j, :], stats[:, j, :])
                ln_stats.done(last)
                ln_rstd.wait(dve, 3 * b + n)
                for j in range(TT):
                    last = dve.tensor_scalar(dst[:, j, :], src[:, j, :], mv[:, j, 0:1], rstd[:, j:j + 1],
                                             ALU.subtract, ALU.mult)
                ln_out.done(last)
                dve.drain()

            def two(ap, jj):
                return ap[:, 2 * jj:2 * jj + 2, :]

            def add_bank(key, dst, jj, b):
                bk = G.wait_full(dve, key, b)
                G.read(key, dve.tensor_tensor(two(dst, jj), two(dst, jj), bk[:, :].rearrange("p (j f) -> p j f", j=2), ALU.add))

            s_mask.wait(dve, 0)
            s_w.wait(dve, 0)
            dve.memset(ones_bf[:, :], 1.0)
            dve.tensor_copy(ident_bf[:, :], ident[:, :])
            last = dve.tensor_scalar(keep_bf[:, :, :], maskT_i[:, :, :], 0.0, None, ALU.not_equal)
            setup_dve.done(last)
            setup_pe.wait(dve, 0)
            dve.tensor_scalar(not_full[:, :], y_bank[:, :], 0.0, None, ALU.is_gt)
            dve.tensor_scalar(keep[:, :, :], maskT_i[:, :, :], 0.0, MASKED, ALU.is_equal, ALU.mult)
            dve.drain()
            dve.tensor_tensor(mask_biasT[:, :, :], keep[:, :, :],
                              not_full[:, :].unsqueeze(1).broadcast_to((P, TT, T)), ALU.mult)
            dve.drain()
            dve.tensor_scalar(keep[:, :, :], mask_i[:, :, :], 0.0, None, ALU.not_equal)
            dve.drain()
            dve.reduce_max(row_keep[:, :], keep[:, :, :], AX.X)
            dve.drain()
            dve.tensor_scalar(keep[:, :, :], mask_i[:, :, :], 0.0, MASKED, ALU.is_equal, ALU.mult)
            dve.drain()
            for j in range(TT):
                last = dve.tensor_scalar(mask_bias[:, j, :], keep[:, j, :], row_keep[:, j:j + 1], None, ALU.mult)
            setup_dve.done(last)
            dve.drain()

            with dve.Fori(0, B) as b:
                s_x.wait(dve, b)
                norm(0, b, x0, xn)
                x_free.done(dve.tensor_tensor(x1[:, :, :], x_in[:, :, :], x0[:, :, :], ALU.add))
                dve.drain()
                dve.tensor_tensor(x1[:, :, :], x1[:, :, :], rows[:, 0, :].unsqueeze(1).broadcast_to((P, TT, D)), ALU.add)
                dve.drain()
                for jj in range(TT // 2):
                    add_bank(("w2", jj), x1, jj, b)
                dve.drain()

                def cut_three(n):
                    qk_hi.wait(dve, 4 * b + 2 * n)
                    qk_lo.done(dve.tensor_tensor(qk[:, n], qk[:, n], qk_part[:, n, 0], ALU.subtract))
                    qk_hi.wait(dve, 4 * b + 2 * n + 1)
                    s_part.done(dve.tensor_tensor(qk_part[:, n, 2], qk[:, n], qk_part[:, n, 1], ALU.subtract))

                norm(1, b, x1, xn)
                cut_three(0)
                for jj in range(TT // 2):
                    key = ("v", jj)
                    bk = G.wait_full(dve, key, b)
                    G.read(key, dve.tensor_tensor(
                        v_sb[:, 2 * jj:2 * jj + 2, :, 0:DH], bk[:, :].rearrange("p (j h e) -> p j h e", j=2, h=H),
                        rows[:, 1, :].rearrange("p (h e) -> p h e", h=H).unsqueeze(1).broadcast_to((P, 2, H, DH)), ALU.add))
                for m in range(KD):
                    bk = G.wait_full(dve, ("q", m), b)
                    G.read(("q", m), dve.scalar_tensor_tensor(qk[:, 1, m, :], bk[:, :], col("bq", m), not_full[:, :],
                                                              ALU.add, ALU.mult))
                cut_three(1)
                with dve.Fori(0, H) as h_:
                    for j in range(TT):
                        s_pre.wait(dve, (b * H + h_) * TT + j)
                        s_max.done(dve.reduce_max(m_col[:, j, bass.ds(h_, 1)], bank[j], AX.X))
                bk = G.wait_full(dve, ("mt",), b)
                dve.tensor_scalar(m_part[:, 0, :], bk[0:H, :], -1.0, None, ALU.mult)
                dve.drain()
                G.read(("mt",), dve.scalar_tensor_tensor(m_rest[:, :], bk[0:H, :], -1.0, m_part[:, 0, :], ALU.mult, ALU.subtract))
                dve.drain()
                dve.tensor_copy(m_part[:, 1, :], m_rest[:, :])
                dve.drain()
                m_cut.done(dve.tensor_tensor(m_part[:, 2, :], m_rest[:, :], m_part[:, 1, :], ALU.subtract))
                for g in range(H // 4):
                    bk = G.wait_full(dve, ("ot", g), b)
                    o = bk[:, :].rearrange("p (j h e) -> p j h e", j=TT, h=4)
                    dve.reciprocal(rsum[:, :, :], o[:, :, :, DH:DH + 1].squeeze(3))
                    dve.drain()
                    dst = o_sb[:, :, g * 4 * DH:(g + 1) * 4 * DH].rearrange("p j (h e) -> p j h e", h=4)
                    for j in range(TT):
                        last = dve.tensor_tensor(dst[:, j], o[:, j, :, 0:DH],
                                                 rsum[:, j, :].unsqueeze(2).broadcast_to((P, 4, DH)), ALU.mult)
                        if j == TT - 2:
                            o_last = last
                    G.read(("ot", g), last)
                    dve.drain()
                    o_ready.done(dve.memset(rsum[:, 0, 0:1], 0.0))
                    dve.drain()
                for jj in range(TT // 2):
                    add_bank(("wo", jj), x1, jj, b)
                dve.drain()
                dve.tensor_tensor(x1[:, :, :], x1[:, :, :], rows[:, 2, :].unsqueeze(1).broadcast_to((P, TT, D)), ALU.add)
                dve.drain()
                norm(2, b, x1, xn)
                for jj in range(TT // 2):
                    key = ("pr", jj)
                    bk = G.wait_full(dve, key, b)
                    G.read(key, dve.tensor_copy(two(y_sb, jj), bk[:, :].rearrange("p (j f) -> p j f", j=2)))
                dve.drain()
                A3 = (slice(None),) * 3
                s_out.wait(dve, b - 1)
                dve.tensor_scalar(spk[A3], y_sb[A3], THRESHOLD, None, ALU.is_gt)
                dve.tensor_scalar(cnt[A3], y_sb[A3], THRESHOLD, None, ALU.is_gt)
                for step in range(1, STEPS):
                    prev = y_sb if step == 1 else mem
                    dve.drain()
                    dve.scalar_tensor_tensor(tmp[A3], prev[A3], BETA, y_sb[A3], ALU.mult, ALU.add)
                    dve.drain()
                    dve.tensor_tensor(mem[A3], tmp[A3], spk[A3], ALU.subtract)
                    dve.drain()
                    dve.scalar_tensor_tensor(cnt[A3], mem[A3], THRESHOLD, cnt[A3], ALU.is_gt, ALU.add)
                    if step < STEPS - 1:
                        dve.tensor_scalar(spk[A3], mem[A3], THRESHOLD, None, ALU.is_gt)
                dve.drain()
                out_ready.done(dve.scalar_tensor_tensor(tmp[A3], cnt[A3], 1.0 / STEPS, x1[A3], ALU.mult, ALU.add))
                dve.drain()

        @block.gpsimd
        def _(pool):
            handover.wait(pool, 0)

            def rstd_of(n, b):
                ln_stats.wait(pool, 3 * b + n)
                settle(pool)
                pool.tensor_scalar(rstd[:, :], mv[:, :, 1], EPS, None, ALU.add)
                pool.drain()
                ln_rstd.done(pool.tensor_tensor(rstd[:, :], rstd[:, :], minus_half[:, :], ALU.pow))
                pool.drain()

            setup_dve.wait(pool, 1)
            pool.memset(k_st[6 * DH:QR, :, :], 1.0)
            pool.drain()
            pool.memset(v_sb[:, :, :, DH:32], 0.0)
            pool.drain()
            s_v.done(pool.memset(v_sb[:, :, :, DH:DH + 1], 1.0))
            pool.drain()
            with pool.Fori(0, B) as b:
                for n in range(3):
                    rstd_of(n, b)


def build(nc, a, out):
    f32, bf16 = mybir.dt.float32, mybir.dt.bfloat16
    where = {"next": -(-nc.sbuf_base // 32) * 32}

    def sb(name, shape, dt=f32, offset=None):
        size = -(-int(np.prod(shape[1:])) * (2 if dt == bf16 else 4) // 32) * 32
        if offset is None:
            offset = where["next"]
            where["next"] += size
            assert where["next"] <= nc.sbuf_usable_end, (name, where["next"])
        where[name] = offset
        return nc.alloc_sbuf_tensor_at(name, shape, dt, offset=offset)

    ident = sb("ident", [P, P])
    flip = sb("flip", [P, P])
    cols = sb("cols", [P, COLS["end"]])
    minus_half = sb("minus_half", [P, TT])
    mid = nc.dram_tensor("mid", ((B + 1) * TT, P, D), f32).ap()

    with ExitStack() as ctx:
        pair = [ctx.enter_context(nc.psum_tensor(f"pair{i}", [P, 2, T], f32)) for i in range(2)]
        bank = [pair[i // 2][:, i % 2, :] for i in range(4)]
        y_bank = ctx.enter_context(nc.psum_tensor("y_bank", [P, T], f32))
        general = [ctx.enter_context(nc.psum_tensor(f"general{i}", [P, T], f32)) for i in range(3)]

        def stage(name, step=1, ahead=0):
            return Stage(ctx.enter_context(nc.semaphore(name)), step, ahead)

        s_const = stage("const_dma", 16 * 3)
        carrier = stage("carrier")
        handover = stage("handover", 5)

        def col(name, k=0, n=1):
            return cols[:, COLS[name] + k:COLS[name] + k + n]

        def settle(eng):
            eng.sem_inc(carrier.sem, 1)

        consts = (ident, flip, cols, minus_half, col, settle, s_const)
        psum = (pair, bank, y_bank, general)
        shared = where["next"]
        mamba_pass(nc, ctx, a, mid, sb, where, stage, psum, consts, handover)
        where["next"] = shared
        attention_pass(nc, ctx, a, mid, out, sb, where, stage, psum, consts, handover)


def _selectors():
    i = np.arange(P)
    ident = np.eye(P, dtype=np.float32)
    sel_r = np.zeros((P, 2, NV, P), np.float32)
    sel_y = np.zeros((P, NV, 32), np.float32)
    sel_bc = np.zeros((RK + 2 * NS, 2, P), np.float32)
    for v in range(NV):
        for p in range(P):
            channel = CC * v + p // NS
            for part in range(2):
                sel_r[32 * part + channel, 0, v, p] = 1
                sel_r[64 + 32 * part + channel, 1, v, p] = 1
            sel_y[p, v, channel] = 1
    for n in range(2):
        sel_bc[RK + NS * n + i % NS, n, i] = 1
    return {"ident": ident, "flip": ident[::-1].copy(), "sel_r": sel_r, "sel_y": sel_y, "sel_bc": sel_bc}


def _layout(x):
    def blocks(v):
        return v.reshape(-1, P).T

    cols = np.zeros((P, COLS["end"]), np.float32)

    def put(name, v):
        cols[:, COLS[name]:COLS[name] + v.shape[1]] = v

    m, t = "L0_attn_", "L0_xattn_"
    for name, key in [("norm_g", m + "norm_g"), ("norm_b", m + "norm_b"), ("ffn_g", m + "ffn_g"), ("ffn_b", m + "ffn_b"),
                      ("b1", m + "b1"), ("bq", t + "bq"), ("bk", t + "bk")]:
        put(name, blocks(x[key]))
    for d in "fb":
        p = m + d + "_"
        put(d + "conv_w", x[p + "conv_w"].reshape(KI, P, CW).transpose(1, 0, 2).reshape(P, KI * CW))
        put(d + "conv_b", blocks(x[p + "conv_b"]))
        put(d + "dt_b", blocks(x[p + "dt_proj_b"]))
        put(d + "D", blocks(x[p + "D"]))
        al = x[p + "A_log"].reshape(NM, NQ, NV, CC, NS).transpose(3, 4, 0, 2, 1)
        put(d + "A_log", al.reshape(P, NC))

    def both(key):
        return np.stack([np.ascontiguousarray(x[m + d + "_" + key].T) for d in "fb"])

    arrays = _selectors()
    arrays["x"] = x["x"].reshape(B * TT, P, D)
    arrays["ctxT"] = x["ctx_1024"].reshape(B * T, D).T
    arrays["mask"] = x["mask_1x1xSxS2_ik0"].reshape(T, T)
    arrays["maskT"] = arrays["mask"].T
    arrays["cols"] = cols
    arrays["rows"] = np.stack([x[m + "b2"], x[t + "bv"], x[t + "bo"]])
    arrays["w_in"] = both("in_proj_w")
    arrays["w_xp"] = both("x_proj_w")
    arrays["w_dt"] = both("dt_proj_w")
    arrays["w_out"] = both("out_proj_w")
    arrays["w_att"] = np.stack([x[t + w].T for w in ("wq", "wk", "wv", "wo")])
    arrays["w1"] = x[m + "w1"].T
    arrays["w2"] = x[m + "w2"].T
    arrays["w_fc"] = x["L0_ffn_W_fc"].T
    arrays["w_proj"] = x["L0_ffn_W_proj"].T
    return {k: np.ascontiguousarray(v) for k, v in arrays.items()}


def kernel(**inputs):
    import concourse.bacc as bacc
    from concourse.bass_utils import run_bass_kernel_spmd

    arrays = _layout({k: np.asarray(v) for k, v in inputs.items()})
    nc = bacc.Bacc("TRN2", target_bir_lowering=False, num_devices=1)
    aps = {k: nc.dram_tensor(k, v.shape, mybir.dt.from_np(v.dtype), kind="ExternalInput").ap() for k, v in arrays.items()}
    out = nc.dram_tensor("out", (B * TT, P, D), mybir.dt.float32, kind="ExternalOutput").ap()
    build(nc, aps, out)
    r = run_bass_kernel_spmd(nc, [arrays], core_ids=[0])
    return r.results[0]["out"].reshape(B, T, D)
```

```python
import concourse.bass as bass
import concourse.mybir as mybir
import numpy as np
from contextlib import ExitStack

B, T, D = 8, 512, 256
DI, NS, RK, CW = 512, 16, 16, 4
FF = 1024
H, DH = 16, 16
P = 128
KD, KI, KF, TT = D // P, DI // P, FF // P, T // P
CC = P // NS
NM = KI
NV = 4
NQ = 4
NG, NC = NM * NV, NM * NV * NQ
QR = 6 * DH + 3
EPS = 1e-5
MASKED = -float(2 ** 32)
FLOOR = -3.0e38
STEPS, BETA, THRESHOLD = 5, 0.9, 1.0

COLS = {}
def _cols():
    at = 0
    for name, n in [("norm_g", KD), ("norm_b", KD), ("ffn_g", KD), ("ffn_b", KD), ("b1", KF), ("bq", KD), ("bk", KD)]:
        COLS[name] = at
        at += n
    for d in "fb":
        for name, n in [("conv_w", KI * CW), ("conv_b", KI), ("dt_b", KI), ("D", KI), ("A_log", NC)]:
            COLS[d + name] = at
            at += n
    COLS["end"] = at
_cols()

Q_PART = [0, 0, 1, 0, 2, 1]
K_PART = [0, 1, 0, 2, 0, 1]


class Stage:

    def __init__(self, sem, step=1, ahead=0):
        self.sem, self.step, self.ahead = sem, step, ahead

    def credit(self, eng, less=0):
        if self.ahead > less:
            eng.sem_inc(self.sem, self.ahead - less)

    def done(self, instruction):
        instruction.then_inc(self.sem, 1)

    def wait(self, eng, index):
        value = (index + 1) * self.step + self.ahead
        if not isinstance(value, int) or value > 0:
            eng.wait_ge(self.sem, value)


def attention_keys():
    def many(kind, n):
        return [(kind, i) for i in range(n)]

    ff = many("w1", KF)
    heads = []
    for g in range(H // 4):
        heads += [("av", g)] + ([("ot", g - 1)] if g else [])
    before = many("hT", KD) + ff + many("w2", 2) + many("k", KD) + many("v", 2) + many("qn", KD) + many("q", KD)
    loop = many("hT", KD) + ff + [("w2", 0), ("mt", 0), ("w2", 1), ("mt", 1)] + heads + many("k", KD) + [("ot", H // 4 - 1)]
    loop += many("on", KD) + many("wo", 2) + many("v", 2) + many("qn", KD) + many("q", KD)
    loop += many("fn", KD) + many("fc", KF) + many("pr", 2)
    skip = ("hT", "w1", "w2", "k", "v", "qn", "q")
    return before, loop, [key for key in loop if key[0] not in skip]


IN_AT = [((0, 1), (3, 4)), ((5, 7), (8, 9)), ((23, 24), (25, 27)), ((29, 31), (32, 33))]
XD_AT = (37, 39, 40, 41)
DT_AT = (12, 28, 44, 60)
REP_AT = (45, 47)
OP_AT = [(11, 13, 15, 16), (17, 19, 20, 21)]
FL_AT = (35, 36)
NF_AT = (52, 53)
NR_AT = [(55, 56), (57, 59)]
SUM_AT, READ_AT = 2, 8
LN_AT = ((28, 30, 33, 41), (44, 45, 46, 50))
LN_GROUP = (7, 10)
ACC_AT = 40


def mamba_keys():
    before = [("nf", k) for k in range(KD)] + [("nr", k) for k in range(KD)]
    for k in range(KI):
        before += [("xi", k), ("z", k)]
    before += [("xd", 0), ("dt", 0), ("rep", 0), ("rep", 1), ("dt", 1)]
    loop = []
    for d in range(2):
        at = [(IN_AT[k][n][0], (kind, KI * d + k)) for k in range(KI) for n, kind in enumerate(("xi", "z"))]
        at += [(XD_AT[0], ("xd", d))] + [(p, ("dt", NM * d + i)) for i, p in enumerate(DT_AT)]
        at += [(p, ("rep", 2 * d + i)) for i, p in enumerate(REP_AT)]
        at += [(OP_AT[j][0], (("opb", "opf")[d], j)) for j in range(TT // 2)]
        if d == 0:
            at += [(p, ("fl", j)) for j, p in enumerate(FL_AT)]
            at += [(p, ("nf", k)) for k, p in enumerate(NF_AT)] + [(p[0], ("nr", k)) for k, p in enumerate(NR_AT)]
        loop += [key for _, key in sorted(at)]
    after = [("opb", j) for j in range(TT // 2)] + [("fl", j) for j in range(TT // 2)]
    return before, loop, after


BEFORE, AFTER = "before", "after"


class Ring:

    def __init__(self, banks, kinds, rounds, before, loop, after):
        self.banks, self.kinds, self.rounds, self.where = banks, kinds, rounds, {}
        users = {}
        for n, key in enumerate(before):
            k = n % len(banks)
            self.where[BEFORE, key] = (k, (BEFORE, users.get(k)))
            users[k] = key
        final = {}
        for n, key in enumerate(loop):
            final[n % len(banks)] = key
        users = {}
        for n, key in enumerate(loop):
            k = n % len(banks)
            self.where["loop", key] = (k, ("this", users[k]) if k in users else ("last", final[k]))
            users[k] = key
        users = {}
        for n, key in enumerate(after):
            k = n % len(banks)
            self.where[AFTER, key] = (k, ("this", users[k]) if k in users else ("last", final[k]))
            users[k] = key

    def index(self, key, b):
        kind, i = key
        full, done, per, first = self.kinds[kind]
        if isinstance(b, str) and b == BEFORE:
            return i
        return per * (self.rounds if isinstance(b, str) else b) + first + i

    def _at(self, key, b):
        return self.where[b if isinstance(b, str) else "loop", key]

    def bank(self, key, b):
        return self.banks[self._at(key, b)[0]]

    def claim(self, pe, key, b):
        k, (when, prev) = self._at(key, b)
        if prev is not None:
            per = self.kinds[prev[0]][2]
            self.kinds[prev[0]][1].wait(pe, self.index(prev, b) - (per if when == "last" else 0))
        return self.banks[k]

    def written(self, key, instruction):
        self.kinds[key[0]][0].done(instruction)

    def wait_full(self, eng, key, b):
        self.kinds[key[0]][0].wait(eng, self.index(key, b))
        return self.bank(key, b)

    def read(self, key, instruction):
        self.kinds[key[0]][1].done(instruction)

    def wait_read(self, eng, key, b):
        self.kinds[key[0]][1].wait(eng, self.index(key, b))


def mamba_pass(nc, ctx, a, mid, sb, where, stage, psum, consts, handover):
    f32, f32r = mybir.dt.float32, mybir.dt.float32r
    ALU, ACT = mybir.AluOpType, mybir.ActivationFunctionType
    ident, flip, cols, minus_half, col, settle, s_const = consts
    pair, bank, y_bank, general = psum

    sel_r = sb("sel_r", [P, 2, NV, P], f32r)
    sel_y = sb("sel_y", [P, NV, 32])
    sel_bc = sb("sel_bc", [RK + 2 * NS, 2, P])
    w_xp = sb("w_xp", [P, 2, KI, RK + 2 * NS])
    w_dt = sb("w_dt", [RK, 2, DI])
    w_out = sb("w_out", [P, 2, KI, D])
    w_in = sb("w_in", [P, 2, KD, 2 * DI])
    x_in = sb("x_in", [P, TT, D])
    x0 = sb("x0", [P, TT, D])
    acc = sb("acc", [P, TT, D])
    xn = sb("xn", [P, TT, D])
    r_bwd = sb("r_bwd", [P, TT, D])
    x_out = sb("x_out", [P, TT, D])
    xnT = sb("xnT", [P, 2, KD, T])
    stats = sb("stats", [P, TT, 6])
    mv = sb("mv", [P, TT, 2])
    rstd = sb("rstd", [P, TT])
    u = sb("u", [P, 2, KI, T])
    zs = sb("zs", [P, 2, KI, T])
    B_rep = sb("B_rep", [P, 2, T])
    C_rep = sb("C_rep", [P, 2, T])
    yT = sb("yT", [P, KI, T])
    yt = sb("yt", [P, T])
    xd_sb = sb("xd_sb", [RK + 2 * NS, T])
    xi = sb("xi", [P, T + CW - 1])
    cv = sb("cv", [P, 2, T])
    th_c = sb("th_c", [P, T])
    th_z = sb("th_z", [P, T])
    ab = sb("ab", [P, T])
    delta = sb("delta", [P, T])
    du = sb("du", [P, T])
    cut = [sb(f"cut{s}", [P, T], f32r) for s in range(4)]
    parts = sb("parts", [P, 2, NQ, T], f32r)
    h = sb("h", [P, 2, NQ, T])
    hC = sb("hC", [P, 2, NQ, T])
    dA = sb("dA", [P, NQ, T])
    dBu = sb("dBu", [P, 2, T])
    sel_raw = sb("sel_raw", [P, 2, NV, P], f32, where["h"])

    def kind(name, per, first=0):
        return stage(name + "_full"), stage(name + "_done", ahead=per), per, first

    kinds = {"nf": kind("nf", KD, KD), "nr": kind("nr", KD, KD), "xi": kind("xi", 2 * KI, KI),
             "z": kind("z", 2 * KI, KI), "xd": kind("xd", 2, 1), "dt": kind("dt", 2 * NM, 2),
             "rep": kind("rep", 4, 2), "opf": kind("opf", TT // 2), "opb": kind("opb", TT // 2),
             "fl": kind("fl", TT // 2)}
    readers = {"z": "dve", "opf": "dve", "fl": "dve"}
    G = Ring(general, kinds, B, *mamba_keys())
    s_w = stage("mamba_weights_dma", 16 * 11)
    s_x = stage("x_dma", 16)
    s_parts = stage("parts_dma", 16 * 16)
    s_mid = stage("mid_dma", 16, ahead=16)
    setup = stage("setup_dve")
    a_log = stage("a_log")
    ln_stats = stage("ln_stats")
    ln_rstd = stage("ln_rstd")
    ln_out = stage("ln_out")
    acc_set = stage("acc_set")
    tap = stage("conv_tap")
    th_conv = stage("th_conv")
    th_gate = stage("th_gate")
    u_done = stage("u_done")
    soft_exp = stage("soft_exp")
    soft = stage("soft")
    d_ready = stage("d_ready")
    du_ready = stage("du_ready")
    hi_ready = stage("hi_ready")
    lo_ready = stage("lo_ready", ahead=2)
    s_rd = stage("spread_delta")
    s_ru = stage("spread_du", ahead=1)
    s_dA = stage("dA", ahead=2)
    s_dBu = stage("dBu", ahead=2)
    s_scan = stage("scan", ahead=4)
    s_hC = stage("hC", ahead=2)
    s_y = stage("y_sum", ahead=4)
    s_yread = stage("y_read", ahead=2 * NM)
    s_yT = stage("yT", ahead=2 * NM)

    def credits(eng, name):
        for k, (_, done, _, _) in kinds.items():
            if readers.get(k, "act") == name:
                done.credit(eng)

    def targets(U, d):
        return [(p, U * NM + 1 + i, (d + (1 + i) // NM) % 2, (1 + i) % NM)
                for i, p in enumerate((DT_AT[-1] - NC,) + DT_AT)]

    def gate_y(eng, tb, n, m):
        s_yread.wait(eng, tb)
        s_yT.done(eng.tensor_tensor(yT[:, m, :], yt[:, :], zs[:, n, m, :], ALU.mult))

    class Plan:

        def __init__(self):
            self.steps = {}

        def at(self, p, fn):
            if 0 <= p < NC:
                self.steps.setdefault(p, []).append(fn)

        def run(self, p):
            for fn in self.steps.get(p, []):
                fn()

    with nc.Block() as block:
        @block.sync
        def _(sp):
            s_mid.credit(sp)

            def dma(st, o, i):
                sp.dma_start(o, i).then_inc(st.sem, 16)

            def load_x(b):
                dma(s_x, x_in[:, :, :], a["x"][bass.ds(b * TT, TT)].rearrange("j p f -> p j f"))

            def stack(tb, m):
                if not isinstance(tb, int):
                    s_ru.wait(sp, (tb - 2) * NV * NQ + NV * NQ - 1)
                for s in range(4):
                    (lo_ready if s % 2 else hi_ready).wait(sp, 2 * tb + s // 2)
                    for q in range(NQ):
                        dma(s_parts, parts[32 * s:32 * s + 32, m % 2, q, :].bitcast(f32),
                            cut[s][32 * q:32 * q + 32, :].bitcast(f32))

            def store(b, slot):
                G.wait_read(sp, ("fl", TT // 2 - 1), b)
                dma(s_mid, mid[bass.ds(slot * TT, TT)].rearrange("j p f -> p j f"), x_out[:, :, :])

            load_x(0)
            dma(s_const, ident[:, :], a["ident"])
            dma(s_const, flip[:, :], a["flip"])
            dma(s_const, cols[:, :], a["cols"])
            for d in range(2):
                dma(s_w, w_in[:, d], a["w_in"][d].rearrange("(k p) e -> p k e", p=P))
            dma(s_w, sel_raw[:, :, :, :], a["sel_r"])
            dma(s_w, sel_y[:, :, :], a["sel_y"])
            dma(s_w, sel_bc[:, :, :], a["sel_bc"])
            for d in range(2):
                dma(s_w, w_xp[:, d], a["w_xp"][d].rearrange("(k p) e -> p k e", p=P))
                dma(s_w, w_out[:, d], a["w_out"][d].rearrange("(k p) e -> p k e", p=P))
                dma(s_w, w_dt[:, d], a["w_dt"][d])
            ln_out.wait(sp, 0)
            load_x(1)
            stack(0, 0)
            with sp.Fori(0, B) as b:
                for d in range(2):
                    U = 2 * b + d
                    stack(U * NM + 1, 1)
                    stack(U * NM + 2, 2)
                    if d == 0:
                        store(b, b)
                    stack(U * NM + 3, 3)
                    if d == 0:
                        ln_out.wait(sp, 2 * b + 2)
                        settle(sp)
                        load_x((b + 2) % B)
                    stack(U * NM + 4, 0)
                settle(sp)
            s_mid.wait(sp, B - 1)
            store(AFTER, B)
            s_mid.wait(sp, B)
            s_x.wait(sp, B + 1)
            s_parts.wait(sp, 2 * B * NM)
            sp.sem_inc(handover.sem, 1)

        @block.tensor
        def _(pe):
            s_ru.credit(pe)
            s_y.credit(pe, less=2)

            def mm(o, lhsT, rhs, start=True, stop=True):
                return pe.matmul(o, lhsT, rhs, start=start, stop=stop)

            def step(key, b, n, steps, products):
                bk = G.claim(pe, key, b) if n == 0 else G.bank(key, b)
                last = products(bk)
                if n == steps - 1:
                    G.written(key, last)

            def in_proj(kind, slot, beta, n, k, kk, b):
                if k == 0 and kk == 0 and kind == "xi":
                    kinds["nr" if n else "nf"][1].wait(pe, KD * beta + KD - 1)
                e = (DI if kind == "z" else 0) + k * P
                step((kind, KI * slot + k), b, kk, KD,
                     lambda bk: mm(bk[:, :], w_in[:, n, kk, e:e + P], xnT[:, n, kk, :], kk == 0, kk == KD - 1))

            def x_proj(slot, N, n, kk, b):
                u_done.wait(pe, N * KI + kk)
                step(("xd", slot), b, kk, KI,
                     lambda bk: mm(bk[0:RK + 2 * NS, :], w_xp[:, n, kk, :], u[:, n, kk, :], kk == 0, kk == KI - 1))

            def dt_proj(i, N, n, m, b):
                if m == 0:
                    kinds["xd"][1].wait(pe, N)
                step(("dt", i), b, 0, 1, lambda bk: mm(bk[:, :], w_dt[:, n, m * P:(m + 1) * P], xd_sb[0:RK, :]))

            def rep(slot, n, b):
                step(("rep", 2 * slot + n), b, 0, 1, lambda bk: mm(bk[:, :], sel_bc[:, n, :], xd_sb[:, :]))

            def out_proj(kind, U, d, jj, part, b):
                half, first = part // 2, 2 * (part % 2)
                if jj == 0 and part == 0:
                    s_yT.wait(pe, U * NM + NM - 1)

                def products(bk):
                    j = 2 * jj + half
                    for k in (first, first + 1):
                        last = mm(bk[:, half * D:(half + 1) * D], yT[:, k, j * P:(j + 1) * P], w_out[:, d, k, :],
                                  k == 0, k == KI - 1)
                    return last
                step((kind, jj), b, part, 4, products)

            def flip_back(jj, b):
                G.wait_read(pe, ("opb", TT // 2 - 1), b)

                def products(bk):
                    for half in range(2):
                        j = TT - 1 - (2 * jj + half)
                        last = mm(bk[:, half * D:(half + 1) * D], flip[:, :], r_bwd[:, j, :])
                    return last
                step(("fl", jj), b, 0, 1, products)

            def to_features(k, beta, b):
                ln_out.wait(pe, 2 * beta + 1)

                def products(bk):
                    for j in range(TT):
                        last = pe.transpose(bk[:, j * P:(j + 1) * P], xn[:, j, k * P:(k + 1) * P], ident[:, :])
                    return last
                step(("nf", k), b, 0, 1, products)

            def to_features_reversed(k, part, b):
                def products(bk):
                    for j in (2 * part, 2 * part + 1):
                        r = TT - 1 - j
                        last = mm(bk[:, r * P:(r + 1) * P], xn[:, j, k * P:(k + 1) * P], flip[:, :])
                    return last
                step(("nr", k), b, part, 2, products)

            def spread_delta(U, g):
                m, v, q = g // (NV * NQ), g // NQ % NV, g % NQ
                if g % (NV * NQ) == 0:
                    s_parts.wait(pe, U * NM + m)
                s_dA.wait(pe, U * NC + g - 2)
                s_rd.done(mm(bank[g % 2], sel_r[:, 0, v, :], parts[:, m % 2, q, :]))

            def spread_du(U, g):
                m, v, q = g // (NV * NQ), g // NQ % NV, g % NQ
                s_dBu.wait(pe, U * NC + g - 2)
                s_ru.done(mm(bank[2 + g % 2], sel_r[:, 1, v, :], parts[:, m % 2, q, :]))

            def sum_states(U, g):
                v = g % NV
                s_hC.wait(pe, U * NG + g)
                if v == 0:
                    s_yread.wait(pe, U * NM + g // NV - 1)
                for q in range(NQ):
                    last = mm(y_bank[32 * q:32 * q + 32, :], sel_y[:, v, :], hC[:, v % 2, q, :], v == 0, v == NV - 1)
                s_y.done(last)

            s_const.wait(pe, 0)
            s_w.wait(pe, 0)
            setup.wait(pe, 0)
            for v in range(2):
                for q in range(NQ):
                    mm(y_bank[32 * q:32 * q + 32, :], sel_y[:, v, :], hC[:, v % 2, q, :], v == 0, False)
            for k in range(KD):
                to_features(k, 0, BEFORE)
            for k in range(KD):
                for part in range(2):
                    to_features_reversed(k, part, BEFORE)
            for k in range(KI):
                for kind in ("xi", "z"):
                    for kk in range(KD):
                        in_proj(kind, 0, 0, 0, k, kk, BEFORE)
            for kk in range(KI):
                x_proj(0, 0, 0, kk, BEFORE)
            dt_proj(0, 0, 0, 0, BEFORE)
            for n in range(2):
                rep(0, n, BEFORE)
            dt_proj(1, 0, 0, 1, BEFORE)
            spread_delta(0, 0)
            for key in mamba_keys()[0][-3:]:
                G.wait_read(pe, key, BEFORE)

            with pe.Fori(0, B) as b:
                for d in range(2):
                    U, N, n, beta = 2 * b + d, 2 * b + d + 1, 1 - d, b + d
                    plan = Plan()
                    for k in range(KI):
                        for kind, at in zip(("xi", "z"), IN_AT[k]):
                            for kk in range(KD):
                                plan.at(at[kk], lambda kind=kind, k=k, kk=kk: in_proj(kind, d, beta, n, k, kk, b))
                    for kk, p in enumerate(XD_AT):
                        plan.at(p, lambda kk=kk: x_proj(d, N, n, kk, b))
                    for i, p in enumerate(DT_AT):
                        ahead = (i + 2) // NM
                        plan.at(p, lambda i=i, ahead=ahead: dt_proj(NM * d + i, N, (d + ahead) % 2, (i + 2) % NM, b))
                    for i, p in enumerate(REP_AT):
                        plan.at(p, lambda i=i: rep(d, i, b))
                    for jj in range(TT // 2):
                        for part, p in enumerate(OP_AT[jj]):
                            plan.at(p, lambda jj=jj, part=part: out_proj(("opb", "opf")[d], U - 1, 1 - d, jj, part, b))
                    if d == 0:
                        for jj, p in enumerate(FL_AT):
                            plan.at(p, lambda jj=jj: flip_back(jj, b))
                        for k, p in enumerate(NF_AT):
                            plan.at(p, lambda k=k: to_features(k, b + 1, b))
                        for k in range(KD):
                            for part, p in enumerate(NR_AT[k]):
                                plan.at(p, lambda k=k, part=part: to_features_reversed(k, part, b))
                    for g in range(NC):
                        spread_du(U, g)
                        spread_delta(U, g + 1)
                        if g % NQ == SUM_AT:
                            sum_states(U, g // NQ - 2)
                        plan.run(g)
            for i in range(2):
                sum_states(2 * B, i - 2)
            for jj in range(TT // 2):
                for part in range(4):
                    out_proj("opb", 2 * B - 1, 1, jj, part, AFTER)
            for jj in range(TT // 2):
                flip_back(jj, AFTER)
            settle(pe)
            pe.sem_inc(handover.sem, 1)

        @block.scalar
        def _(act):
            s_dA.credit(act)
            credits(act, "act")

            def f(o, i, fn=ACT.Copy, **kw):
                return act.activation(o, i, fn, **kw)

            def evacuate(key, o, b, fn=ACT.Copy, view=None, **kw):
                bk = G.wait_full(act, key, b)
                G.read(key, f(o, bk[:, :] if view is None else view(bk), fn, **kw))

            def normed(kind, n, k, b):
                evacuate((kind, k), xnT[:, n, k, :], b, ACT.Identity, scale=col("norm_g", k), bias=col("norm_b", k))

            def conv_in(slot, N, n, k, b):
                tap.wait(act, (CW - 1) * (N * KI + k) - 1)
                u_done.wait(act, N * KI + k - 2)
                key = ("xi", KI * slot + k)
                bk = G.wait_full(act, key, b)
                f(xi[:, CW - 1:], bk[:, :])
                G.read(key, f(cv[:, k % 2, :], bk[:, :], ACT.Identity, scale=col("fb"[n] + "conv_w", CW * k + CW - 1),
                              bias=col("fb"[n] + "conv_b", k)))

            def gate_tanh(slot, N, k, b):
                kinds["z"][1].wait(act, N * KI + k - 1)
                bk = G.wait_full(act, ("z", KI * slot + k), b)
                th_gate.done(f(th_z[:, :], bk[:, :], ACT.Tanh, scale=0.5))

            def conv_tanh(N, k):
                tap.wait(act, (CW - 1) * (N * KI + k) + CW - 2)
                th_conv.done(f(th_c[:, :], cv[:, k % 2, :], ACT.Tanh))

            def soft_in(i, tb, n, m, b):
                lo_ready.wait(act, 2 * tb - 2)
                du_ready.wait(act, tb - 1)
                bk = G.wait_full(act, ("dt", i), b)
                bias = col("fb"[n] + "dt_b", m)
                f(ab[:, :], bk[:, :], ACT.Abs, bias=bias)
                G.read(("dt", i), f(delta[:, :], bk[:, :], ACT.Relu, bias=bias))

            def soft_1(tb):
                kinds["dt"][1].wait(act, tb)
                soft_exp.done(f(ab[:, :], ab[:, :], ACT.Exp, scale=-1.0))

            def soft_2(tb):
                soft_exp.wait(act, tb)
                soft.done(f(ab[:, :], ab[:, :], ACT.Ln, bias=1.0))

            def high(tb, which):
                if which == 0:
                    s_parts.wait(act, tb - 1)
                (du_ready if which else d_ready).wait(act, tb)
                hi_ready.done(f(cut[2 * which][:, :], (du if which else delta)[:, :]))

            def copy_acc(b):
                G.wait_read(act, ("fl", TT // 2 - 1), b)
                ln_out.wait(act, 2 * b)
                acc_set.done(f(acc[:, :, :], x0[:, :, :]))

            s_const.wait(act, 0)
            for d in "fb":
                last = f(col(d + "A_log", 0, NC), col(d + "A_log", 0, NC), ACT.Exp)
            a_log.done(last)
            setup.wait(act, 0)
            for n, kind in enumerate(("nf", "nr")):
                for k in range(KD):
                    normed(kind, n, k, BEFORE)
            for k in range(KI):
                conv_in(0, 0, 0, k, BEFORE)
                gate_tanh(0, 0, k, BEFORE)
                conv_tanh(0, k)
            evacuate(("xd", 0), xd_sb[:, :], BEFORE, view=lambda bk: bk[0:RK + 2 * NS, :])
            soft_in(0, 0, 0, 0, BEFORE)
            soft_1(0)
            soft_2(0)
            evacuate(("rep", 0), B_rep[:, 0, :], BEFORE)
            evacuate(("rep", 1), C_rep[:, 0, :], BEFORE)
            high(0, 0)
            high(0, 1)
            soft_in(1, 1, 0, 1, BEFORE)
            soft_1(1)
            soft_2(1)

            with act.Fori(0, B) as b:
                for d in range(2):
                    U, N, n = 2 * b + d, 2 * b + d + 1, 1 - d
                    plan = Plan()
                    for k in range(KI):
                        (_, x_end), (_, z_end) = IN_AT[k]
                        plan.at(x_end + 1, lambda k=k: conv_in(d, N, n, k, b))
                        plan.at(z_end + 1, lambda k=k: gate_tanh(d, N, k, b))
                        plan.at(x_end + 6, lambda k=k: conv_tanh(N, k))
                    plan.at(XD_AT[-1] + 1, lambda: evacuate(("xd", d), xd_sb[:, :], b, view=lambda bk: bk[0:RK + 2 * NS, :]))
                    for i, rows in enumerate((B_rep, C_rep)):
                        plan.at(REP_AT[i] + 1, lambda i=i, rows=rows: evacuate(("rep", 2 * d + i), rows[:, n, :], b))
                    for i, (p, tb, nt, m) in enumerate(targets(U, d)):
                        plan.at(p + 1, lambda i=i, tb=tb, nt=nt, m=m: soft_in(NM * d + i - 1, tb, nt, m, b))
                        plan.at(p + 2, lambda tb=tb: soft_1(tb))
                        plan.at(p + 3, lambda tb=tb: soft_2(tb))
                        plan.at(p + 6, lambda tb=tb: high(tb, 0))
                        plan.at(p + 8, lambda tb=tb: high(tb, 1))
                    if d == 0:
                        for jj in range(TT // 2):
                            plan.at(OP_AT[jj][-1] + 1, lambda jj=jj: evacuate(
                                ("opb", jj), r_bwd[:, 2 * jj:2 * jj + 2, :], b,
                                view=lambda bk: bk[:, :].rearrange("p (j f) -> p j f", j=2)))
                        plan.at(ACC_AT, lambda: copy_acc(b))
                        for k, p in enumerate(NF_AT):
                            plan.at(p + 1, lambda k=k: normed("nf", 0, k, b))
                        for k, p in enumerate(NR_AT):
                            plan.at(p[-1] + 1, lambda k=k: normed("nr", 1, k, b))
                    for g in range(NC):
                        m, v, q = g // (NV * NQ), g // NQ % NV, g % NQ
                        c = U * NC + g
                        s_rd.wait(act, c)
                        s_scan.wait(act, c - 4)
                        s_dA.done(f(dA[:, q, :], bank[q % 2], ACT.Exp, scale=col("fb"[d] + "A_log", g)))
                        plan.run(g)
            for jj in range(TT // 2):
                evacuate(("opb", jj), r_bwd[:, 2 * jj:2 * jj + 2, :], AFTER,
                         view=lambda bk: bk[:, :].rearrange("p (j f) -> p j f", j=2))
            act.sem_inc(handover.sem, 1)

        @block.vector
        def _(dve):
            s_dBu.credit(dve)
            s_scan.credit(dve)
            s_yread.credit(dve, less=1)
            s_yT.credit(dve, less=1)
            credits(dve, "dve")

            def norm_stats(src, half):
                for j in (2 * half, 2 * half + 1):
                    dve.bn_stats(stats[:, j, :], src[:, j, :])

            def norm_mean():
                dve.drain()
                for j in range(TT):
                    last = dve.bn_aggr(mv[:, j, :], stats[:, j, :])
                ln_stats.done(last)

            def norm_apply(n, beta, src, dst):
                ln_rstd.wait(dve, 2 * beta + n)
                for j in range(TT):
                    last = dve.tensor_scalar(dst[:, j, :], src[:, j, :], mv[:, j, 0:1], rstd[:, j:j + 1],
                                             ALU.subtract, ALU.mult)
                ln_out.done(last)

            def norm_steps(beta, b):
                def load():
                    s_x.wait(dve, beta)
                    norm_stats(x_in, 0)

                def apply_0():
                    if not isinstance(beta, int):
                        acc_set.wait(dve, b)
                    norm_apply(0, beta, x_in, x0)

                def stats_1():
                    ln_out.wait(dve, 2 * beta)
                    norm_stats(x0, 0)

                def apply_1():
                    if not isinstance(beta, int):
                        kinds["nr"][0].wait(dve, KD * beta - 1)
                    norm_apply(1, beta, x0, xn)
                return ((load, lambda: norm_stats(x_in, 1), norm_mean, apply_0),
                        (stats_1, lambda: norm_stats(x0, 1), norm_mean, apply_1))

            def conv_tap(N, n, k, t):
                i = (CW - 1) * (N * KI + k) + t
                if t == 0:
                    kinds["xi"][1].wait(dve, N * KI + k)
                else:
                    tap.wait(dve, i - 1)
                tap.done(dve.scalar_tensor_tensor(cv[:, k % 2, :], xi[:, t:t + T], col("fb"[n] + "conv_w", CW * k + t),
                                                  cv[:, k % 2, :], ALU.mult, ALU.add))

            def gate(slot, N, n, k, b):
                th_gate.wait(dve, N * KI + k)
                s_yT.wait(dve, (N - 2) * NM + k)
                key = ("z", KI * slot + k)
                G.read(key, dve.scalar_tensor_tensor(zs[:, n, k, :], th_z[:, :], 1.0, G.bank(key, b)[:, :], ALU.add, ALU.mult))

            def make_u(N, n, k):
                th_conv.wait(dve, N * KI + k)
                s_yread.wait(dve, (N - 2) * NM + k)
                u_done.done(dve.scalar_tensor_tensor(u[:, n, k, :], th_c[:, :], 1.0, cv[:, k % 2, :], ALU.add, ALU.mult))

            def read_y(tb, n, m):
                s_y.wait(dve, NV * tb + NV - 1)
                s_yT.wait(dve, tb - 1)
                s_yread.done(dve.scalar_tensor_tensor(yt[:, :], u[:, n, m, :], col("fb"[n] + "D", m), y_bank[:, :],
                                                      ALU.mult, ALU.add))

            def tiles(ap, jj):
                return ap[:, 2 * jj:2 * jj + 2, :]

            def add_forward(jj, b):
                acc_set.wait(dve, b)
                bk = G.wait_full(dve, ("opf", jj), b)
                G.read(("opf", jj), dve.tensor_tensor(tiles(acc, jj), tiles(acc, jj),
                                                      bk[:, :].rearrange("p (j f) -> p j f", j=2), ALU.add))

            def add_backward(jj, b):
                bb = B if isinstance(b, str) else b
                s_mid.wait(dve, bb - 1)
                kinds["opf"][1].wait(dve, (TT // 2) * bb - 1)
                bk = G.wait_full(dve, ("fl", jj), b)
                G.read(("fl", jj), dve.tensor_tensor(tiles(x_out, jj), tiles(acc, jj),
                                                     bk[:, :].rearrange("p (j f) -> p j f", j=2), ALU.add))

            dve.memset(hC[:, :, :, :], 0.0)
            dve.memset(u[:, 1], 0.0)
            dve.memset(zs[:, 1], 0.0)
            dve.memset(yT[:, :, :], 0.0)
            dve.memset(acc[:, :, :], 0.0)
            dve.memset(xi[:, 0:CW - 1], 0.0)
            dve.memset(minus_half[:, :], -0.5)
            s_const.wait(dve, 0)
            s_w.wait(dve, 0)
            dve.tensor_copy(sel_r[:, :, :, :], sel_raw[:, :, :, :])
            for dn in "fb":
                cw = col(dn + "conv_w", 0, KI * CW + KI)
                dve.tensor_scalar(cw, cw, 0.5, None, ALU.mult)
            a_log.wait(dve, 0)
            for dn in "fb":
                al = col(dn + "A_log", 0, NC)
                dve.tensor_scalar(al, al, -1.0, None, ALU.mult)
            setup.done(dve.tensor_scalar(w_out[:, :, :, :], w_out[:, :, :, :], 0.25, None, ALU.mult))
            dve.drain()
            for norm in norm_steps(0, BEFORE):
                for fn in norm:
                    fn()
            for k in range(KI):
                for t in range(CW - 1):
                    conv_tap(0, 0, k, t)
                gate(0, 0, 0, k, BEFORE)
                make_u(0, 0, k)

            with dve.Fori(0, B) as b:
                for d in range(2):
                    U, N, n = 2 * b + d, 2 * b + d + 1, 1 - d
                    plan = Plan()
                    for k in range(KI):
                        (_, x_end), (_, z_end) = IN_AT[k]
                        for t in range(CW - 1):
                            plan.at(x_end + 2 + t, lambda k=k, t=t: conv_tap(N, n, k, t))
                        plan.at(z_end + 3, lambda k=k: gate(d, N, n, k, b))
                        plan.at(x_end + 8, lambda k=k: make_u(N, n, k))
                    for m in range(NM):
                        tb = U * NM + m - 1
                        nm = (1 - d, NM - 1) if m == 0 else (d, m - 1)
                        plan.at(NV * NQ * m + READ_AT, lambda tb=tb, nm=nm: read_y(tb, *nm))
                        if m == 0:
                            plan.at(READ_AT + 1, lambda tb=tb, nm=nm: gate_y(dve, tb, *nm))
                    if d == 0:
                        for jj, p in enumerate(FL_AT):
                            plan.at(p + 2, lambda jj=jj: add_backward(jj, b))
                        for at, norm in zip(LN_AT, norm_steps(b + 1, b)):
                            for p, fn in zip(at, norm):
                                plan.at(p, fn)
                    else:
                        for jj in range(TT // 2):
                            plan.at(OP_AT[jj][-1] + 2, lambda jj=jj: add_forward(jj, b))
                    for g in range(NC + 1):
                        c = U * NC + g
                        if g < NC:
                            if g == 0:
                                kinds["rep"][1].wait(dve, 2 * U + 1)
                            s_ru.wait(dve, c)
                            s_scan.wait(dve, c - 2)
                            s_dBu.done(dve.tensor_tensor(dBu[:, g % 2, :], bank[2 + g % 2], B_rep[:, d, :], ALU.mult))
                        if g > 0:
                            v, q = (g - 1) // NQ % NV, (g - 1) % NQ
                            if q == 0:
                                s_hC.wait(dve, U * NG + (g - 1) // NQ - 2)
                            s_dA.wait(dve, c - 1)
                            s_dBu.wait(dve, c - 1)
                            s_scan.done(dve.tensor_tensor_scan(h[:, v % 2, q, :], dA[:, q, :], dBu[:, (g - 1) % 2, :],
                                                               0.0, ALU.mult, ALU.add))
                        plan.run(g)
            read_y(2 * B * NM - 1, 1, NM - 1)
            gate_y(dve, 2 * B * NM - 1, 1, NM - 1)
            for jj in range(TT // 2):
                add_backward(jj, AFTER)
            dve.sem_inc(handover.sem, 1)

        @block.gpsimd
        def _(pool):
            s_hC.credit(pool)

            def rstd_of(n, beta):
                ln_stats.wait(pool, 2 * beta + n)
                settle(pool)
                pool.tensor_scalar(rstd[:, :], mv[:, :, 1], EPS, None, ALU.add)
                pool.drain()
                ln_rstd.done(pool.tensor_tensor(rstd[:, :], rstd[:, :], minus_half[:, :], ALU.pow))
                pool.drain()

            def make_delta(tb):
                soft.wait(pool, tb)
                d_ready.done(pool.tensor_tensor(delta[:, :], delta[:, :], ab[:, :], ALU.add))

            def make_du(tb, n, m):
                lo_ready.wait(pool, 2 * tb - 1)
                u_done.wait(pool, tb)
                d_ready.wait(pool, tb)
                du_ready.done(pool.tensor_tensor(du[:, :], delta[:, :], u[:, n, m, :], ALU.mult))

            def low(tb, which):
                hi_ready.wait(pool, 2 * tb + which)
                if which:
                    du_ready.wait(pool, tb)
                lo_ready.done(pool.tensor_tensor(cut[2 * which + 1][:, :], (du if which else delta)[:, :],
                                                cut[2 * which][:, :].bitcast(f32), ALU.subtract))

            lo_ready.credit(pool)
            setup.wait(pool, 0)
            rstd_of(0, 0)
            rstd_of(1, 0)
            make_delta(0)
            make_du(0, 0, 0)
            low(0, 0)
            low(0, 1)
            make_delta(1)
            make_du(1, 0, 1)
            with pool.Fori(0, B) as b:
                for d in range(2):
                    U = 2 * b + d
                    kinds["rep"][1].wait(pool, 2 * U + 1)
                    plan = Plan()
                    for p, tb, nt, m in targets(U, d):
                        plan.at(p // NQ - 1, lambda tb=tb, nt=nt, m=m: (make_delta(tb), make_du(tb, nt, m)))
                        if p < 0:
                            low(tb, 0)
                            low(tb, 1)
                        elif p < DT_AT[-1]:
                            plan.at(p // NQ, lambda tb=tb: (low(tb, 0), low(tb, 1)))
                    for m in range(1, NM):
                        plan.at(NV * m + READ_AT // NQ - 1, lambda m=m: gate_y(pool, U * NM + m - 1, d, m - 1))
                    if d == 0:
                        for n, g in enumerate(LN_GROUP):
                            plan.at(g, lambda n=n: rstd_of(n, b + 1))
                    for g in range(NG):
                        s_scan.wait(pool, U * NC + g * NQ + NQ - 1)
                        s_y.wait(pool, U * NG + g - 2)
                        s_hC.done(pool.tensor_tensor(hC[:, g % 2], h[:, g % 2],
                                                     C_rep[:, d, :].unsqueeze(1).broadcast_to((P, NQ, T)), ALU.mult))
                        plan.run(g)
            pool.sem_inc(handover.sem, 1)


def attention_pass(nc, ctx, a, mid, out, sb, where, stage, psum, consts, handover):
    f32, bf16, i32 = mybir.dt.float32, mybir.dt.bfloat16, mybir.dt.int32
    ALU, ACT, AX = mybir.AluOpType, mybir.ActivationFunctionType, mybir.AxisListType
    ident, flip, cols, minus_half, col, settle, s_const = consts
    pair, bank, y_bank, general = psum
    KB = 1024

    ident_bf = sb("ident_bf", [P, P], bf16)
    ones_bf = sb("ones_bf", [P, P], bf16)
    rows = sb("rows", [P, 3, D])
    w_att = sb("w_att", [P, 4, KD, D])
    w_up = sb("w_up", [P, 2, KD, FF])
    w_down = sb("w_down", [P, 2, KF, D])
    x_in = sb("x_in2", [P, TT, D])
    x0 = sb("x_mid", [P, TT, D])
    x1n = sb("x1n", [P, TT, D])
    x1 = sb("x1", [P, TT, D])
    x_res = sb("x_res", [P, TT, D])
    xn = sb("xn2", [P, TT, D])
    xn_q = sb("xn_q", [P, TT, D])
    o_sb = sb("o_sb", [P, TT, D])
    xT = sb("xT", [P, 2, KD, T])
    ctxT = sb("ctxT", [P, KD, T])
    mask_bias = sb("mask_bias", [P, TT, T], bf16)
    mask_biasT = sb("mask_biasT", [P, TT, T], bf16)
    not_full = sb("not_full", [P, T])
    stats = sb("stats2", [P, TT, 6])
    mv = sb("mv2", [P, TT, 2])
    rstd = sb("rstd2", [P, TT])
    row_keep = sb("row_keep", [P, TT])
    q_st = sb("q_st", [P, H, T], bf16)
    k_st = sb("k_st", [P, H, T], bf16)
    pr = sb("pr", [P, 4, TT, T])
    v_sb = sb("v_sb", [P, TT, H, 32])
    qk = sb("qk", [P, 2, KD, T])
    qk_part = sb("qk_part", [P, 2, 3, KD, T], bf16)
    oT = sb("oT", [P, 2, T])
    m_col = sb("m_col", [P, TT, H])
    m_part = sb("m_part", [H // 2, 2, 3, T], bf16)
    m_rest = sb("m_rest", [H // 2, T])
    rsum = sb("rsum", [P, TT, 4])
    y_sb = sb("y_sb", [P, TT, D])
    g1 = sb("g1", [P, KF, T], f32, where["pr"])
    g0 = sb("g0", [P, T], f32, where["pr"] + 16 * KB)
    masked = sb("masked", [P, 2, T], f32, where["pr"] + 20 * KB)
    mem, spk, cnt, tmp = (sb(name, [P, TT, D], f32, where["qk"] + 4 * KB * n)
                          for n, name in enumerate(("mem", "spk", "cnt", "tmp")))
    mask_i = sb("mask_i", [P, TT, T], i32, where["q_st"])
    maskT_i = sb("maskT_i", [P, TT, T], i32, where["q_st"] + 8 * KB)
    keep = sb("keep", [P, TT, T], f32, where["k_st"])
    keep_bf = sb("keep_bf", [P, TT, T], bf16, where["k_st"] + 8 * KB)

    qk_dram = nc.dram_tensor("qk_parts", (2, 3, D, T), bf16).ap()
    m_dram = nc.dram_tensor("max_parts", (3, H, T), bf16).ap()


    def kind(name, per, first=0):
        return stage(name + "_full"), stage(name + "_done", ahead=per), per, first

    kinds = {"hT": kind("hT", KD, KD), "w1": kind("w1", KF, KF), "mt": kind("mt", 2), "w2": kind("w2", 2, 2),
             "av": kind("av", H // 4), "ot": kind("ot", H // 4), "k": kind("k", KD, KD), "on": kind("on", KD),
             "wo": kind("wo", 2), "v": kind("v", 2, 2), "qn": kind("qn", KD, KD), "q": kind("q", KD, KD),
             "fn": kind("fn", KD), "fc": kind("fc", KF), "pr": kind("pr", 2)}
    on_dve = ("mt", "w2", "ot", "wo", "v", "q", "pr")
    G = Ring(general + [y_bank], kinds, B - 1, *attention_keys())
    s_up = stage("w1_dma", 16)
    s_w = stage("attention_weights_dma", 16 * 3)
    s_ffw = stage("spiking_weights_dma", 16 * 2)
    s_mask = stage("mask_dma", 32)
    s_x = stage("x2_dma", 32)
    s_ctx = stage("ctx_dma", 16)
    s_qkw = stage("qk_write_dma", 48)
    s_qkr = stage("qk_read_dma", 16 * 6)
    s_mw = stage("max_write_dma", 16)
    s_mr = [stage(f"max_read_dma{i}", 16) for i in range(2)]
    s_out = stage("out_dma", 16, ahead=16)
    setup_dve = stage("setup2_dve")
    setup_pe = stage("setup2_pe")
    FF1, ATT, FF2 = range(3)
    ln_stats = [stage(f"ln{n}_stats") for n in range(3)]
    ln_rstd = [stage(f"ln{n}_rstd") for n in range(3)]
    ln_out = [stage(f"ln{n}_out") for n in range(3)]
    x1n_set = stage("x1n_set")
    x1_set = stage("x1_set")
    s_v = stage("v_const")
    s_part = stage("qk_cut")
    qk_hi = stage("qk_hi")
    qk_lo = stage("qk_lo")
    s_pre = stage("prescore")
    s_max = stage("maximum", ahead=4)
    m_cut = stage("m_cut")
    s_sc = stage("score")
    s_exp = stage("exp", ahead=2)
    g_out = stage("g_out")
    out_ready = stage("out_ready")

    with nc.Block() as block:
        @block.sync
        def _(sp):
            s_out.credit(sp)
            handover.wait(sp, 0)

            def dma(st, o, i):
                sp.dma_start(o, i).then_inc(st.sem, 16)

            def load_x(b):
                dma(s_x, x_in[:, :, :], a["x"][bass.ds(b * TT, TT)].rearrange("j p f -> p j f"))
                dma(s_x, x0[:, :, :], mid[bass.ds((b + 1) * TT, TT)].rearrange("j p f -> p j f"))

            def load_ctx(b):
                dma(s_ctx, ctxT[:, :, :], a["ctxT"][:, bass.ds(b * T, T)].rearrange("(k p) t -> p k t", p=P))

            def stacks(n, beta):
                dst, which = ((k_st, K_PART), (q_st, Q_PART))[n]
                s_part.wait(sp, 2 * beta + n)
                for part in range(3):
                    dma(s_qkw, qk_dram[n, part].rearrange("(k p) t -> p k t", p=P), qk_part[:, n, part])
                s_qkw.wait(sp, 2 * beta + n)
                for band, part in enumerate(which):
                    dma(s_qkr, dst[DH * band:DH * band + DH, :, :],
                        qk_dram[n, part].rearrange("(h e) t -> e h t", e=DH))

            def x_used(beta):
                x1n_set.wait(sp, beta)
                ln_out[FF1].wait(sp, beta)

            def store(beta, slot):
                out_ready.wait(sp, beta)
                settle(sp)
                dma(s_out, out[bass.ds(slot * TT, TT)].rearrange("j p f -> p j f"), tmp[:, :, :])

            def m_rows(b):
                for i in range(2):
                    heads = slice(i * H // 2, (i + 1) * H // 2)
                    m_cut.wait(sp, 2 * b + i)
                    dma(s_mw, m_dram[:, heads].rearrange("s h t -> h s t"), m_part[:, i])
                    s_mw.wait(sp, 2 * b + i)
                    dma(s_mr[i], q_st[6 * DH:QR, heads, :], m_dram[:, heads])

            load_x(0)
            dma(s_up, w_up[:, 0], a["w1"].rearrange("(k p) e -> p k e", p=P))
            dma(s_mask, maskT_i[:, :, :], a["maskT"].rearrange("(j p) t -> p j t", p=P))
            dma(s_mask, mask_i[:, :, :], a["mask"].rearrange("(j p) t -> p j t", p=P))
            dma(s_w, rows[:, :, :], a["rows"].unsqueeze(0).broadcast_to((P, 3, D)))
            dma(s_w, w_down[:, 0], a["w2"].rearrange("(k p) e -> p k e", p=P))
            load_ctx(0)
            dma(s_w, w_att[:, :, :, :].rearrange("p w k e -> p (w k) e"),
                a["w_att"].rearrange("w (k p) e -> p (w k) e", p=P))
            dma(s_ffw, w_up[:, 1], a["w_fc"].rearrange("(k p) e -> p k e", p=P))
            dma(s_ffw, w_down[:, 1], a["w_proj"].rearrange("(k p) e -> p k e", p=P))
            x_used(0)
            load_x(1)
            stacks(0, 0)
            G.wait_full(sp, ("v", 1), BEFORE)
            load_ctx(1)
            stacks(1, 0)
            with sp.Fori(0, B - 1) as b:
                x_used(b + 1)
                settle(sp)
                load_x((b + 2) % B)
                m_rows(b)
                store(b, (b + B - 1) % B)
                stacks(0, b + 1)
                G.wait_full(sp, ("v", 1), b)
                settle(sp)
                load_ctx((b + 2) % B)
                stacks(1, b + 1)
            m_rows(B - 1)
            store(B - 1, B - 2)
            s_out.wait(sp, B - 1)
            store(B, B - 1)
            s_out.wait(sp, B)
            s_x.wait(sp, B)
            s_ctx.wait(sp, B)

        @block.tensor
        def _(pe):
            handover.wait(pe, 0)

            def mm(o, lhsT, rhs, start=True, stop=True):
                return pe.matmul(o, lhsT, rhs, start=start, stop=stop)

            def to_features(keys, src, it):
                for k in range(KD):
                    bk = G.claim(pe, (keys, k), it)
                    for j in range(TT):
                        last = pe.transpose(bk[:, j * P:(j + 1) * P], src[:, j, k * P:(k + 1) * P], ident[:, :])
                    G.written((keys, k), last)

            def project(key, w, rhs, kn, it):
                bk = G.claim(pe, key, it)
                for k in range(kn):
                    last = mm(bk[:, :], w(k), rhs(k), k == 0, k == kn - 1)
                G.written(key, last)

            def project_tokens(key, lhsT, w, kn, jj, it):
                bk = G.claim(pe, key, it)
                for half_ in range(2):
                    for k in range(kn):
                        last = mm(bk[:, half_ * D:(half_ + 1) * D], lhsT(k, 2 * jj + half_), w(k), k == 0, k == kn - 1)
                G.written(key, last)

            def tok(src):
                return lambda k, j: src[:, k, j * P:(j + 1) * P]

            def up_input(beta, it):
                ln_out[FF1].wait(pe, beta)
                to_features("hT", xn, it)

            def up(m, k, it):
                if m == 0 and k == 0:
                    G.wait_read(pe, ("hT", KD - 1), it)
                key = ("w1", m)
                bk = G.claim(pe, key, it) if k == 0 else G.bank(key, it)
                last = mm(bk[:, :], w_up[:, 0, k, m * P:(m + 1) * P], xT[:, 0, k, :], k == 0, k == KD - 1)
                if k == KD - 1:
                    G.written(key, last)

            def down(step, it):
                j, first = step // 2, step % 2 * KF // 2
                key = ("w2", j // 2)
                if step == 0:
                    G.wait_read(pe, ("w1", KF - 1), it)
                bk = G.claim(pe, key, it) if step % 4 == 0 else G.bank(key, it)
                for k in range(first, first + KF // 2):
                    last = mm(bk[:, j % 2 * D:(j % 2 + 1) * D], g1[:, k, j * P:(j + 1) * P], w_down[:, 0, k, :],
                              k == 0, k == KF - 1)
                if step % 4 == 3:
                    G.written(key, last)

            def maxima(b, i, it):
                s_max.wait(pe, (b * H + (i + 1) * H // 2) * TT - 1)
                bk = G.claim(pe, ("mt", i), it)
                for j in range(TT):
                    last = pe.transpose(bk[0:H // 2, j * P:(j + 1) * P], m_col[:, j, i * H // 2:(i + 1) * H // 2],
                                        ident[:, :])
                G.written(("mt", i), last)

            def project_k(beta, it):
                s_ctx.wait(pe, beta)
                for m in range(KD):
                    project(("k", m), lambda k: w_att[:, 1, k, m * P:(m + 1) * P], lambda k: ctxT[:, k, :], KD, it)

            def project_vq(beta, it):
                for jj in range(TT // 2):
                    project_tokens(("v", jj), tok(ctxT), lambda k: w_att[:, 2, k, :], KD, jj, it)
                ln_out[ATT].wait(pe, beta)
                to_features("qn", xn_q, it)
                G.wait_read(pe, ("qn", KD - 1), it)
                for m in range(KD):
                    project(("q", m), lambda k: w_att[:, 0, k, m * P:(m + 1) * P], lambda k: xT[:, 0, k, :], KD, it)

            def prescore(b, hd):
                for j in range(TT):
                    n = (b * H + hd) * TT + j
                    s_max.wait(pe, n - 4)
                    s_pre.done(mm(bank[j], q_st[0:6 * DH, hd, j * P:(j + 1) * P], k_st[0:6 * DH, hd, :]))

            def score(b, unit):
                g, s = unit // 2, unit % 2
                if unit == H // 4:
                    s_mr[1].wait(pe, b)
                for hh in range(4):
                    hd = 4 * g + hh
                    n = b * 2 * H + unit * 4 + hh
                    s_exp.wait(pe, n - 2)
                    for t in range(2):
                        kt = 2 * s + t
                        mm(pair[hh % 2][:, t, :], k_st[0:QR, hd, kt * P:(kt + 1) * P], q_st[0:QR, hd, :], True, False)
                        last = mm(pair[hh % 2][:, t, :], ident_bf[:, :], mask_biasT[:, kt, :], False, True)
                    s_sc.done(last)

            def weigh(b, unit, it):
                g, s = unit // 2, unit % 2
                s_exp.wait(pe, b * 2 * H + unit * 4 + 3)
                key = ("av", g)
                bk = G.claim(pe, key, it) if s == 0 else G.bank(key, it)
                for kt in (2 * s, 2 * s + 1):
                    for hh in range(4):
                        last = mm(bk[32 * hh:32 * hh + 32, :], v_sb[:, kt, 4 * g + hh, :], pr[:, hh, kt, :],
                                  kt == 0, kt == TT - 1)
                if s == 1:
                    G.written(key, last)

            def to_tokens(g, it):
                G.wait_read(pe, ("av", g), it)
                bk = G.claim(pe, ("ot", g), it)
                for j in range(TT):
                    last = pe.transpose(bk[:, j * P:(j + 1) * P], oT[:, g % 2, j * P:(j + 1) * P], ident[:, :])
                G.written(("ot", g), last)

            up_input(0, BEFORE)
            setup_dve.wait(pe, 0)
            for k in range(TT):
                last = mm(bank[0], ones_bf[:, :], keep_bf[:, k, :], k == 0, k == TT - 1)
            setup_pe.done(last)
            s_up.wait(pe, 0)
            for m in range(KF):
                for k in range(KD):
                    up(m, k, BEFORE)
            s_w.wait(pe, 0)
            for step in range(2 * TT):
                down(step, BEFORE)
            project_k(0, BEFORE)
            project_vq(0, BEFORE)
            for key in attention_keys()[0][-4:]:
                G.wait_read(pe, key, BEFORE)
            s_v.wait(pe, 0)
            s_ffw.wait(pe, 0)
            setup_dve.wait(pe, 1)

            def batch(b, it, more):
                if more:
                    up_input(b + 1, it)
                s_qkr.wait(pe, 2 * b + 1)
                for hd in range(H):
                    prescore(b, hd)
                    if more and hd < H // 2:
                        for k in range(KD):
                            up(hd, k, it)
                    elif more:
                        down(hd - H // 2, it)
                    if hd == H // 2:
                        maxima(b, 0, it)
                maxima(b, 1, it)
                s_max.wait(pe, (b + 1) * H * TT - 1)
                s_mr[0].wait(pe, b)
                score(b, 0)
                for unit in range(H // 2):
                    if unit + 1 < H // 2:
                        score(b, unit + 1)
                    weigh(b, unit, it)
                    if unit % 2 == 0 and unit > 0:
                        to_tokens(unit // 2 - 1, it)
                if more:
                    project_k(b + 1, it)
                to_tokens(H // 4 - 1, it)
                G.wait_read(pe, ("ot", H // 4 - 1), it)
                to_features("on", o_sb, it)
                G.wait_read(pe, ("on", KD - 1), it)
                for jj in range(TT // 2):
                    project_tokens(("wo", jj), tok(xT[:, 1]), lambda k: w_att[:, 3, k, :], KD, jj, it)
                if more:
                    project_vq(b + 1, it)
                ln_out[FF2].wait(pe, b)
                to_features("fn", xn, it)
                G.wait_read(pe, ("fn", KD - 1), it)
                for m in range(KF):
                    project(("fc", m), lambda k: w_up[:, 1, k, m * P:(m + 1) * P], lambda k: xT[:, 1, k, :], KD, it)
                g_out.wait(pe, KF * (b + 1) - 1)
                for jj in range(TT // 2):
                    project_tokens(("pr", jj), tok(g1), lambda k: w_down[:, 1, k, :], KF, jj, it)

            with pe.Fori(0, B - 1) as b:
                batch(b, b, True)
            batch(B - 1, AFTER, False)

        @block.scalar
        def _(act):
            s_exp.credit(act)
            for name, (_, done, _, _) in kinds.items():
                if name not in on_dve:
                    done.credit(act)
            handover.wait(act, 0)

            def f(o, i, fn=ACT.Copy, **kw):
                return act.activation(o, i, fn, **kw)

            def evacuate(key, o, it, fn=ACT.Copy, **kw):
                bk = G.wait_full(act, key, it)
                G.read(key, f(o, bk[:, :], fn, **kw))

            def up(it):
                for k in range(KD):
                    evacuate(("hT", k), xT[:, 0, k, :], it, ACT.Identity, scale=col("ffn_g", k), bias=col("ffn_b", k))
                for m in range(KF):
                    evacuate(("w1", m), g1[:, m, :], it, ACT.Gelu, bias=col("b1", m))

            def high(beta, n):
                if n == 1:
                    kinds["q"][1].wait(act, KD * beta + KD - 1)
                qk_hi.done(f(qk_part[:, n, 0], qk[:, n]))

            def middle(beta, n):
                qk_lo.wait(act, 2 * beta + n)
                qk_hi.done(f(qk_part[:, n, 1], qk[:, n]))

            def project_k(beta, it):
                s_qkw.wait(act, 2 * beta - 1)
                if not isinstance(it, str):
                    out_ready.wait(act, beta - 1)
                    s_out.wait(act, beta - 1)
                for m in range(KD):
                    evacuate(("k", m), qk[:, 0, m, :], it, ACT.Identity, bias=col("bk", m))
                G.wait_read(act, ("k", KD - 1), it)
                high(beta, 0)

            def input_q(it):
                for k in range(KD):
                    evacuate(("qn", k), xT[:, 0, k, :], it)

            up(BEFORE)
            project_k(0, BEFORE)
            middle(0, 0)
            input_q(BEFORE)
            high(0, 1)
            middle(0, 1)

            def batch(b, it, more):
                if more:
                    up(it)
                for unit in range(H // 2):
                    g, s = unit // 2, unit % 2
                    for hh in range(4):
                        n = b * 2 * H + unit * 4 + hh
                        s_sc.wait(act, n)
                        s_exp.done(f(pr[:, hh, 2 * s:2 * s + 2, :], pair[hh % 2][:, :, :], ACT.Exp, scale=0.25))
                    if s == 0 and g > 0:
                        evacuate(("av", g - 1), oT[:, (g - 1) % 2, :], it)
                evacuate(("av", H // 4 - 1), oT[:, (H // 4 - 1) % 2, :], it)
                if more:
                    project_k(b + 1, it)
                for k in range(KD):
                    evacuate(("on", k), xT[:, 1, k, :], it)
                if more:
                    middle(b + 1, 0)
                    input_q(it)
                    high(b + 1, 1)
                    middle(b + 1, 1)
                for k in range(KD):
                    evacuate(("fn", k), xT[:, 1, k, :], it)
                for m in range(KF):
                    evacuate(("fc", m), g0[:, :], it, ACT.Relu)
                    G.wait_read(act, ("fc", m), it)
                    g_out.done(f(g1[:, m, :], g0[:, :], ACT.Square))
                    g_out.wait(act, KF * b + m)

            with act.Fori(0, B - 1) as b:
                batch(b, b, True)
            batch(B - 1, AFTER, False)

        @block.vector
        def _(dve):
            s_max.credit(dve)
            for name in on_dve:
                kinds[name][1].credit(dve)
            handover.wait(dve, 0)
            A3 = (slice(None),) * 3

            def norm_stats(n, src):
                dve.drain()
                for j in range(TT):
                    dve.bn_stats(stats[:, j, :], src[:, j, :])
                dve.drain()
                for j in range(TT):
                    last = dve.bn_aggr(mv[:, j, :], stats[:, j, :])
                ln_stats[n].done(last)

            def norm_apply(n, beta, src, dst):
                ln_rstd[n].wait(dve, beta)
                for j in range(TT):
                    last = dve.tensor_scalar(dst[:, j, :], src[:, j, :], mv[:, j, 0:1], rstd[:, j:j + 1],
                                             ALU.subtract, ALU.mult)
                ln_out[n].done(last)

            def two(ap, jj):
                return ap[:, 2 * jj:2 * jj + 2, :]

            def bank_tiles(bk):
                return bk[:, :].rearrange("p (j f) -> p j f", j=2)

            def first_norm(beta):
                s_x.wait(dve, beta)
                settle(dve)
                norm_stats(FF1, x0)
                norm_apply(FF1, beta, x0, xn)

            def add_down(beta, it):
                x1n_set.wait(dve, beta)
                for jj in range(TT // 2):
                    bk = G.wait_full(dve, ("w2", jj), it)
                    G.read(("w2", jj), dve.tensor_tensor(two(x1n, jj), two(x1n, jj), bank_tiles(bk), ALU.add))

            def cut_lo(beta, n):
                qk_hi.wait(dve, 4 * beta + 2 * n)
                qk_lo.done(dve.tensor_tensor(qk[:, n], qk[:, n], qk_part[:, n, 0], ALU.subtract))

            def cut_last(beta, n):
                qk_hi.wait(dve, 4 * beta + 2 * n + 1)
                s_part.done(dve.tensor_tensor(qk_part[:, n, 2], qk[:, n], qk_part[:, n, 1], ALU.subtract))

            def take_v(it):
                for jj in range(TT // 2):
                    key = ("v", jj)
                    bk = G.wait_full(dve, key, it)
                    G.read(key, dve.tensor_tensor(
                        v_sb[:, 2 * jj:2 * jj + 2, :, 0:DH], bk[:, :].rearrange("p (j h e) -> p j h e", j=2, h=H),
                        rows[:, 1, :].rearrange("p (h e) -> p h e", h=H).unsqueeze(1).broadcast_to((P, 2, H, DH)), ALU.add))

            def take_q(it):
                for m in range(KD):
                    bk = G.wait_full(dve, ("q", m), it)
                    G.read(("q", m), dve.scalar_tensor_tensor(qk[:, 1, m, :], bk[:, :], col("bq", m), not_full[:, :],
                                                              ALU.add, ALU.mult))

            def normalise(g, it):
                dve.drain()
                bk = G.wait_full(dve, ("ot", g), it)
                o = bk[:, :].rearrange("p (j h e) -> p j h e", j=TT, h=4)
                dve.reciprocal(rsum[:, :, :], o[:, :, :, DH:DH + 1].squeeze(3))
                dve.drain()
                dst = o_sb[:, :, g * 4 * DH:(g + 1) * 4 * DH].rearrange("p j (h e) -> p j h e", h=4)
                for j in range(TT):
                    last = dve.tensor_tensor(dst[:, j], o[:, j, :, 0:DH],
                                             rsum[:, j, :].unsqueeze(2).broadcast_to((P, 4, DH)), ALU.mult)
                G.read(("ot", g), last)

            def cut_maxima(b, i, it):
                bk = G.wait_full(dve, ("mt", i), it)
                high, mid_, low = (m_part[:, i, n, :] for n in range(3))
                dve.tensor_scalar(high, bk[0:H // 2, :], -1.0, None, ALU.mult)
                dve.drain()
                G.read(("mt", i), dve.scalar_tensor_tensor(m_rest[:, :], bk[0:H // 2, :], -1.0, high,
                                                           ALU.mult, ALU.subtract))
                dve.drain()
                dve.tensor_copy(mid_, m_rest[:, :])
                dve.drain()
                m_cut.done(dve.tensor_tensor(low, m_rest[:, :], mid_, ALU.subtract))

            def spikes(beta):
                def start():
                    s_out.wait(dve, beta - 1)
                    settle(dve)
                    dve.drain()
                    dve.tensor_scalar(spk[A3], y_sb[A3], THRESHOLD, None, ALU.is_gt)
                    dve.tensor_scalar(cnt[A3], y_sb[A3], THRESHOLD, None, ALU.is_gt)

                def step(i):
                    prev = y_sb if i == 1 else mem
                    dve.drain()
                    dve.scalar_tensor_tensor(tmp[A3], prev[A3], BETA, y_sb[A3], ALU.mult, ALU.add)
                    dve.drain()
                    dve.tensor_tensor(mem[A3], tmp[A3], spk[A3], ALU.subtract)
                    dve.drain()
                    dve.scalar_tensor_tensor(cnt[A3], mem[A3], THRESHOLD, cnt[A3], ALU.is_gt, ALU.add)
                    if i < STEPS - 1:
                        dve.tensor_scalar(spk[A3], mem[A3], THRESHOLD, None, ALU.is_gt)

                def finish():
                    dve.drain()
                    out_ready.done(dve.scalar_tensor_tensor(tmp[A3], cnt[A3], 1.0 / STEPS, x_res[A3], ALU.mult, ALU.add))
                return start, step, finish

            first_norm(0)
            dve.memset(y_sb[A3], 0.0)
            dve.memset(x_res[A3], 0.0)
            s_mask.wait(dve, 0)
            dve.memset(ones_bf[:, :], 1.0)
            dve.tensor_copy(ident_bf[:, :], ident[:, :])
            last = dve.tensor_scalar(keep_bf[:, :, :], maskT_i[:, :, :], 0.0, None, ALU.not_equal)
            setup_dve.done(last)
            setup_pe.wait(dve, 0)
            dve.tensor_scalar(not_full[:, :], bank[0], 0.0, None, ALU.is_gt)
            dve.tensor_scalar(keep[:, :, :], maskT_i[:, :, :], 0.0, MASKED, ALU.is_equal, ALU.mult)
            dve.drain()
            dve.tensor_tensor(mask_biasT[:, :, :], keep[:, :, :],
                              not_full[:, :].unsqueeze(1).broadcast_to((P, TT, T)), ALU.mult)
            dve.drain()
            dve.tensor_scalar(keep[:, :, :], mask_i[:, :, :], 0.0, None, ALU.not_equal)
            dve.drain()
            dve.reduce_max(row_keep[:, :], keep[:, :, :], AX.X)
            dve.drain()
            dve.tensor_scalar(keep[:, :, :], mask_i[:, :, :], 0.0, MASKED, ALU.is_equal, ALU.mult)
            dve.drain()
            for j in range(TT):
                last = dve.tensor_scalar(mask_bias[:, j, :], keep[:, j, :], row_keep[:, j:j + 1], None, ALU.mult)
            setup_dve.done(last)
            dve.drain()


            s_w.wait(dve, 0)
            add_down(0, BEFORE)
            norm_stats(ATT, x1n)
            norm_apply(ATT, 0, x1n, xn_q)
            cut_lo(0, 0)
            cut_last(0, 0)
            take_v(BEFORE)
            take_q(BEFORE)
            cut_lo(0, 1)
            cut_last(0, 1)
            G.wait_read(dve, ("hT", KD - 1), BEFORE)
            first_norm(1)

            def batch(b, it, more):
                for hd in range(H):
                    for j in range(TT):
                        s_max.wait(dve, (b * H + hd) * TT + j - 2)
                        s_pre.wait(dve, (b * H + hd) * TT + j)
                        settle(dve)
                        s_max.done(dve.tensor_tensor_reduce(
                            masked[:, j % 2, :], bank[j], mask_bias[:, j, :], 1.0, FLOOR, ALU.add, ALU.max, m_col[:, j, hd:hd + 1]))
                    if hd == H // 2 + 1:
                        cut_maxima(b, 0, it)
                cut_maxima(b, 1, it)
                start, step, finish = spikes(b)
                start()
                step(1)
                if more:
                    add_down(b + 1, it)
                    norm_stats(ATT, x1n)
                    norm_apply(ATT, b + 1, x1n, xn_q)
                step(2)
                normalise(0, it)
                step(3)
                normalise(1, it)
                step(4)
                finish()
                normalise(2, it)
                normalise(3, it)
                if more:
                    cut_lo(b + 1, 0)
                x1_set.wait(dve, b)
                for jj in range(TT // 2):
                    bk = G.wait_full(dve, ("wo", jj), it)
                    G.read(("wo", jj), dve.tensor_tensor(two(x_res, jj), two(x1, jj), bank_tiles(bk), ALU.add))
                norm_stats(FF2, x_res)
                if more:
                    take_v(it)
                norm_apply(FF2, b, x_res, xn)
                if more:
                    cut_last(b + 1, 0)
                    take_q(it)
                    cut_lo(b + 1, 1)
                    cut_last(b + 1, 1)
                    G.wait_read(dve, ("fn", KD - 1), it)
                    first_norm(b + 2)
                for jj in range(TT // 2):
                    key = ("pr", jj)
                    bk = G.wait_full(dve, key, it)
                    G.read(key, dve.tensor_copy(two(y_sb, jj), bank_tiles(bk)))

            with dve.Fori(0, B - 1) as b:
                batch(b, b, True)
            batch(B - 1, AFTER, False)
            start, step, finish = spikes(B)
            start()
            for i in range(1, STEPS):
                step(i)
            finish()

        @block.gpsimd
        def _(pool):
            handover.wait(pool, 0)

            def rstd_of(n, beta):
                ln_stats[n].wait(pool, beta)
                settle(pool)
                pool.tensor_scalar(rstd[:, :], mv[:, :, 1], EPS, None, ALU.add)
                pool.drain()
                ln_rstd[n].done(pool.tensor_tensor(rstd[:, :], rstd[:, :], minus_half[:, :], ALU.pow))
                pool.drain()

            def row(n):
                return rows[:, n, :].unsqueeze(1).broadcast_to((P, TT, D))

            def start_x1n(beta):
                s_x.wait(pool, beta)
                settle(pool)
                pool.tensor_tensor(x1n[:, :, :], x_in[:, :, :], x0[:, :, :], ALU.add)
                pool.drain()
                x1n_set.done(pool.tensor_tensor(x1n[:, :, :], x1n[:, :, :], row(0), ALU.add))
                pool.drain()

            def take_x1(beta):
                kinds["w2"][1].wait(pool, 2 * beta + 1)
                settle(pool)
                x1_set.done(pool.tensor_tensor(x1[:, :, :], x1n[:, :, :], row(2), ALU.add))
                pool.drain()

            rstd_of(FF1, 0)
            setup_dve.wait(pool, 1)
            settle(pool)
            pool.memset(k_st[6 * DH:QR, :, :], 1.0)
            pool.drain()
            pool.memset(v_sb[:, :, :, DH:32], 0.0)
            pool.drain()
            s_v.done(pool.memset(v_sb[:, :, :, DH:DH + 1], 1.0))
            pool.drain()
            s_w.wait(pool, 0)
            start_x1n(0)
            rstd_of(ATT, 0)
            take_x1(0)
            rstd_of(FF1, 1)

            def batch(b, more):
                if more:
                    start_x1n(b + 1)
                    rstd_of(ATT, b + 1)
                rstd_of(FF2, b)
                if more:
                    kinds["wo"][1].wait(pool, 2 * b + 1)
                    take_x1(b + 1)
                    rstd_of(FF1, b + 2)

            with pool.Fori(0, B - 1) as b:
                batch(b, True)
            batch(B - 1, False)


def build(nc, a, out):
    f32, bf16 = mybir.dt.float32, mybir.dt.bfloat16
    where = {"next": -(-nc.sbuf_base // 32) * 32}

    def sb(name, shape, dt=f32, offset=None):
        size = -(-int(np.prod(shape[1:])) * (2 if dt == bf16 else 4) // 32) * 32
        if offset is None:
            offset = where["next"]
            where["next"] += size
            assert where["next"] <= nc.sbuf_usable_end, (name, where["next"])
        where[name] = offset
        return nc.alloc_sbuf_tensor_at(name, shape, dt, offset=offset)

    ident = sb("ident", [P, P])
    flip = sb("flip", [P, P])
    cols = sb("cols", [P, COLS["end"]])
    minus_half = sb("minus_half", [P, TT])
    mid = nc.dram_tensor("mid", ((B + 1) * TT, P, D), f32).ap()

    with ExitStack() as ctx:
        pair = [ctx.enter_context(nc.psum_tensor(f"pair{i}", [P, 2, T], f32)) for i in range(2)]
        bank = [pair[i // 2][:, i % 2, :] for i in range(4)]
        y_bank = ctx.enter_context(nc.psum_tensor("y_bank", [P, T], f32))
        general = [ctx.enter_context(nc.psum_tensor(f"general{i}", [P, T], f32)) for i in range(3)]

        def stage(name, step=1, ahead=0):
            return Stage(ctx.enter_context(nc.semaphore(name)), step, ahead)

        s_const = stage("const_dma", 16 * 3)
        carrier = stage("carrier")
        handover = stage("handover", 5)

        def col(name, k=0, n=1):
            return cols[:, COLS[name] + k:COLS[name] + k + n]

        def settle(eng):
            eng.sem_inc(carrier.sem, 1)

        consts = (ident, flip, cols, minus_half, col, settle, s_const)
        psum = (pair, bank, y_bank, general)
        shared = where["next"]
        mamba_pass(nc, ctx, a, mid, sb, where, stage, psum, consts, handover)
        where["next"] = shared
        attention_pass(nc, ctx, a, mid, out, sb, where, stage, psum, consts, handover)


def _selectors():
    i = np.arange(P)
    ident = np.eye(P, dtype=np.float32)
    sel_r = np.zeros((P, 2, NV, P), np.float32)
    sel_y = np.zeros((P, NV, 32), np.float32)
    sel_bc = np.zeros((RK + 2 * NS, 2, P), np.float32)
    for v in range(NV):
        for p in range(P):
            channel = CC * v + p // NS
            for part in range(2):
                sel_r[32 * part + channel, 0, v, p] = 1
                sel_r[64 + 32 * part + channel, 1, v, p] = 1
            sel_y[p, v, channel] = 1
    for n in range(2):
        sel_bc[RK + NS * n + i % NS, n, i] = 1
    return {"ident": ident, "flip": ident[::-1].copy(), "sel_r": sel_r, "sel_y": sel_y, "sel_bc": sel_bc}


def _layout(x):
    def blocks(v):
        return v.reshape(-1, P).T

    cols = np.zeros((P, COLS["end"]), np.float32)

    def put(name, v):
        cols[:, COLS[name]:COLS[name] + v.shape[1]] = v

    m, t = "L0_attn_", "L0_xattn_"
    for name, key in [("norm_g", m + "norm_g"), ("norm_b", m + "norm_b"), ("ffn_g", m + "ffn_g"), ("ffn_b", m + "ffn_b"),
                      ("b1", m + "b1"), ("bq", t + "bq"), ("bk", t + "bk")]:
        put(name, blocks(x[key]))
    for d in "fb":
        p = m + d + "_"
        put(d + "conv_w", x[p + "conv_w"].reshape(KI, P, CW).transpose(1, 0, 2).reshape(P, KI * CW))
        put(d + "conv_b", blocks(x[p + "conv_b"]))
        put(d + "dt_b", blocks(x[p + "dt_proj_b"]))
        put(d + "D", blocks(x[p + "D"]))
        al = x[p + "A_log"].reshape(NM, NQ, NV, CC, NS).transpose(3, 4, 0, 2, 1)
        put(d + "A_log", al.reshape(P, NC))

    def both(key):
        return np.stack([np.ascontiguousarray(x[m + d + "_" + key].T) for d in "fb"])

    arrays = _selectors()
    arrays["x"] = x["x"].reshape(B * TT, P, D)
    arrays["ctxT"] = x["ctx_1024"].reshape(B * T, D).T
    arrays["mask"] = x["mask_1x1xSxS2_ik0"].reshape(T, T)
    arrays["maskT"] = arrays["mask"].T
    arrays["cols"] = cols
    arrays["rows"] = np.stack([x[m + "b2"], x[t + "bv"], x[t + "bo"]])
    arrays["w_in"] = both("in_proj_w")
    arrays["w_xp"] = both("x_proj_w")
    arrays["w_dt"] = both("dt_proj_w")
    arrays["w_out"] = both("out_proj_w")
    arrays["w_att"] = np.stack([x[t + w].T for w in ("wq", "wk", "wv", "wo")])
    arrays["w1"] = x[m + "w1"].T
    arrays["w2"] = x[m + "w2"].T
    arrays["w_fc"] = x["L0_ffn_W_fc"].T
    arrays["w_proj"] = x["L0_ffn_W_proj"].T
    return {k: np.ascontiguousarray(v) for k, v in arrays.items()}


def kernel(**inputs):
    import concourse.bacc as bacc
    from concourse.bass_utils import run_bass_kernel_spmd

    arrays = _layout({k: np.asarray(v) for k, v in inputs.items()})
    nc = bacc.Bacc("TRN2", target_bir_lowering=False, num_devices=1)
    aps = {k: nc.dram_tensor(k, v.shape, mybir.dt.from_np(v.dtype), kind="ExternalInput").ap() for k, v in arrays.items()}
    out = nc.dram_tensor("out", (B * TT, P, D), mybir.dt.float32, kind="ExternalOutput").ap()
    build(nc, aps, out)
    r = run_bass_kernel_spmd(nc, [arrays], core_ids=[0])
    return r.results[0]["out"].reshape(B, T, D)
```
